# Optimizing a Trainium2 kernel written in Bass

```python
import numpy as np
import jax
import jax.numpy as jnp

def _softmax(x, axis=-1):
    return jax.nn.softmax(x, axis=axis)

def _gelu(x):
    return jax.nn.gelu(x, approximate=True)

def _silu(x):
    return jax.nn.silu(x)

def _sigmoid(x):
    return jax.nn.sigmoid(x)

def _layernorm(x, axis=-1, eps=1e-05):
    m = jnp.mean(x, axis=axis, keepdims=True)
    v = jnp.var(x, axis=axis, keepdims=True)
    return (x - m) / jnp.sqrt(v + eps)

def _scatter_add(tgt, idx, src, axis=0):
    return tgt.at[idx].add(src)

def _segment_sum(src, seg, n):
    return jax.ops.segment_sum(src, seg, n)
kernel_name = 'mk_adaln_d1_jaxref_r8_8dd2cb'

def setup_inputs(seed: int=0):
    np.random.seed(seed)
    _w = jnp.asarray

    def _L0_attn_setup():
        import jax, jax.numpy as jnp
        import numpy as np
        WINDOWP = 64
        LN_EPS = 1e-05

        def _layer_norm(y, g, b):
            mu = jnp.mean(y, axis=-1, keepdims=True)
            var = jnp.mean((y - mu) ** 2, axis=-1, keepdims=True)
            return (y - mu) * jax.lax.rsqrt(var + LN_EPS) * g + b
        key = jax.random.key(seed)
        ks = jax.random.split(key, 4)
        B, T, D = (8, 256, 128)
        feature = jax.random.normal(ks[0], (B, T, D), dtype=jnp.float32)
        wq_w = jax.random.normal(ks[1], (D, D), dtype=jnp.float32) * 0.02
        wq_b = jnp.zeros((D,), dtype=jnp.float32)
        w2_w = jax.random.normal(ks[2], (D,), dtype=jnp.float32) * 0.02
        w2_b = jnp.zeros((1,), dtype=jnp.float32)
        ln_g = jnp.ones((D,), dtype=jnp.float32)
        ln_b = jnp.zeros((D,), dtype=jnp.float32)
        return {'feature': feature, 'wq_w': wq_w, 'wq_b': wq_b, 'w2_w': w2_w, 'w2_b': w2_b, 'ln_g': ln_g, 'ln_b': ln_b}
    _L0_attn_in = _L0_attn_setup()

    def _L0_ffn_setup():
        import jax, jax.numpy as jnp
        import numpy as np
        D_MODEL = 128
        D_FF = 512
        NUM_EXPERTS = 8
        TOP_K = 2
        BATCH = 4
        SEQ = 256
        key = jax.random.key(seed)
        ks = jax.random.split(key, 8)
        s = 0.02
        x = jax.random.normal(ks[0], (BATCH, SEQ, D_MODEL), dtype=jnp.float32)
        router_w = jax.random.normal(ks[1], (D_MODEL, NUM_EXPERTS), dtype=jnp.float32) * s
        router_b = jnp.zeros((NUM_EXPERTS,), dtype=jnp.float32)
        W1 = jax.random.normal(ks[2], (NUM_EXPERTS, D_MODEL, D_FF), dtype=jnp.float32) * s
        b1 = jnp.zeros((NUM_EXPERTS, D_FF), dtype=jnp.float32)
        W2 = jax.random.normal(ks[3], (NUM_EXPERTS, D_FF, D_MODEL), dtype=jnp.float32) * s
        b2 = jnp.zeros((NUM_EXPERTS, D_MODEL), dtype=jnp.float32)
        return {'x': x, 'router_w': router_w, 'router_b': router_b, 'W1': W1, 'b1': b1, 'W2': W2, 'b2': b2}
    _L0_ffn_in = _L0_ffn_setup()
    _L0_c = _w((lambda *s: np.random.randn(*s).astype(np.float32) * 0.05)(32, 128))
    _L0_wmod = _w((lambda *s: np.random.randn(*s).astype(np.float32) * 0.05)(128, 6 * 128) * 128 ** (-0.5))
    _d = {'L0_attn_feature': _L0_attn_in['feature'], 'L0_attn_wq_w': _L0_attn_in['wq_w'], 'L0_attn_wq_b': _L0_attn_in['wq_b'], 'L0_attn_w2_w': _L0_attn_in['w2_w'], 'L0_attn_w2_b': _L0_attn_in['w2_b'], 'L0_attn_ln_g': _L0_attn_in['ln_g'], 'L0_attn_ln_b': _L0_attn_in['ln_b'], 'L0_ffn_router_w': _L0_ffn_in['router_w'], 'L0_ffn_router_b': _L0_ffn_in['router_b'], 'L0_ffn_W1': _L0_ffn_in['W1'], 'L0_ffn_b1': _L0_ffn_in['b1'], 'L0_ffn_W2': _L0_ffn_in['W2'], 'L0_ffn_b2': _L0_ffn_in['b2'], 'L0_c': _L0_c, 'L0_wmod': _L0_wmod}
    _x0 = _d['L0_attn_feature']
    _d['L0_attn_feature'] = jax.random.normal(jax.random.fold_in(jax.random.key(seed), 1), (32, 256, 128), dtype=_x0.dtype)
    del _x0
    return _d

def reference(L0_attn_feature, L0_attn_wq_w, L0_attn_wq_b, L0_attn_w2_w, L0_attn_w2_b, L0_attn_ln_g, L0_attn_ln_b, L0_ffn_router_w, L0_ffn_router_b, L0_ffn_W1, L0_ffn_b1, L0_ffn_W2, L0_ffn_b2, L0_c, L0_wmod):

    def _L0_attn_ref(feature, wq_w, wq_b, w2_w, w2_b, ln_g, ln_b):
        import jax, jax.numpy as jnp
        import numpy as np
        WINDOWP = 64
        LN_EPS = 1e-05

        def _layer_norm(y, g, b):
            mu = jnp.mean(y, axis=-1, keepdims=True)
            var = jnp.mean((y - mu) ** 2, axis=-1, keepdims=True)
            return (y - mu) * jax.lax.rsqrt(var + LN_EPS) * g + b
        B, T, D = feature.shape
        W = WINDOWP
        q_local = feature @ wq_w + wq_b
        init_buf = feature[:, :W, :]

        def step(buf, q_i):
            ki = jnp.concatenate([buf, jnp.zeros((B, 1, D), feature.dtype)], axis=1)
            scores = jnp.einsum('bwd,d->bw', q_i[:, None, :] * ki, w2_w) + w2_b[0]
            alpha = jax.nn.softmax(scores, axis=1)
            v_i = jnp.einsum('bwd,bw->bd', ki, alpha)
            new_buf = jnp.concatenate([buf[:, 1:, :], v_i[:, None, :]], axis=1)
            return (new_buf, v_i)
        qs = jnp.transpose(q_local[:, W:, :], (1, 0, 2))
        _, vs = jax.lax.scan(step, init_buf, qs)
        v_local = jnp.concatenate([feature[:, :W, :], jnp.transpose(vs, (1, 0, 2))], axis=1)
        y = jnp.tanh(v_local) * feature + feature
        return _layer_norm(y, ln_g, ln_b)

    def _L0_ffn_ref(x, router_w, router_b, W1, b1, W2, b2):
        import jax, jax.numpy as jnp
        import numpy as np
        D_MODEL = 128
        D_FF = 512
        NUM_EXPERTS = 8
        TOP_K = 2
        BATCH = 4
        SEQ = 256
        logits = jnp.einsum('bsd,de->bse', x, router_w) + router_b
        topk_scores, topk_idx = jax.lax.top_k(logits, TOP_K)
        topk_gates = jax.nn.softmax(topk_scores, axis=-1)
        onehot = jax.nn.one_hot(topk_idx, NUM_EXPERTS, dtype=x.dtype)
        combine = jnp.einsum('bsk,bske->bse', topk_gates, onehot)
        combine_e = jnp.moveaxis(combine, -1, 0)

        def expert_step(acc, params):
            w1, bb1, w2, bb2, c = params
            h = jax.nn.relu(jnp.einsum('bsd,df->bsf', x, w1) + bb1)
            y = jnp.einsum('bsf,fd->bsd', h, w2) + bb2
            return (acc + y * c[..., None], None)
        out, _ = jax.lax.scan(expert_step, jnp.zeros_like(x), (W1, b1, W2, b2, combine_e))
        return out
    x = L0_attn_feature
    mod = (_silu(L0_c) @ L0_wmod).reshape(L0_c.shape[0], 6, 1, -1)
    sa, ca, ga, sb, cb, gb = (mod[:, 0], mod[:, 1], mod[:, 2], mod[:, 3], mod[:, 4], mod[:, 5])
    ga = (2 * (ga >= 0) - 1) * jnp.maximum(jnp.abs(ga), 0.25)
    gb = (2 * (gb >= 0) - 1) * jnp.maximum(jnp.abs(gb), 0.25)
    h = _layernorm(x, axis=-1) * (1 + ca) + sa
    x = x + ga * _L0_attn_ref(h, L0_attn_wq_w, L0_attn_wq_b, L0_attn_w2_w, L0_attn_w2_b, L0_attn_ln_g, L0_attn_ln_b)
    h = _layernorm(x, axis=-1) * (1 + cb) + sb
    x = x + gb * _L0_ffn_ref(h, L0_ffn_router_w, L0_ffn_router_b, L0_ffn_W1, L0_ffn_b1, L0_ffn_W2, L0_ffn_b2)
    return x

_drawn_inputs = setup_inputs


def setup_inputs(seed=0):
    import zlib

    import numpy as np

    out = dict(_drawn_inputs(seed))
    spreads = {'L0_attn_wq_b': (0.0, 0.8),
     'L0_attn_ln_g': (1.0, 0.2),
     'L0_attn_ln_b': (0.0, 0.309),
     'L0_ffn_router_b': (0.0, 0.682),
     'L0_ffn_b1': (0.0, 0.8),
     'L0_ffn_b2': (0.0, 0.477)}
    factors = {'L0_attn_wq_w': 8.0,
     'L0_attn_w2_w': 8.0,
     'L0_ffn_router_w': 3.053,
     'L0_ffn_W1': 5.411,
     'L0_ffn_W2': 4.244}
    for name, (base, spread) in spreads.items():
        noise = np.random.default_rng([zlib.crc32(name.encode()), seed]).standard_normal(out[name].shape)
        drawn = base * np.exp(spread * noise) if base else spread * noise
        out[name] = jnp.asarray(drawn.astype(out[name].dtype))
    for name, factor in factors.items():
        out[name] = (out[name] * factor).astype(out[name].dtype)
    return out
```

```python
from contextlib import ExitStack

import concourse.bass as bass
from concourse import mybir

F32 = mybir.dt.float32
ALU = mybir.AluOpType
ACT = mybir.ActivationFunctionType
AX = mybir.AxisListType

B, T, D = 32, 256, 128
W = 64
TB = 16
NBLK = T // TB
NSLOT = W // TB
G, GB = 4, B // 4
E, F = 8, 512
FC = F // 128
TOK = B * TB
NSCAN = NBLK - NSLOT
TICKS = E * FC
LN_EPS = 1e-5
MASKED = -2e38
TAKEN = -3e38
Q32 = 32


def adaln_block_kernel(nc, feature, wq_w, wq_b, w2_w, w2_b, ln_g, ln_b, router_w, router_b,
                       W1, b1, W2, b2, c, wmod, out):
    with ExitStack() as ctx:
        def sb(name, shape):
            return ctx.enter_context(nc.sbuf_tensor(name, shape, F32))

        def sem(name):
            return ctx.enter_context(nc.semaphore(name))

        ps_h = ctx.enter_context(nc.psum_tensor("ps_h", [128, 2, 512], F32))
        ps_y = ctx.enter_context(nc.psum_tensor("ps_y", [128, 2, 512], F32))
        ps_wide = ctx.enter_context(nc.psum_tensor("ps_wide", [128, 1024], F32))
        ps_scan = ctx.enter_context(nc.psum_tensor("ps_scan", [128, 512], F32))
        ps_epi = ctx.enter_context(nc.psum_tensor("ps_epi", [128, 512], F32))

        x_sb = sb("x_sb", [128, NBLK, G, D])
        h_T = sb("h_T", [128, NBLK, TOK])
        w1_sb = sb("w1_sb", [128, E, F])
        w2_sb = sb("w2_sb", [128, E, FC, D])
        ring_rows = sb("ring_rows", [W, B, D])
        ring_T = sb("ring_T", [128, B, W])
        hidden = sb("hidden", [128, 2, FC, TOK])
        q_blk = sb("q_blk", [128, B, Q32])
        score = sb("score", [128, GB, W])
        prob = sb("prob", [128, GB, W])
        prob_T = sb("prob_T", [W, GB, 128])
        o_rows = sb("o_rows", [128, GB, D])
        o_T = sb("o_T", [128, B, TB])
        r_pad = sb("r_pad", [128, TB + 1, Q32])
        cross = sb("cross", [128, TB + 1, Q32])
        prod = sb("prod", [128, TB, TB])
        wgt = sb("wgt", [128, TB, TB])
        coef = sb("coef", [128, Q32, Q32])
        v_rows = sb("v_rows", [128, GB, D])
        mask = sb("mask", [128, NSLOT, W])
        below = sb("below", [128, TB])
        diag = sb("diag", [128, TB])
        unit = sb("unit", [128, 2 * TB - 1])
        ident = sb("ident", [128, 128])
        small = sb("small", [128, 16 * TB])
        m_score, m_old, z_old, z_zero, m_rel = (small[:, 8 * k:8 * k + 8] for k in range(5))
        neg_max, z_sum, z_all, z_inv = (small[:, 64 + TB * k:64 + TB * (k + 1)] for k in range(4))
        z_one = small[:, 128:136]
        z_less = small[:, 136:144]
        tmp_r = sb("tmp_r", [128, TB, GB])
        tmp_d = sb("tmp_d", [128, TB, GB])
        col = sb("col", [128, TB])

        gate_T = sb("gate_T", [128, 512])
        y_T = sb("y_T", [128, 512])
        z_sb = sb("z_sb", [128, G, D])
        u_sb = sb("u_sb", [128, G, D])
        h2_next = sb("h2_next", [128, TOK])
        h2_T = sb("h2_T", [128, TOK])
        acc_next = sb("acc_next", [128, G, D])
        acc = sb("acc", [128, G, D])
        out_sb = sb("out_sb", [128, G, D])
        stats = sb("stats", [128, G, 6])
        idle = sb("idle", [128, 1])
        mv = sb("mv", [128, G, 2])
        eps_t = sb("eps_t", [128, NBLK * G])
        mhalf = sb("mhalf", [128, NBLK * G])
        rstd = sb("rstd", [128, G])
        mv_all = sb("mv_all", [128, NBLK * G, 2])
        rstd_all = sb("rstd_all", [128, NBLK * G])
        rt = sb("rt", [128, 12, G * E])
        logit, eq1, key1, hot1, logit2, eq2, key2, hot2, gates_a, gates_b, gates_n, gates = (
            rt[:, k, :].rearrange("p (g e) -> p g e", e=E) for k in range(12))
        rv = sb("rv", [128, 8, G])
        top1, arg1, top2, arg2, dtop, etop, g1, g2 = (rv[:, k, :] for k in range(8))
        dsum = sb("dsum", [128, G])
        rank_w = sb("rank_w", [128, E])
        gates_T = sb("gates_T", [E, TOK])

        wq_sb = sb("wq_sb", [128, D])
        rw_sb = sb("rw_sb", [128, E])
        rb_sb = sb("rb_sb", [128, E])
        b1_sb = sb("b1_sb", [128, E, FC])
        b2_sb = sb("b2_sb", [E, D])
        wqb_col = sb("wqb_col", [128, 1])
        w2_col = sb("w2_col", [128, 1])
        w2b_col = sb("w2b_col", [128, 1])
        mod_T = sb("mod_T", [128, 4, B])
        g_scale = sb("g_scale", [128, G, D])
        g_shift = sb("g_shift", [128, G, D])
        g_ffn = sb("g_ffn", [128, G, D])

        wmod_sb = hidden[:, 0, 0:2, :].rearrange("p a t -> p (a t)")[:, 0:6 * D]
        c_sb = hidden[0:B, 0, 2, 0:128]
        c_exp = hidden[0:B, 0, 2, 128:256]
        c_den = hidden[0:B, 0, 2, 256:384]
        c_silu = hidden[0:B, 0, 2, 384:512]
        c_T = hidden[:, 0, 3, 0:B]
        c_rep = hidden[:, 1, 0, :].rearrange("p (g q) -> p g q", g=G)
        ga_sb = hidden[:, 1, 1, :].rearrange("p (g q) -> p g q", g=G)
        ga_abs = hidden[:, 1, 2, :].rearrange("p (g q) -> p g q", g=G)
        ga_sgn = hidden[:, 1, 3, :].rearrange("p (g q) -> p g q", g=G)
        lng_bc = hidden[:, 0, 3, 128:256]
        lnb_bc = hidden[:, 0, 3, 256:384]
        b1_rows = hidden[0:E * FC, 0, 3, 384:512]

        s_x = sem("s_x")
        s_cond = sem("s_cond")
        s_attn_w = sem("s_attn_w")
        s_w1 = sem("s_w1")
        s_w2 = sem("s_w2")
        s_router = sem("s_router")
        s_const = sem("s_const")
        s_pool = sem("s_pool")
        s_cexp = sem("s_cexp")
        s_pro = sem("s_pro")
        s_ct = sem("s_ct")
        s_ctrep = sem("s_ctrep")
        s_mod = sem("s_mod")
        s_moded = sem("s_moded")
        s_gprod = sem("s_gprod")
        s_mv1 = sem("s_mv1")
        s_rstd1 = sem("s_rstd1")
        s_xn1 = sem("s_xn1")
        s_xt1 = sem("s_xt1")
        s_hmul = sem("s_hmul")
        s_h = sem("s_h")
        s_shift = sem("s_shift")
        s_rows_ps = sem("s_rows_ps")

        s_h2c = sem("s_h2c")
        s_accc = sem("s_accc")
        s_hid_ps = sem("s_hid_ps")
        s_hid = sem("s_hid")
        s_y = sem("s_y")
        s_yacc = sem("s_yacc")
        s_mulgb = sem("s_mulgb")
        s_outsb = sem("s_outsb")
        s_out = sem("s_out")

        s_tanh = sem("s_tanh")
        s_yT = sem("s_yT")
        s_ytok = sem("s_ytok")
        s_st = sem("s_st")
        s_mvv = sem("s_mvv")
        s_var = sem("s_var")
        s_rs = sem("s_rs")
        s_z = sem("s_z")
        s_zg = sem("s_zg")
        s_x1 = sem("s_x1")
        s_xn2 = sem("s_xn2")
        s_xt2 = sem("s_xt2")
        s_h2m = sem("s_h2m")
        s_h2 = sem("s_h2")
        s_lg = sem("s_lg")
        s_rt = sem("s_rt")
        s_etop = sem("s_etop")
        s_gt_ps = sem("s_gt_ps")
        s_gt = sem("s_gt")
        s_b2 = sem("s_b2")
        s_acc0 = sem("s_acc0")

        s_q_ps = sem("s_q_ps")
        s_q = sem("s_q")
        s_s_ps = sem("s_s_ps")
        s_s = sem("s_s")
        s_sm = sem("s_sm")
        s_cen = sem("s_cen")
        s_ez = sem("s_ez")
        s_p = sem("s_p")
        s_pT_ps = sem("s_pT_ps")
        s_pT = sem("s_pT")
        s_o_ps = sem("s_o_ps")
        s_o = sem("s_o")
        s_oT_ps = sem("s_oT_ps")
        s_oT = sem("s_oT")
        s_r_ps = sem("s_r_ps")
        s_r = sem("s_r")
        s_cross = sem("s_cross")
        s_max = sem("s_max")
        s_e = sem("s_e")
        s_prod = sem("s_prod")
        s_sum = sem("s_sum")
        s_zall = sem("s_zall")
        s_zinv = sem("s_zinv")
        s_col = sem("s_col")
        s_row = sem("s_row")
        s_coef = sem("s_coef")
        s_v_ps = sem("s_v_ps")
        s_v = sem("s_v")
        s_vT_ps = sem("s_vT_ps")
        s_vT = sem("s_vT")
        s_ring = sem("s_ring")

        block = ctx.enter_context(nc.Block())

        def wait_apart(eng, semaphore, value):
            value = value if isinstance(value, int) else eng.snap(value)
            eng.wait_ge(s_const, 1)
            eng.wait_ge(semaphore, value)

        @block.sync
        def _(sp):
            sp.dma_start(c_sb, c).then_inc(s_cond, 16)
            sp.dma_start(wmod_sb, wmod).then_inc(s_cond, 16)
            sp.dma_start(b1_rows, b1.rearrange("e (c p) -> (e c) p", p=128)).then_inc(s_cond, 16)
            for blk in range(NBLK):
                for g in range(G):
                    sp.dma_start(x_sb[:, blk, g, :],
                                 feature[GB * g:GB * (g + 1), TB * blk:TB * (blk + 1), :]).then_inc(s_x, 16)
            sp.dma_start(wq_sb[:, :], wq_w).then_inc(s_attn_w, 16)
            sp.dma_start(wqb_col[:, :], wq_b.rearrange("(d a) -> d a", a=1)).then_inc(s_attn_w, 16)
            sp.dma_start(w2_col[:, :], w2_w.rearrange("(d a) -> d a", a=1)).then_inc(s_attn_w, 16)
            sp.dma_start(w2b_col[:, :], w2_b.rearrange("(d a) -> d a", a=1).to_broadcast([128, 1])
                         ).then_inc(s_attn_w, 16)
            sp.dma_start(lng_bc, ln_g.rearrange("(a d) -> a d", a=1).to_broadcast([128, D])).then_inc(s_attn_w, 16)
            sp.dma_start(lnb_bc, ln_b.rearrange("(a d) -> a d", a=1).to_broadcast([128, D])).then_inc(s_attn_w, 16)
            sp.dma_start(rw_sb[:, :], router_w).then_inc(s_router, 16)
            sp.dma_start(rb_sb[:, :], router_b.rearrange("(a e) -> a e", a=1).to_broadcast([128, E])
                         ).then_inc(s_router, 16)
            sp.dma_start(b2_sb[:, :], b2).then_inc(s_router, 16)
            sp.dma_start(w1_sb[:, :, :], W1.rearrange("e d f -> d e f")).then_inc(s_w1, 16)
            for e in range(E):
                sp.dma_start(w2_sb[:, e, :, :], W2[e].rearrange("(c p) d -> p c d", p=128)).then_inc(s_w2, 16)

            def store_values(s, slot):
                sp.wait_ge(s_v, s + 1)
                for g in range(G):
                    sp.dma_start(ring_rows[TB * slot:TB * (slot + 1), GB * g:GB * (g + 1), :],
                                 v_rows[Q32 * g:Q32 * g + TB, :, :]).then_inc(s_ring, 16)

            def store_result(s):
                sp.wait_ge(s_outsb, s + 1)
                for g in range(G):
                    sp.dma_start(out[GB * g:GB * (g + 1), bass.ds(s * TB, TB), :],
                                 out_sb[:, g, :]).then_inc(s_out, 16)

            with sp.Fori(0, NSCAN // NSLOT) as k:
                for slot in range(NSLOT):
                    store_values(k * NSLOT + slot, slot)
                    store_result(k * NSLOT + slot)
            with sp.Fori(NSCAN, NBLK) as s:
                store_result(s)
            sp.wait_ge(s_out, 16 * G * NBLK + SEED)
            sp.wait_ge(s_ring, 16 * G * NSCAN + ROWS0)

        @block.gpsimd
        def _(pool):
            n = [0]

            def order(ins):
                ins.then_inc(s_pool, 1)
                n[0] += 1
                pool.wait_ge(s_pool, n[0])

            order(pool.memset(mask[:, :, :], 0.0))
            order(pool.memset(below[:, :], 1.0))
            order(pool.memset(diag[:, :], 0.0))
            order(pool.memset(unit[:, :], 0.0))
            order(pool.memset(ident[:, :], 0.0))
            order(pool.memset(q_blk[:, :, :], 0.0))
            order(pool.memset(r_pad[:, :, :], 0.0))
            order(pool.memset(coef[:, :, :], 0.0))
            order(pool.memset(eps_t[:, :], LN_EPS))
            order(pool.memset(mhalf[:, :], -0.5))
            for e in range(E):
                order(pool.memset(rank_w[:, e:e + 1], float(E - e)))
            pool.wait_ge(s_pool, n[0])
            order(pool.memset(unit[:, TB - 1:TB], 1.0))
            order(pool.affine_select(out=ident[:, :], in_=ident[:, :], compare_op=ALU.not_equal, fill=1.0,
                                     base=0, pattern=[[-1, 128]], channel_multiplier=1))
            for g in range(G):
                rows = slice(Q32 * g, Q32 * (g + 1))
                order(pool.affine_select(out=below[rows, :], in_=below[rows, :], compare_op=ALU.is_gt, fill=0.0,
                                         base=0, pattern=[[-1, TB]], channel_multiplier=1))
                order(pool.affine_select(out=diag[rows, :], in_=diag[rows, :], compare_op=ALU.not_equal, fill=1.0,
                                         base=0, pattern=[[-1, TB]], channel_multiplier=1))
                for q in range(NSLOT):
                    m = mask[rows, q, TB * q:TB * (q + 1)]
                    order(pool.affine_select(out=m, in_=m, compare_op=ALU.is_ge, fill=MASKED,
                                             base=0, pattern=[[1, TB]], channel_multiplier=-1))
            pool.wait_ge(s_pool, n[0])
            pool.memset(small[:, :], 0.0).then_inc(s_const, 1)

            pool.wait_ge(s_mv1, 1)
            pool.tensor_tensor(rstd_all[:, :], mv_all[:, :, 1], eps_t[:, :], ALU.add).then_inc(s_rstd1, 1)
            pool.wait_ge(s_rstd1, 1)
            pool.tensor_tensor(rstd_all[:, :], rstd_all[:, :], mhalf[:, :], ALU.pow).then_inc(s_rstd1, 1)

            def rstd_of(n_th):
                pool.wait_ge(s_mvv, n_th * G)
                pool.tensor_tensor(rstd[:, :], mv[:, :, 1], eps_t[:, 0:G], ALU.add).then_inc(s_var, 1)
                pool.wait_ge(s_var, n_th)
                pool.tensor_tensor(rstd[:, :], rstd[:, :], mhalf[:, 0:G], ALU.pow).then_inc(s_rs, 1)

            with pool.Fori(0, NBLK) as s:
                rstd_of(2 * s + 1)
                rstd_of(2 * s + 2)

        @block.scalar
        def _(act):
            act.wait_ge(s_cond, 48)
            act.activation(c_exp, c_sb, ACT.Exp, scale=-1.0).then_inc(s_cexp, 1)

            def tanh_values(s1, slot):
                wait_apart(act, s_yT, s1)
                act.activation(gate_T[:, :].rearrange("p (b t) -> p b t", t=TB),
                               ring_T[:, :, bass.ds(slot * TB, TB)], ACT.Tanh).then_inc(s_tanh, 1)

            def top_exp(s1):
                act.wait_ge(s_rt, s1 * N_RT + RT_DTOP)
                act.activation(etop, dtop, ACT.Exp).then_inc(s_etop, 1)

            def relu(s, t):
                e, f = t // FC, t % FC
                act.wait_ge(s_hid_ps, s * TICKS + t + 1)
                if e >= 2:
                    act.wait_ge(s_y, s * TICKS + FC * (e - 1))
                act.activation(hidden[:, e % 2, f, :], ps_h[:, t % 2, :], ACT.Relu,
                               bias=b1_sb[:, e, f:f + 1]).then_inc(s_hid, 1)

            def window_exp(s):
                act.wait_ge(s_cen, s + 1)
                act.activation(prob[:, :, :], score[:, :, :], ACT.Exp).then_inc(s_p, 1)

            def zero_exp(s):
                act.activation(z_zero, m_old, ACT.Exp, scale=-1.0, bias=w2b_col[:, 0:1]).then_inc(s_ez, 1)

            def step_exp(s, j):
                act.wait_ge(s_max, s * TB + j + 1)
                act.activation(wgt[:, j, 0:j + 1], cross[:, 0:j + 1, j], ACT.Exp,
                               bias=neg_max[:, j:j + 1], accum_out=z_sum[:, j:j + 1]).then_inc(s_e, 1)

            act.wait_ge(s_vT, 1)
            act.wait_ge(s_const, 1)
            tanh_values(0, 0)
            top_exp(0)
            act.wait_ge(s_router, 16 * 3)
            act.wait_ge(s_attn_w, 16 * 6)

            def body(s, epi, scan):
                for t in range(TICKS):
                    relu(s, t)
                    if epi and t == 0:
                        tanh_values(s + 1, (s + 1) % NSLOT)
                    if epi and t == EPI_EXP:
                        top_exp(s + 1)
                    if scan and t == 3:
                        window_exp(s)
                        zero_exp(s)
                    if scan and STEP0 <= t < STEP0 + TB:
                        step_exp(s, t - STEP0)

            with act.Fori(0, NSCAN) as s:
                body(s, True, True)
            with act.Fori(NSCAN, NBLK - 1) as s:
                body(s, True, False)
            body(NBLK - 1, False, False)

        @block.tensor
        def _(pe):
            pe.wait_ge(s_const, 1)
            pe.wait_ge(s_pro, PRO_SILU)
            pe.wait_ge(s_cond, 48)
            pe.transpose(ps_epi[:, B:B + E * FC], b1_rows, ident[0:E * FC, 0:E * FC])
            pe.transpose(ps_epi[:, 0:B], c_silu, ident[0:B, 0:B]).then_inc(s_ct, 1)
            pe.wait_ge(s_pro, PRO_CT)
            for n, k in enumerate((0, 1, 3, 4)):
                m = pe.matmul(ps_scan[:, B * n:B * (n + 1)], wmod_sb[:, D * k:D * (k + 1)], c_T,
                              start=True, stop=True)
            m.then_inc(s_mod, 1)
            pe.wait_ge(s_ctrep, 1)
            for n, k in enumerate((2, 5)):
                for g in range(G):
                    m = pe.matmul(ps_wide[:, 512 * n + D * g:512 * n + D * (g + 1)], c_rep[:, g, :],
                                  wmod_sb[:, D * k:D * (k + 1)], start=True, stop=True)
            m.then_inc(s_gprod, 1)

            def transpose_groups(dst, src, sem_done):
                for g in range(G):
                    m = pe.transpose(dst[:, 128 * g:128 * (g + 1)], src[:, 128 * g:128 * (g + 1)], ident[:, :])
                m.then_inc(sem_done, 1)

            z_flat = z_sb[:, :, :].rearrange("p g d -> p (g d)")
            with pe.Fori(0, NBLK) as blk:
                pe.wait_ge(s_xn1, blk + 1)
                pe.wait_ge(s_h, blk + SEED)
                transpose_groups(ps_epi, z_flat, s_xt1)

            for n in range(B // 8):
                if n:
                    pe.wait_ge(s_ring, n)
                else:
                    pe.wait_ge(s_vT, 1)
                    pe.wait_ge(s_pro, PRO_GATES)
                for b in range(8):
                    m = pe.transpose(ps_wide[0:W, 128 * b:128 * (b + 1)], ring_T[:, 8 * n + b, :], ident[:, :])
                m.then_inc(s_rows_ps, 1)

            def y_to_rows(s1):
                pe.wait_ge(s_yT, s1 + 1)
                transpose_groups(ps_epi, y_T, s_ytok)

            def xn_to_cols(s1):
                pe.wait_ge(s_xn2, s1 + 1)
                transpose_groups(ps_epi, z_flat, s_xt2)

            def logits(s1):
                pe.wait_ge(s_h2, s1 + 1)
                for g in range(G):
                    m = pe.matmul(ps_epi[:, E * g:E * (g + 1)], h2_next[:, 128 * g:128 * (g + 1)], rw_sb[:, :],
                                  start=True, stop=True)
                m.then_inc(s_lg, 1)

            def gates_to_cols(s1):
                pe.wait_ge(s_rt, (s1 + 1) * N_RT)
                for g in range(G):
                    m = pe.transpose(ps_epi[0:E, 128 * g:128 * (g + 1)], gates_n[:, g, :], ident[:, :])
                m.then_inc(s_gt_ps, 1)

            def bias2(s1):
                wait_apart(pe, s_gt, s1 + 1)
                for g in range(G):
                    m = pe.matmul(ps_epi[:, D * g:D * (g + 1)], gates_T[:, 128 * g:128 * (g + 1)], b2_sb[:, :],
                                  start=True, stop=True)
                m.then_inc(s_b2, 1)

            def queries(s):
                pe.wait_ge(s_r, s * N_R + SEED)
                pe.matmul(ps_scan[:, :], wq_sb[:, :], h_T[:, s + NSLOT, :], start=True, stop=True).then_inc(s_q_ps, 1)

            def scores(s):
                pe.wait_ge(s_q, s + 1)
                wait_apart(pe, s_vT, s + 1)
                for b in range(B):
                    g, b8 = b // GB, b % GB
                    m = pe.matmul(ps_scan[Q32 * g:Q32 * (g + 1), W * b8:W * (b8 + 1)], q_blk[:, b, :],
                                  ring_T[:, b, :], start=True, stop=True)
                m.then_inc(s_s_ps, 1)

            def probs_to_cols(s):
                wait_apart(pe, s_p, s + SEED + 1)
                for b8 in range(GB):
                    m = pe.transpose(ps_wide[0:W, 128 * b8:128 * (b8 + 1)], prob[:, b8, :], ident[:, :])
                m.then_inc(s_pT_ps, 1)

            def weigh_old(s):
                wait_apart(pe, s_pT, s + 1)
                for b in range(B):
                    g, b8 = b // GB, b % GB
                    m = pe.matmul(ps_wide[Q32 * g:Q32 * (g + 1), D * b8:D * (b8 + 1)],
                                  prob_T[:, b8, Q32 * g:Q32 * (g + 1)], ring_rows[:, b, :], start=True, stop=True)
                m.then_inc(s_o_ps, 1)

            def rows_to_cols(src, sem_ready, sem_done, s):
                pe.wait_ge(sem_ready, s + 1)
                for b8 in range(GB):
                    m = pe.transpose(ps_wide[:, 128 * b8:128 * (b8 + 1)], src[:, b8, :], ident[:, :])
                m.then_inc(sem_done, 1)

            def cross_scores(s):
                wait_apart(pe, s_oT, s + 1)
                for b in range(B):
                    g, b8 = b // GB, b % GB
                    m = pe.matmul(ps_scan[Q32 * g:Q32 * (g + 1), TB * b8:TB * (b8 + 1)], q_blk[:, b, :],
                                  o_T[:, b, :], start=True, stop=True)
                m.then_inc(s_r_ps, 1)

            def values(s):
                wait_apart(pe, s_coef, s + 1)
                for b in range(B):
                    g, b8 = b // GB, b % GB
                    quad = slice(Q32 * g, Q32 * (g + 1))
                    m = pe.matmul(ps_wide[quad, D * b8:D * (b8 + 1)], coef[quad, :, b8], o_rows[quad, b8, :],
                                  start=True, stop=True)
                m.then_inc(s_v_ps, 1)

            def mm1(s, t):
                e, f = t // FC, t % FC
                if t == 0:
                    pe.wait_ge(s_h2c, s + 1)
                pe.wait_ge(s_hid, s * TICKS + SEED + max(t - 1, 0))
                pe.matmul(ps_h[:, t % 2, :], w1_sb[:, e, 128 * f:128 * (f + 1)], h2_T[:, :],
                          start=True, stop=True).then_inc(s_hid_ps, 1)

            def mm2(s, t):
                e, g = t // FC, t % FC
                if g == 0:
                    pe.wait_ge(s_hid, s * TICKS + SEED + FC * (e + 1))
                    if e >= 2:
                        pe.wait_ge(s_yacc, s * TICKS + SEED + FC * (e - 1))
                    else:
                        pe.wait_ge(s_yacc, s * TICKS + SEED)
                for f in range(FC):
                    m = pe.matmul(ps_y[:, e % 2, D * g:D * (g + 1)], hidden[:, e % 2, f, 128 * g:128 * (g + 1)],
                                  w2_sb[:, e, f, :], start=(f == 0), stop=(f == FC - 1))
                m.then_inc(s_y, 1)

            pe.wait_ge(s_attn_w, 16 * 6)
            pe.wait_ge(s_router, 16 * 3)
            y_to_rows(0)
            xn_to_cols(0)
            logits(0)
            gates_to_cols(0)
            bias2(0)
            pe.wait_ge(s_w1, 16)
            pe.wait_ge(s_w2, 16 * E)

            def body(s, epi, scan):
                for t in range(TICKS + FC):
                    if scan and t == 4:
                        pe.wait_ge(s_ring, 16 * G * s + ROWS0)
                    if t < TICKS:
                        mm1(s, t)
                    if t >= FC:
                        mm2(s, t - FC)
                    if epi:
                        for when, step in ((2, y_to_rows), (6, xn_to_cols), (8, logits), (13, gates_to_cols),
                                           (15, bias2)):
                            if t == when:
                                step(s + 1)
                    if scan:
                        if t == 0:
                            queries(s)
                        if t == 1:
                            scores(s)
                        if t == 4:
                            probs_to_cols(s)
                        if t == 6:
                            weigh_old(s)
                        if t == 8:
                            rows_to_cols(o_rows, s_o, s_oT_ps, s)
                        if t == 10:
                            cross_scores(s)
                        if t == STEP0 + TB:
                            values(s)
                        if t == STEP0 + TB + 2:
                            rows_to_cols(v_rows, s_v, s_vT_ps, s)

            with pe.Fori(0, NSCAN) as s:
                body(s, True, True)
            with pe.Fori(NSCAN, NBLK - 1) as s:
                body(s, True, False)
            body(NBLK - 1, False, False)

        @block.vector
        def _(dve):
            n = [0]

            def order(ins):
                ins.then_inc(s_pro, 1)
                n[0] += 1
                dve.wait_ge(s_pro, n[0])

            for free in (s_h, s_xt1, s_r, s_hid, s_yacc, s_p, s_out):
                dve.sem_inc(free, SEED)

            dve.wait_ge(s_const, 1)
            dve.wait_ge(s_cexp, 1)
            order(dve.tensor_scalar(c_den, c_exp, 1.0, None, ALU.add))
            order(dve.reciprocal(c_den, c_den))
            order(dve.tensor_tensor(c_silu, c_sb, c_den, ALU.mult))
            assert n[0] == PRO_SILU
            dve.wait_ge(s_ct, 1)
            dve.tensor_copy(b1_sb[:, :, :].rearrange("p e c -> p (e c)"), ps_epi[:, B:B + E * FC])
            order(dve.tensor_copy(c_T, ps_epi[:, 0:B]))
            assert n[0] == PRO_CT
            for g in range(G):
                m = dve.tensor_copy(c_rep[:, g, :].rearrange("p (b t) -> p b t", t=TB),
                                    c_T[:, GB * g:GB * (g + 1)].unsqueeze(2).to_broadcast([128, GB, TB]))
            m.then_inc(s_ctrep, 1)
            dve.wait_ge(s_mod, 1)
            for k in range(4):
                src = ps_scan[:, B * k:B * (k + 1)]
                if k % 2:
                    m = dve.tensor_scalar(mod_T[:, k, :], src, 1.0, None, ALU.add)
                else:
                    m = dve.tensor_copy(mod_T[:, k, :], src)
            m.then_inc(s_moded, 1)

            def clip(dst, src):
                order(dve.tensor_copy(ga_sb, src))
                order(dve.scalar_tensor_tensor(ga_abs, ga_sb, -1.0, ga_sb, ALU.mult, ALU.max))
                order(dve.tensor_scalar(ga_abs, ga_abs, 0.25, None, ALU.max))
                order(dve.tensor_scalar(ga_sgn, ga_sb, 0.0, 2.0, ALU.is_ge, ALU.mult))
                order(dve.scalar_tensor_tensor(dst, ga_sgn, -1.0, ga_abs, ALU.add, ALU.mult))

            dve.wait_ge(s_gprod, 1)
            dve.wait_ge(s_attn_w, 16 * 6)
            clip(g_scale[:, :, :], ps_wide[:, 0:512].rearrange("p (g d) -> p g d", g=G))
            order(dve.tensor_tensor(g_shift[:, :, :], g_scale[:, :, :],
                                    lnb_bc.unsqueeze(1).to_broadcast([128, G, D]), ALU.mult))
            order(dve.tensor_tensor(g_scale[:, :, :], g_scale[:, :, :],
                                    lng_bc.unsqueeze(1).to_broadcast([128, G, D]), ALU.mult))
            clip(g_ffn[:, :, :], ps_wide[:, 512:1024].rearrange("p (g d) -> p g d", g=G))
            assert n[0] == PRO_GATES

            dve.wait_ge(s_x, 16 * NBLK * G)
            st_all = score[:, :, :].rearrange("p a b -> p (a b)")[:, 0:NBLK * G * 6].rearrange(
                "p (n k) -> p n k", k=6)
            for i in range(NBLK * G):
                m = dve.bn_stats(st_all[:, i, :], x_sb[:, i // G, i % G, :])
            order(m)
            for i in range(NBLK * G):
                m = dve.bn_aggr(mv_all[:, i, :], st_all[:, i, :])
            m.then_inc(s_mv1, 1)
            dve.wait_ge(s_rstd1, 2)
            dve.wait_ge(s_moded, 1)

            with dve.Fori(0, NBLK) as blk:
                dve.wait_ge(s_xt1, blk + SEED)
                for g in range(G):
                    i = blk * G + g
                    m = dve.tensor_scalar(z_sb[:, g, :], x_sb[:, blk, g, :], mv_all[:, i, 0:1],
                                          rstd_all[:, bass.ds(i, 1)], ALU.subtract, ALU.mult)
                m.then_inc(s_xn1, 1)
                dve.wait_ge(s_xt1, blk + SEED + 1)
                dve.tensor_tensor(y_T[:, :].rearrange("p (b t) -> p b t", t=TB),
                                  ps_epi[:, :].rearrange("p (b t) -> p b t", t=TB),
                                  mod_T[:, 1, :].unsqueeze(2).to_broadcast([128, B, TB]),
                                  ALU.mult).then_inc(s_hmul, 1)
                dve.tensor_tensor(x_sb[:, blk, :, :], x_sb[:, blk, :, :], g_shift[:, :, :],
                                  ALU.add).then_inc(s_shift, 1)
                dve.wait_ge(s_hmul, blk + 1)
                dve.tensor_tensor(h_T[:, blk, :].rearrange("p (b t) -> p b t", t=TB),
                                  y_T[:, :].rearrange("p (b t) -> p b t", t=TB),
                                  mod_T[:, 0, :].unsqueeze(2).to_broadcast([128, B, TB]),
                                  ALU.add).then_inc(s_h, 1)

            dve.wait_ge(s_h, NBLK + SEED)
            for q in range(NSLOT):
                m = dve.tensor_copy(ring_T[:, :, TB * q:TB * (q + 1)],
                                    h_T[:, q, :].rearrange("p (b t) -> p b t", t=TB))
            m.then_inc(s_vT, 1)
            for k in range(B // 8):
                dve.wait_ge(s_rows_ps, k + 1)
                dve.tensor_copy(ring_rows[:, 8 * k:8 * (k + 1), :],
                                ps_wide[0:W, :].rearrange("p (b d) -> p b d", d=D)).then_inc(s_ring, 1)

            by_batch = "p (b t) -> p b t"

            def gate_h(s1):
                dve.wait_ge(s_tanh, s1 + 1)
                dve.scalar_tensor_tensor(y_T[:, :], gate_T[:, :], 1.0, h_T[:, s1, :], ALU.add,
                                         ALU.mult).then_inc(s_yT, 1)

            def norm_stats(src, n_th):
                for g in range(G):
                    m = dve.bn_stats(stats[:, g, :], src(g))
                m.then_inc(s_st, 1)
                dve.wait_ge(s_st, n_th)
                dve.tensor_copy(idle[:, :], stats[:, G - 1, 0:1])
                for g in range(G):
                    dve.bn_aggr(mv[:, g, :], stats[:, g, :]).then_inc(s_mvv, 1)

            def stats_attn(s1):
                dve.wait_ge(s_ytok, s1 + 1)
                norm_stats(lambda g: ps_epi[:, D * g:D * (g + 1)], 2 * s1 + 1)

            def residual(s1):
                dve.wait_ge(s_rs, 2 * s1 + 1)
                for g in range(G):
                    m = dve.tensor_scalar(z_sb[:, g, :], ps_epi[:, D * g:D * (g + 1)], mv[:, g, 0:1],
                                          rstd[:, g:g + 1], ALU.subtract, ALU.mult)
                m.then_inc(s_z, 1)
                dve.wait_ge(s_z, s1 + 1)
                dve.tensor_tensor(u_sb[:, :, :], z_sb[:, :, :], g_scale[:, :, :], ALU.mult).then_inc(s_zg, 1)
                dve.wait_ge(s_zg, s1 + 1)
                dve.tensor_tensor(x_sb[:, s1, :, :], u_sb[:, :, :], x_sb[:, s1, :, :], ALU.add).then_inc(s_x1, 1)
                wait_apart(dve, s_x1, s1 + 1)
                norm_stats(lambda g: x_sb[:, s1, g, :], 2 * s1 + 2)

            def normalise(s1):
                dve.wait_ge(s_rs, 2 * s1 + 2)
                for g in range(G):
                    m = dve.tensor_scalar(z_sb[:, g, :], x_sb[:, s1, g, :], mv[:, g, 0:1],
                                          rstd[:, g:g + 1], ALU.subtract, ALU.mult)
                m.then_inc(s_xn2, 1)

            def modulate(s1):
                dve.wait_ge(s_xt2, s1 + 1)
                dve.tensor_tensor(y_T[:, :].rearrange(by_batch, t=TB), ps_epi[:, :].rearrange(by_batch, t=TB),
                                  mod_T[:, 3, :].unsqueeze(2).to_broadcast([128, B, TB]),
                                  ALU.mult).then_inc(s_h2m, 1)
                dve.wait_ge(s_h2m, s1 + 1)
                dve.tensor_tensor(h2_next[:, :].rearrange(by_batch, t=TB), y_T[:, :].rearrange(by_batch, t=TB),
                                  mod_T[:, 2, :].unsqueeze(2).to_broadcast([128, B, TB]),
                                  ALU.add).then_inc(s_h2, 1)

            def over_e(v):
                return v.unsqueeze(2).to_broadcast([128, G, E])

            def over_g(v):
                return v.unsqueeze(1).to_broadcast([128, G, E])

            def route_a(s1):
                k = [0]

                def step(ins):
                    ins.then_inc(s_rt, 1)
                    k[0] += 1
                    dve.wait_ge(s_rt, s1 * N_RT + k[0])

                dve.wait_ge(s_lg, s1 + 1)
                step(dve.tensor_tensor(logit, ps_epi[:, 0:G * E].rearrange("p (g e) -> p g e", e=E),
                                       over_g(rb_sb[:, :]), ALU.add))
                for lg, eq, key, hot, top, arg in ((logit, eq1, key1, hot1, top1, arg1),
                                                   (logit2, eq2, key2, hot2, top2, arg2)):
                    if lg is logit2:
                        step(dve.scalar_tensor_tensor(logit2, hot1, TAKEN, logit, ALU.mult, ALU.add))
                    step(dve.tensor_reduce(top, lg, AX.X, ALU.max))
                    step(dve.tensor_tensor(eq, lg, over_e(top), ALU.is_equal))
                    step(dve.tensor_tensor(key, eq, over_g(rank_w[:, :]), ALU.mult))
                    step(dve.tensor_reduce(arg, key, AX.X, ALU.max))
                    step(dve.tensor_tensor(hot, over_g(rank_w[:, :]), over_e(arg), ALU.is_equal))
                ins = dve.tensor_tensor(dtop, top2, top1, ALU.subtract)
                ins.then_inc(s_rt, 1)
                assert k[0] + 1 == RT_DTOP

            def route_b(s1):
                k = [RT_DTOP]

                def step(ins, last=False):
                    ins.then_inc(s_rt, 1)
                    k[0] += 1
                    if not last:
                        dve.wait_ge(s_rt, s1 * N_RT + k[0])

                dve.wait_ge(s_etop, s1 + 1)
                step(dve.tensor_scalar(dsum[:, :], etop, 1.0, None, ALU.add))
                step(dve.reciprocal(g1, dsum[:, :]))
                step(dve.tensor_tensor(g2, etop, g1, ALU.mult))
                step(dve.tensor_tensor(gates_a, hot1, over_e(g1), ALU.mult))
                step(dve.tensor_tensor(gates_b, hot2, over_e(g2), ALU.mult))
                step(dve.tensor_tensor(gates_n, gates_a, gates_b, ALU.add), last=True)
                assert k[0] == N_RT

            def gates_cols(s1):
                dve.wait_ge(s_gt_ps, s1 + 1)
                dve.tensor_copy(gates_T[:, :], ps_epi[0:E, :]).then_inc(s_gt, 1)

            def acc_start(s1):
                dve.wait_ge(s_b2, s1 + 1)
                dve.tensor_copy(acc_next[:, :, :], ps_epi[:, :].rearrange("p (g d) -> p g d", g=G)
                                ).then_inc(s_acc0, 1)

            def take_block(s):
                dve.wait_ge(s_h2, s + 1)
                dve.tensor_copy(h2_T[:, :], h2_next[:, :]).then_inc(s_h2c, 1)
                dve.wait_ge(s_acc0, s + 1)
                dve.tensor_copy(gates, gates_n)
                dve.tensor_copy(acc[:, :, :], acc_next[:, :, :]).then_inc(s_accc, 1)

            def add_expert(s, t):
                e, g = t // FC, t % FC
                if t == 0:
                    dve.wait_ge(s_accc, s + 1)
                else:
                    if e >= 1:
                        dve.wait_ge(s_yacc, s * TICKS + SEED + t - FC + 1)
                if g == 0:
                    dve.wait_ge(s_y, s * TICKS + FC * (e + 1))
                dve.scalar_tensor_tensor(acc[:, g, :], ps_y[:, e % 2, D * g:D * (g + 1)], gates[:, g, e:e + 1],
                                         acc[:, g, :], ALU.mult, ALU.add).then_inc(s_yacc, 1)

            def finish(s):
                dve.wait_ge(s_yacc, s * TICKS + SEED + TICKS)
                dve.tensor_tensor(u_sb[:, :, :], acc[:, :, :], g_ffn[:, :, :], ALU.mult).then_inc(s_mulgb, 1)
                dve.wait_ge(s_out, 16 * G * s + SEED)
                dve.wait_ge(s_mulgb, s + 1)
                dve.tensor_tensor(out_sb[:, :, :], u_sb[:, :, :], x_sb[:, s, :, :], ALU.add).then_inc(s_outsb, 1)

            def queries_out(s):
                dve.wait_ge(s_q_ps, s + 1)
                dve.tensor_scalar(q_blk[:, :, 0:TB], ps_scan[:, :].rearrange(by_batch, t=TB), wqb_col[:, 0:1],
                                  w2_col[:, 0:1], ALU.add, ALU.mult).then_inc(s_q, 1)

            def window_max(s):
                k = [0]

                def step(ins):
                    ins.then_inc(s_sm, 1)
                    k[0] += 1
                    dve.wait_ge(s_sm, s * N_SM + k[0])

                dve.wait_ge(s_s_ps, s + 1)
                dve.wait_ge(s_p, s + SEED)
                step(dve.scalar_tensor_tensor(score[:, :, :], ps_scan[:, :].rearrange("p (b k) -> p b k", k=W),
                                              w2b_col[:, 0:1],
                                              mask[:, s % NSLOT, :].unsqueeze(1).to_broadcast([128, GB, W]),
                                              ALU.add, ALU.add))
                step(dve.tensor_reduce(m_score, score[:, :, :], AX.X, ALU.max))
                step(dve.tensor_scalar(m_old, m_score, w2b_col[:, 0:1], None, ALU.max))
                dve.tensor_tensor(score[:, :, :], score[:, :, :], m_old.unsqueeze(2).to_broadcast([128, GB, W]),
                                  ALU.subtract).then_inc(s_cen, 1)
                step(dve.tensor_scalar(m_rel, m_old, w2b_col[:, 0:1], None, ALU.subtract))

            def window_sum(s):
                dve.wait_ge(s_p, s + SEED + 1)
                dve.tensor_reduce(z_old, prob[:, :, :], AX.X, ALU.add).then_inc(s_sm, 1)
                dve.wait_ge(s_sm, s * N_SM + 5)
                dve.wait_ge(s_ez, s + 1)
                dve.scalar_tensor_tensor(z_less, z_old, -1.0, z_zero, ALU.add, ALU.add).then_inc(s_sm, 1)

            def probs_cols(s):
                dve.wait_ge(s_pT_ps, s + 1)
                dve.tensor_copy(prob_T[:, :, :], ps_wide[0:W, :].rearrange("p (b q) -> p b q", q=128)
                                ).then_inc(s_pT, 1)

            def old_rows(s):
                dve.wait_ge(s_o_ps, s + 1)
                dve.tensor_copy(o_rows[:, :, :], ps_wide[:, :].rearrange("p (b d) -> p b d", d=D)
                                ).then_inc(s_o, 1)

            def old_cols(s):
                dve.wait_ge(s_oT_ps, s + 1)
                dve.tensor_copy(o_T[:, :, :].rearrange("p (g b) t -> p g b t", g=G),
                                ps_wide[:, :].rearrange("p (b g t) -> p g b t", g=G, t=Q32)[:, :, :, 0:TB]
                                ).then_inc(s_oT, 1)

            def build_system(s):
                dve.wait_ge(s_r_ps, s + 1)
                r_v = ps_scan[:, 0:GB * TB].rearrange("p (b j) -> p j b", j=TB)
                dve.tensor_tensor(tmp_r[:, :, :], r_v, below[:, :].unsqueeze(2).to_broadcast([128, TB, GB]),
                                  ALU.mult).then_inc(s_r, 1)
                dve.tensor_tensor(tmp_d[:, :, :], diag[:, :].unsqueeze(2).to_broadcast([128, TB, GB]),
                                  m_rel.unsqueeze(1).to_broadcast([128, TB, GB]), ALU.mult).then_inc(s_r, 1)
                dve.wait_ge(s_sm, (s + 1) * N_SM)
                dve.tensor_copy(r_pad[:, TB, 0:GB], z_less).then_inc(s_r, 1)
                dve.wait_ge(s_r, s * N_R + SEED + 3)
                dve.tensor_tensor(r_pad[:, 0:TB, 0:GB], tmp_r[:, :, :], tmp_d[:, :, :], ALU.add).then_inc(s_r, 1)
                dve.wait_ge(s_r, s * N_R + SEED + 4)
                dve.transpose(cross[:, :, :], r_pad[:, :, :]).then_inc(s_cross, 1)

            def step_max(s, j):
                if j == 0:
                    dve.wait_ge(s_cross, s + 1)
                else:
                    dve.wait_ge(s_col, s * TB + j)
                dve.tensor_reduce(neg_max[:, j:j + 1], cross[:, 0:j + 1, j], AX.X, ALU.max,
                                  negate=True).then_inc(s_max, 1)

            def step_mix(s, j):
                dve.wait_ge(s_e, s * TB + j + 1)
                if j:
                    dve.wait_ge(s_row, s * TB + j)
                dve.tensor_tensor(prod[:, :, 0:j + 1], cross[:, 0:j + 1, 0:TB].rearrange("p l i -> p i l"),
                                  wgt[:, j, 0:j + 1].unsqueeze(1).to_broadcast([128, TB, j + 1]),
                                  ALU.mult).then_inc(s_prod, 1)
                dve.scalar_tensor_tensor(z_all[:, j:j + 1], wgt[:, j, j:j + 1], cross[:, TB, j:j + 1],
                                         z_sum[:, j:j + 1], ALU.mult, ALU.add).then_inc(s_zall, 1)
                dve.wait_ge(s_prod, s * TB + j + 1)
                dve.tensor_reduce(col[:, :], prod[:, :, 0:j + 1], AX.X, ALU.add).then_inc(s_sum, 1)
                dve.wait_ge(s_zall, s * TB + j + 1)
                dve.reciprocal(z_inv[:, j:j + 1], z_all[:, j:j + 1]).then_inc(s_zinv, 1)
                dve.wait_ge(s_sum, s * TB + j + 1)
                dve.wait_ge(s_zinv, s * TB + j + 1)
                dve.tensor_scalar(cross[:, j, 0:TB], col[:, :], z_inv[:, j:j + 1], None,
                                  ALU.mult).then_inc(s_col, 1)

            def step_row(s, j):
                dve.scalar_tensor_tensor(cross[:, 0:j + 1, j], wgt[:, j, 0:j + 1], z_inv[:, j:j + 1],
                                         unit[:, TB - 1 - j:TB], ALU.mult, ALU.mult).then_inc(s_row, 1)

            def coefficients(s):
                dve.wait_ge(s_row, s * TB + TB)
                dve.transpose(coef[:, 0:TB, :], cross[:, 0:TB, :]).then_inc(s_coef, 1)

            def values_out(s):
                dve.wait_ge(s_v_ps, s + 1)
                dve.wait_ge(s_ring, 16 * G * s + ROWS0)
                dve.tensor_copy(v_rows[:, :, :], ps_wide[:, :].rearrange("p (b d) -> p b d", d=D)
                                ).then_inc(s_v, 1)

            def values_cols(s):
                wait_apart(dve, s_vT_ps, s + 1)
                dve.tensor_copy(ring_T[:, :, bass.ds((s % NSLOT) * TB, TB)].rearrange("p (g b) t -> p g b t", g=G),
                                ps_wide[:, :].rearrange("p (b g t) -> p g b t", g=G, t=Q32)[:, :, :, 0:TB]
                                ).then_inc(s_vT, 1)

            dve.wait_ge(s_router, 16 * 3)
            gate_h(0)
            stats_attn(0)
            residual(0)
            normalise(0)
            modulate(0)
            route_a(0)
            route_b(0)
            gates_cols(0)
            acc_start(0)

            def body(s, epi, scan):
                take_block(s)
                for t in range(TICKS + 2 * FC):
                    if t >= 2 * FC:
                        add_expert(s, t - 2 * FC)
                    if epi:
                        for when, step in ((1, gate_h), (3, stats_attn), (4, residual), (5, normalise), (7, modulate),
                                           (9, route_a), (12, route_b), (14, gates_cols), (16, acc_start)):
                            if t == when:
                                step(s + 1)
                    if scan:
                        for when, step in ((0, queries_out), (2, window_max), (4, window_sum), (5, probs_cols),
                                           (7, old_rows), (9, old_cols), (11, build_system),
                                           (STEP0 + TB, coefficients), (STEP0 + TB + 1, values_out),
                                           (STEP0 + TB + 3, values_cols)):
                            if t == when:
                                step(s)
                        j = t - STEP0
                        if 0 <= j < TB:
                            step_max(s, j)
                            if j:
                                step_row(s, j - 1)
                            step_mix(s, j)
                            if j == TB - 1:
                                dve.wait_ge(s_col, s * TB + TB)
                                step_row(s, j)
                finish(s)

            with dve.Fori(0, NSCAN) as s:
                body(s, True, True)
            with dve.Fori(NSCAN, NBLK - 1) as s:
                body(s, True, False)
            body(NBLK - 1, False, False)


SEED = 1
ROWS0 = B // 8
PRO_SILU, PRO_CT, PRO_GATES = 3, 4, 16
RT_DTOP, N_RT = 13, 19
N_SM, N_R = 6, 4
STEP0, EPI_EXP = 13, 11


_INS = ['L0_attn_feature', 'L0_attn_wq_w', 'L0_attn_wq_b', 'L0_attn_w2_w', 'L0_attn_w2_b', 'L0_attn_ln_g',
        'L0_attn_ln_b', 'L0_ffn_router_w', 'L0_ffn_router_b', 'L0_ffn_W1', 'L0_ffn_b1', 'L0_ffn_W2',
        'L0_ffn_b2', 'L0_c', 'L0_wmod']
_OUTS = [((32, 256, 128), 'float32')]


def kernel(**inputs):
    import numpy as _np
    import concourse.bacc as _bacc
    from concourse import mybir as _mybir
    from concourse.bass_utils import run_bass_kernel_spmd as _run

    nc = _bacc.Bacc("TRN2", target_bir_lowering=False, num_devices=1)
    arrays, args = {}, []
    for name in _INS:
        a = _np.ascontiguousarray(inputs[name])
        arrays[f"in_{name}_dram"] = a
        args.append(nc.dram_tensor(f"in_{name}_dram", a.shape, _mybir.dt.from_np(a.dtype), kind="ExternalInput").ap())
    for i, (shape, dtype) in enumerate(_OUTS):
        dt = _mybir.dt.from_np(_np.dtype(dtype))
        args.append(nc.dram_tensor(f"out_{i}_dram", shape, dt, kind="ExternalOutput").ap())
    adaln_block_kernel(nc, *args)
    r = _run(nc, [arrays], core_ids=[0])
    got = tuple(r.results[0][f"out_{i}_dram"] for i in range(len(_OUTS)))
    return got[0]
```

```python
from contextlib import ExitStack

import concourse.bass as bass
from concourse import mybir

F32 = mybir.dt.float32
I32 = mybir.dt.int32
U32 = mybir.dt.uint32
ALU = mybir.AluOpType
ACT = mybir.ActivationFunctionType
AX = mybir.AxisListType

B, T, D = 32, 256, 128
W = 64
TB = 16
NBLK = T // TB
NSLOT = W // TB
G, GB = 4, B // 4
E, F = 8, 512
FC = F // 128
TOK = B * TB
NTOK = B * T
NROWT = NBLK * G
NSCAN = NBLK - NSLOT
LN_EPS = 1e-5
MASKED = -1e37
TAKEN = -3e38
Q32 = 32

CHUNKS = ((0, 6, 56), (6, 4, 42), (10, 3, 32), (13, 3, 32))
TILE0 = [sum(c[2] for c in CHUNKS[:n]) for n in range(len(CHUNKS))]
NTILES = sum(c[2] for c in CHUNKS)
MAXB = max(c[1] for c in CHUNKS)
MAXR = G * MAXB
MAXT = max(c[2] for c in CHUNKS)
RING = 8
LEAD = 5
for _blk0, _nb, _nt in CHUNKS:
    assert _nt >= 2 * G * _nb + E - 1

SEGMENTS = ((0, 3, None, 0, None), (3, 7, 0, 14, None), (7, 10, 1, 14, 0), (10, 12, 2, 16, 1))
TAIL = ((3, 32, (10, 11, 12)),)
TICKS = 21
STEP0 = 2
NEXT_Q = STEP0 + 8

STREAMS = {}


def _streams():
    tile, uses = 0, [0] * RING
    plan = [(("seg", n), c, k, s1 - s0) for n, (s0, s1, c, k, _) in enumerate(SEGMENTS) if k]
    plan += [(("tail", n), c, k, 1) for n, (c, k, _) in enumerate(TAIL)]
    for key, c, k, times in plan:
        STREAMS[key] = (c, k, times, tile, tuple(uses))
        tile += k * times
        for q in range(RING):
            uses[q] += times * ring_uses(k, q)
        CHUNK_USES[c] = tuple(uses)
    assert tile == NTILES
    word = 0
    for key, c, k, times in plan:
        WORD0[key] = word
        PACK.setdefault(c, (word, packed(k), k * times // packed(k)))
        word += k * times // packed(k)
    return word


def ring_uses(k, q):
    return (k - q + RING - 1) // RING


OUT, HIDDEN, RELU, OUTPUT, DONE = 1, 2, 3, 4, 5


def packed(k):
    return min(k // 2, 8)


CHUNK_USES = {}
WORD0, PACK = {}, {}
NWORDS = _streams()


def adaln_block_kernel(nc, feature, wq_w, wq_b, w2_w, w2_b, ln_g, ln_b, router_w, router_b,
                       W1, b1, W2, b2, c, wmod, out):
    h2_dram = nc.dram_tensor("h2_dram", [NTOK, D], F32, kind="Internal").ap()
    y_dram = nc.dram_tensor("y_dram", [1 + 2 * NTOK + 128 * NTILES + RING, D], F32, kind="Internal").ap()
    with ExitStack() as ctx:
        def sb(name, shape, dtype=F32):
            return ctx.enter_context(nc.sbuf_tensor(name, shape, dtype))

        def sem(name):
            return ctx.enter_context(nc.semaphore(name))

        ps_h = ctx.enter_context(nc.psum_tensor("ps_h", [128, 2, 512], F32))
        ps_y = ctx.enter_context(nc.psum_tensor("ps_y", [128, 512], F32))
        ps_x = ctx.enter_context(nc.psum_tensor("ps_x", [128, 512], F32))
        ps_wide = ctx.enter_context(nc.psum_tensor("ps_wide", [128, 1024], F32))
        ps_scan = ctx.enter_context(nc.psum_tensor("ps_scan", [128, 512], F32))
        ps_epi = ctx.enter_context(nc.psum_tensor("ps_epi", [128, 512], F32))

        x_sb = sb("x_sb", [128, NBLK, G, D])
        h_T = sb("h_T", [128, NBLK, TOK])
        w1_sb = sb("w1_sb", [128, E, F + FC])
        w2_sb = sb("w2_sb", [128, E, FC, D])
        ring_rows = sb("ring_rows", [128, 2, GB, D])
        ring_T = sb("ring_T", [128, B, W])
        q_blk = sb("q_blk", [128, B, Q32])
        score = sb("score", [128, GB, W])
        prob = score
        o_rows = sb("o_rows", [128, GB, D])
        s_T = sb("s_T", [128, GB, 2, Q32])
        r_pad = sb("r_pad", [128, TB + 1, Q32])
        cross = sb("cross", [128, TB + 1, Q32])
        prod = sb("prod", [128, TB + 1, TB])
        wgt = sb("wgt", [128, TB, TB])
        coef = sb("coef", [128, Q32, Q32])
        v_rows = sb("v_rows", [128, GB, D])
        prob_T = sb("prob_T", [128, GB, 2, Q32])
        mask = sb("mask", [128, NSLOT, W])
        below = sb("below", [128, TB])
        diag = sb("diag", [128, TB])
        unit = sb("unit", [128, 2 * TB - 1])
        ident = sb("ident", [128, 128])
        small = sb("small", [128, 16 * TB])
        m_score, m_old, z_part, z_zero, m_rel = (small[:, 8 * k:8 * k + 8] for k in range(5))
        neg_max = small[:, 64:64 + TB]
        z_new, z_inv = small[:, 136:137], small[:, 144:145]
        tmp_r = sb("tmp_r", [128, TB, GB])
        tmp_d = sb("tmp_d", [128, TB, GB])
        col = sb("col", [128, TB + 1])

        gate_T = sb("gate_T", [128, 512])
        y_T = sb("y_T", [128, 512])
        z_sb = sb("z_sb", [128, G, D])
        h2_row = sb("h2_row", [128, G, D])
        h2_T = y_T
        stats = sb("stats", [128, G, 6])
        idle = sb("idle", [128, 1])
        mv = sb("mv", [128, G, 2])
        eps_t = sb("eps_t", [128, NROWT])
        mhalf = sb("mhalf", [128, NROWT])
        rstd = sb("rstd", [128, G])
        nmean = sb("nmean", [128, G])
        nmr = sb("nmr", [128, G])
        minus1 = sb("minus1", [128, G])
        mv_all = sb("mv_all", [128, NROWT, 2])
        rstd_all = sb("rstd_all", [128, NROWT])
        rt = sb("rt", [128, 6, G * E])
        logit, eq1, key1, logit2, eq2, key2 = (
            rt[:, k, :].rearrange("p (g e) -> p g e", e=E) for k in range(6))
        rv = sb("rv", [128, 7, G])
        top1, arg1, top2, arg2, dtop, etop, dsum = (rv[:, k, :] for k in range(7))
        rank_w = sb("rank_w", [128, E])
        hot1 = sb("hot1", [128, NROWT, E])
        hot2 = sb("hot2", [128, NROWT, E])
        g1_all = sb("g1_all", [128, NROWT])
        g2_all = sb("g2_all", [128, NROWT])

        lower = sb("lower", [128, 128])
        ones = sb("ones", [128, 128])
        iota_q = sb("iota_q", [128, 128])
        token1 = sb("token1", [128, 2, NROWT])
        spare = sb("spare", [128, MAXT])
        tile_lim = sb("tile_lim", [128, MAXR])
        keep = sb("keep", [128, E * MAXR])
        pick = sb("pick", [128, MAXR, E])
        tot_flat = prod[:, :, :].rearrange("p a b -> p (a b)")
        inc_flat = wgt[:, :, :].rearrange("p a b -> p (a b)")
        tiles_e = sb("tiles_e", [128, E])
        tiles_to = sb("tiles_to", [128, E])
        base_e = sb("base_e", [128, E])
        slot_f = sb("slot_f", [128, 2, MAXR])
        slot_i = sb("slot_i", [128, 2, MAXR], I32)
        part_i = sb("part_i", [128, 2, 2, MAXR], I32)
        lo_f = sb("lo_f", [128, 2, NROWT])
        hi_f = sb("hi_f", [128, 2, NROWT])
        o_flat = o_rows[:, :, :].rearrange("p b t -> p (b t)")
        oh_lo = o_flat[:, 0:256].rearrange("p (c q) -> p c q", c=2)
        oh_hi = o_flat[:, 256:256 + 2 * MAXT].rearrange("p (c q) -> p c q", c=2)
        tab = score[:, :, :].rearrange("p b k -> p (b k)")[:, 0:5 * MAXT].rearrange("p (n j) -> p n j", n=5)
        exp_f = sb("exp_f", [128, MAXT])
        pow8 = sb("pow8", [128, 8])
        word_f = sb("word_f", [128, 8])
        experts = sb("experts", [128, NWORDS], U32)
        take_row = sb("take_row", [128, NTILES], U32)
        give_row = sb("give_row", [128, NTILES], U32)

        xg = sb("xg", [128, RING, D])
        x_T = sb("x_T", [128, 2, 128])
        w1_cur = sb("w1_cur", [128, 2, F])
        b1_cur = sb("b1_cur", [128, 4, FC])
        hid = sb("hid", [128, 2, FC, 128])
        y_out = sb("y_out", [128, RING, D])
        yc = sb("yc", [128, 2, 2, G, D])

        wq_sb = sb("wq_sb", [128, D])
        rw_sb = sb("rw_sb", [128, E])
        rb_sb = sb("rb_sb", [128, E])
        b2_sb = sb("b2_sb", [1, E, D])
        wqb_col = sb("wqb_col", [128, 1])
        wqb_w2 = sb("wqb_w2", [128, 1])
        w2_col = sb("w2_col", [128, 1])
        w2b_col = sb("w2b_col", [128, 1])
        mod_T = sb("mod_T", [128, 2, B])
        g_scale = sb("g_scale", [128, G, D])
        g_ffn = sb("g_ffn", [128, G, D])
        cb_row = sb("cb_row", [128, G, D])
        sb_row = sb("sb_row", [128, G, D])

        early = yc[:, :, :, :, :].rearrange("p a c g d -> p (a c g d)")
        wmod_sb = early[:, 0:6 * D]
        c_sb = early[0:B, 768:896]
        c_exp = early[0:B, 896:1024]
        c_den = early[0:B, 1024:1152]
        c_silu = early[0:B, 1152:1280]
        c_T = early[:, 1280:1280 + B]
        b1_rows = early[0:E * FC, 1312:1440]
        lng_bc = early[:, 1440:1568]
        lnb_bc = early[:, 1568:1696]
        iota_i = oh_lo[:, 0, :].bitcast(I32)
        early2 = hid[:, :, :, :].rearrange("p a c q -> p (a c q)")
        c_rep = early2[:, 0:512].rearrange("p (g q) -> p g q", g=G)
        ga_sb = early2[:, 512:1024].rearrange("p (g q) -> p g q", g=G)
        ga_abs = y_T[:, :].rearrange("p (g q) -> p g q", g=G)
        ga_sgn = z_sb[:, :, :]
        g_shift = h2_row[:, :, :]

        s_x = sem("s_x")
        s_cond = sem("s_cond")
        s_attn_w = sem("s_attn_w")
        s_w1 = sem("s_w1")
        s_w2 = sem("s_w2")
        s_router = sem("s_router")
        s_const = sem("s_const")
        s_pool = sem("s_pool")
        s_cexp = sem("s_cexp")
        s_pro = sem("s_pro")
        s_ct = sem("s_ct")
        s_ctrep = sem("s_ctrep")
        s_mod = sem("s_mod")
        s_moded = sem("s_moded")
        s_gprod = sem("s_gprod")
        s_mv1 = sem("s_mv1")
        s_rstd1 = sem("s_rstd1")
        s_xn1 = sem("s_xn1")
        s_xt1 = sem("s_xt1")
        s_hmul = sem("s_hmul")
        s_h = sem("s_h")
        s_shift = sem("s_shift")
        s_rows_ps = sem("s_rows_ps")


        s_tanh = sem("s_tanh")
        s_yT = sem("s_yT")
        s_ytok = sem("s_ytok")
        s_st = sem("s_st")
        s_st2 = sem("s_st2")
        s_mvv = sem("s_mvv")
        s_var = sem("s_var")
        s_rs = sem("s_rs")
        s_z = sem("s_z")
        s_xn = sem("s_xn")
        s_zg = sem("s_zg")
        s_x1 = sem("s_x1")
        s_lg = sem("s_lg")
        s_rt = sem("s_rt")
        s_etop = sem("s_etop")

        s_q_ps = sem("s_q_ps")
        s_q = sem("s_q")
        s_s_ps = sem("s_s_ps")
        s_sT = sem("s_sT")
        s_s = sem("s_s")
        s_sm = sem("s_sm")
        s_cen = sem("s_cen")
        s_ez = sem("s_ez")
        s_p = sem("s_p")
        s_pT = sem("s_pT")
        s_o_ps = sem("s_o_ps")
        s_o = sem("s_o")
        s_r_ps = sem("s_r_ps")
        s_r = sem("s_r")
        s_cross = sem("s_cross")
        s_max = sem("s_max")
        s_e = sem("s_e")
        s_prod = sem("s_prod")
        s_sum = sem("s_sum")
        s_zsum = sem("s_zsum")
        s_zinv = sem("s_zinv")
        s_col = sem("s_col")
        s_row = sem("s_row")
        s_coef = sem("s_coef")
        s_v_ps = sem("s_v_ps")
        s_v = sem("s_v")
        s_vT_ps = sem("s_vT_ps")
        s_vT = sem("s_vT")
        s_ring = sem("s_ring")

        s_h2a = sem("s_h2a")
        s_h2r = sem("s_h2r")
        s_h2st = sem("s_h2st")
        s_h2ps = sem("s_h2ps")
        s_h2 = sem("s_h2")

        s_route = sem("s_route")
        s_pick = sem("s_pick")
        s_rank = sem("s_rank")
        s_oh = sem("s_oh")
        s_tab = sem("s_tab")
        s_tabs = sem("s_tabs")

        s_xg = [sem(f"s_xg{q}") for q in range(RING)]
        s_xTp = sem("s_xTp")
        s_xT = sem("s_xT")
        s_w1c = sem("s_w1c")
        s_h1 = sem("s_h1")
        s_hid = sem("s_hid")
        s_y = sem("s_y")
        s_yo = sem("s_yo")
        s_give = [sem(f"s_give{q}") for q in range(RING)]
        s_yc = [sem(f"s_yc{b}") for b in range(2)]
        s_cmb = sem("s_cmb")
        s_res = sem("s_res")
        s_out = [sem(f"s_out{b}") for b in range(2)]

        block = ctx.enter_context(nc.Block())

        def wait_apart(eng, semaphore, value):
            value = value if isinstance(value, int) else eng.snap(value)
            eng.wait_ge(s_const, 1)
            eng.wait_ge(semaphore, value)

        @block.sync
        def _(sp):
            sp.dma_start(c_sb, c).then_inc(s_cond, 16)
            sp.dma_start(wmod_sb, wmod).then_inc(s_cond, 16)
            sp.dma_start(b1_rows, b1.rearrange("e (c p) -> (e c) p", p=128)).then_inc(s_cond, 16)
            for blk in range(NBLK):
                for g in range(G):
                    sp.dma_start(x_sb[:, blk, g, :],
                                 feature[GB * g:GB * (g + 1), TB * blk:TB * (blk + 1), :]).then_inc(s_x, 16)
            sp.dma_start(wq_sb[:, :], wq_w).then_inc(s_attn_w, 16)
            sp.dma_start(wqb_col[:, :], wq_b.rearrange("(d a) -> d a", a=1)).then_inc(s_attn_w, 16)
            sp.dma_start(w2_col[:, :], w2_w.rearrange("(d a) -> d a", a=1)).then_inc(s_attn_w, 16)
            sp.dma_start(w2b_col[:, :], w2_b.rearrange("(d a) -> d a", a=1).to_broadcast([128, 1])
                         ).then_inc(s_attn_w, 16)
            sp.dma_start(lng_bc, ln_g.rearrange("(a d) -> a d", a=1).to_broadcast([128, D])).then_inc(s_attn_w, 16)
            sp.dma_start(lnb_bc, ln_b.rearrange("(a d) -> a d", a=1).to_broadcast([128, D])).then_inc(s_attn_w, 16)
            sp.dma_start(rw_sb[:, :], router_w).then_inc(s_router, 16)
            sp.dma_start(rb_sb[:, :], router_b.rearrange("(a e) -> a e", a=1).to_broadcast([128, E])
                         ).then_inc(s_router, 16)
            sp.dma_start(b2_sb[:, :, :], b2.rearrange("(a e) d -> a e d", a=1)).then_inc(s_router, 16)
            sp.dma_start(w1_sb[:, :, 0:F], W1.rearrange("e d f -> d e f")).then_inc(s_w1, 16)
            for e in range(E):
                sp.dma_start(w2_sb[:, e, :, :], W2[e].rearrange("(c p) d -> p c d", p=128)).then_inc(s_w2, 16)


            def store_values(s):
                slot = s % NSLOT
                sp.wait_ge(s_v, 2 * s + 2)
                for g in range(G):
                    row = Q32 * g + TB * (slot % 2)
                    sp.dma_start(ring_rows[row:row + TB, slot // 2, :, :],
                                 v_rows[Q32 * g:Q32 * g + TB, :, :]).then_inc(s_ring, 16)

            def store_h2(blk):
                sp.wait_ge(s_h2r, blk + 1)
                sp.dma_start(h2_dram[TOK * blk:TOK * (blk + 1), :].rearrange("(g p) d -> p g d", p=128),
                             h2_row[:, :, :]).then_inc(s_h2st, 16)

            def load_results(blk):
                b = blk % 2
                for n, (blk0, _, _) in enumerate(CHUNKS):
                    if blk == blk0:
                        for q in range(RING):
                            sp.wait_ge(s_give[q], 16 * CHUNK_USES[n][q] + 16)
                if blk >= 2:
                    sp.wait_ge(s_out[b], 16 * G * (blk // 2))
                else:
                    sp.wait_ge(s_shift, NBLK)
                for k in range(2):
                    rows = 1 + k * NTOK + TOK * blk
                    sp.dma_start(yc[:, b, k, :, :],
                                 y_dram[rows:rows + TOK, :].rearrange("(g p) d -> p g d", p=128)
                                 ).then_inc(s_yc[b], 16)

            def store_result(blk):
                sp.wait_ge(s_res, blk + 1)
                for g in range(G):
                    sp.dma_start(out[GB * g:GB * (g + 1), TB * blk:TB * (blk + 1), :],
                                 yc[:, blk % 2, 0, g, :]).then_inc(s_out[blk % 2], 16)

            for blk in range(NSLOT - 1):
                store_h2(blk)
            for s0, s1, _, _, comb in SEGMENTS:
                for s in range(s0, s1):
                    first = None if comb is None else CHUNKS[comb][0] + 2 * (s - s0)
                    if first is not None:
                        load_results(first)
                        load_results(first + 1)
                        store_result(first)
                    store_h2(s + NSLOT - 1)
                    if first is not None:
                        store_result(first + 1)
                    store_values(s)
            store_h2(NBLK - 1)
            rest = range(TAIL[0][2][0], NBLK)
            for blk in rest[:2]:
                load_results(blk)
            for blk in rest:
                store_result(blk)
                if blk + 2 in rest:
                    load_results(blk + 2)
            sp.wait_ge(s_ring, 16 * G * NSCAN + ROWS0)
            sp.wait_ge(s_h2st, 16 * NBLK + SEED)
            for b in range(2):
                sp.wait_ge(s_out[b], 16 * G * (NBLK // 2))
            for q in range(RING):
                sp.wait_ge(s_give[q], 16 * CHUNK_USES[len(CHUNKS) - 1][q] + 16)

        @block.gpsimd
        def _(pool):
            n = [0]

            def order(ins):
                ins.then_inc(s_pool, 1)
                n[0] += 1
                pool.wait_ge(s_pool, n[0])

            order(pool.memset(mask[:, :, :], 0.0))
            order(pool.memset(below[:, :], 1.0))
            order(pool.memset(diag[:, :], 0.0))
            order(pool.memset(unit[:, :], 0.0))
            order(pool.memset(ident[:, :], 0.0))
            order(pool.memset(q_blk[:, :, :], 0.0))
            order(pool.memset(r_pad[:, 0:TB, :], 0.0))
            order(pool.memset(r_pad[:, TB, :], 1.0))
            order(pool.memset(coef[:, :, :], 0.0))
            order(pool.memset(eps_t[:, :], LN_EPS))
            order(pool.memset(mhalf[:, :], -0.5))
            order(pool.memset(minus1[:, :], -1.0))
            for e in range(E):
                order(pool.memset(rank_w[:, e:e + 1], float(E - e)))
            for i in range(8):
                order(pool.memset(pow8[:, i:i + 1], float(8 ** i)))
            pool.wait_ge(s_pool, n[0])
            order(pool.memset(unit[:, TB - 1:TB], 1.0))
            order(pool.affine_select(out=ident[:, :], in_=ident[:, :], compare_op=ALU.not_equal, fill=1.0,
                                     base=0, pattern=[[-1, 128]], channel_multiplier=1))
            for g in range(G):
                rows = slice(Q32 * g, Q32 * (g + 1))
                order(pool.affine_select(out=below[rows, :], in_=below[rows, :], compare_op=ALU.is_gt, fill=0.0,
                                         base=0, pattern=[[-1, TB]], channel_multiplier=1))
                order(pool.affine_select(out=diag[rows, :], in_=diag[rows, :], compare_op=ALU.not_equal, fill=1.0,
                                         base=0, pattern=[[-1, TB]], channel_multiplier=1))
                for q in range(NSLOT):
                    m = mask[rows, q, TB * q:TB * (q + 1)]
                    order(pool.affine_select(out=m, in_=m, compare_op=ALU.is_ge, fill=MASKED,
                                             base=0, pattern=[[1, TB]], channel_multiplier=-1))
            order(pool.memset(lower[:, :], 1.0))
            order(pool.affine_select(out=lower[:, :], in_=lower[:, :], compare_op=ALU.is_gt, fill=0.0,
                                     base=0, pattern=[[1, 128]], channel_multiplier=-1))
            order(pool.memset(ones[:, :], 1.0))
            order(pool.memset(y_out[:, :, :], 0.0))
            for dst, count, step, base, per_row in (
                    (iota_q[:, :], 128, 1, 0, 0),
                    (token1[:, 0, :], NROWT, 128, 1, 1),
                    (token1[:, 1, :], NROWT, 128, 1 + NTOK, 1),
                    (spare[:, :], MAXT, 128, 1 + 2 * NTOK, 1),
                    (tile_lim[:, :], MAXR, 128, 0, 0)):
                order(pool.iota(iota_i[:, 0:count], [[step, count]], base=base, channel_multiplier=per_row))
                order(pool.tensor_copy(dst, iota_i[:, 0:count]))
            pool.wait_ge(s_pool, n[0])
            pool.memset(small[:, :], 0.0).then_inc(s_const, 1)

            for q in range(RING):
                row = 1 + 2 * NTOK + 128 * NTILES + q
                pool.dma_start(y_dram[row:row + 1, :], y_out[0:1, q, :]).then_inc(s_give[q], 16)

            pool.wait_ge(s_mv1, 1)
            pool.tensor_tensor(rstd_all[:, :], mv_all[:, :, 1], eps_t[:, :], ALU.add).then_inc(s_rstd1, 1)
            pool.wait_ge(s_rstd1, 1)
            pool.tensor_tensor(rstd_all[:, :], rstd_all[:, :], mhalf[:, :], ALU.pow).then_inc(s_rstd1, 1)

            def rstd_of(n_th):
                pool.wait_ge(s_mvv, n_th * G)
                pool.tensor_tensor(rstd[:, :], mv[:, :, 1], eps_t[:, 0:G], ALU.add).then_inc(s_var, 1)
                pool.tensor_tensor(nmean[:, :], mv[:, :, 0], minus1[:, :], ALU.mult).then_inc(s_var, 1)
                pool.wait_ge(s_var, 3 * n_th - 1)
                pool.tensor_tensor(rstd[:, :], rstd[:, :], mhalf[:, 0:G], ALU.pow).then_inc(s_var, 1)
                pool.wait_ge(s_var, 3 * n_th)
                pool.tensor_tensor(nmr[:, :], nmean[:, :], rstd[:, :], ALU.mult).then_inc(s_rs, 1)

            taken_by = [None] * RING

            def gather(key, n):
                chunk, k, _, tile0, _ = STREAMS[key]
                blk0, nb, _ = CHUNKS[chunk]
                q = n % k % RING
                if taken_by[q] is not None:
                    pool.wait_ge(s_xTp, taken_by[q] + 1)
                taken_by[q] = tile0 + n
                pool.indirect_dma_start(xg[:, q, :], None, h2_dram[0:TOK * (blk0 + nb), :],
                                        bass.IndirectOffsetOnAxis(take_row[:, tile0 + n:tile0 + n + 1], 0)
                                        ).then_inc(s_xg[q], 16)

            def scatter(key, n):
                _, k, _, tile0, _ = STREAMS[key]
                q = n % k % RING
                pool.wait_ge(s_yo, tile0 + n + 1 + SEED2)
                pool.indirect_dma_start(y_dram, bass.IndirectOffsetOnAxis(give_row[:, tile0 + n:tile0 + n + 1], 0),
                                        y_out[:, q, :], None).then_inc(s_give[q], 16)

            def begin(key):
                pool.wait_ge(s_tabs, STREAMS[key][0] + 1)
                blk0, nb, _ = CHUNKS[STREAMS[key][0]]
                pool.wait_ge(s_h2st, 16 * (blk0 + nb) + SEED)
                for n in range(LEAD):
                    gather(key, n)

            def body(blk, key, it):
                k, times = STREAMS[key][1:3] if key else (0, 0)
                for t in range(TICKS if blk is not None else k + DONE + 1):
                    if blk is not None and t == 1:
                        rstd_of(2 * blk + 1)
                    if blk is not None and t == EPI_NORM - 1:
                        rstd_of(2 * blk + 2)
                    if t < k and it * k + t + LEAD < k * times:
                        gather(key, it * k + t + LEAD)
                    if 0 <= t - DONE < k:
                        scatter(key, it * k + t - DONE)

            for blk in range(NSLOT - 1):
                body(blk, None, 0)
            for n, (s0, s1, chunk, _, _) in enumerate(SEGMENTS):
                key = ("seg", n) if chunk is not None else None
                if key:
                    begin(key)
                for s in range(s0, s1):
                    body(s + NSLOT - 1, key, s - s0)
            body(NBLK - 1, None, 0)
            for n in range(len(TAIL)):
                begin(("tail", n))
                body(None, ("tail", n), 0)

        @block.scalar
        def _(act):
            act.wait_ge(s_cond, 48)
            act.activation(c_exp, c_sb, ACT.Exp, scale=-1.0).then_inc(s_cexp, 1)
            act.wait_ge(s_const, 1)
            act.wait_ge(s_attn_w, 16 * 6)
            act.wait_ge(s_pro, PRO_GATES)

            def tanh_values(blk, slot, done):
                wait_apart(act, s_yT, blk + SEED)
                wait_apart(act, s_vT, done)
                act.activation(gate_T[:, :].rearrange("p (b t) -> p b t", t=TB),
                               ring_T[:, :, bass.ds(slot * TB, TB)], ACT.Tanh).then_inc(s_tanh, 1)

            def scale_attn(blk):
                act.wait_ge(s_rs, 2 * blk + 1)
                for g in range(G):
                    m = act.activation(z_sb[:, g, :], ps_epi[:, D * g:D * (g + 1)], ACT.Identity,
                                       scale=rstd[:, g:g + 1], bias=nmr[:, g:g + 1])
                m.then_inc(s_z, 1)

            def normalise(blk, g):
                if g == 0:
                    wait_apart(act, s_rs, 2 * blk + 2)
                act.activation(z_sb[:, g, :], x_sb[:, blk, g, :], ACT.Identity,
                               scale=rstd[:, g:g + 1], bias=nmr[:, g:g + 1]).then_inc(s_xn, 1)

            def h2_cols(blk):
                act.wait_ge(s_h2ps, blk + 1)
                act.activation(h2_T[:, :], ps_epi[:, :], ACT.Copy).then_inc(s_h2, 1)

            def top_exp(blk):
                act.wait_ge(s_rt, blk * N_RT + RT_DTOP)
                act.activation(etop, dtop, ACT.Exp).then_inc(s_etop, 1)

            def queries_out(s):
                act.wait_ge(s_q_ps, s + 1)
                act.activation(q_blk[:, :, 0:TB], ps_scan[:, :].rearrange("p (b t) -> p b t", t=TB), ACT.Identity,
                               scale=w2_col[:, 0:1], bias=wqb_w2[:, 0:1]).then_inc(s_q, 1)

            def window_exp(s):
                act.wait_ge(s_cen, s + 1)
                act.activation(prob[:, :, :], score[:, :, :], ACT.Exp).then_inc(s_p, 1)

            def zero_exp(s):
                act.activation(z_zero, m_old, ACT.Exp, scale=-1.0, bias=w2b_col[:, 0:1]).then_inc(s_ez, 1)

            def old_rows(s):
                act.wait_ge(s_o_ps, s + 1 + SEED)
                act.activation(o_rows[:, :, :], ps_wide[:, :].rearrange("p (b d) -> p b d", d=D),
                               ACT.Copy).then_inc(s_o, 1)

            def values_out(s, half):
                act.wait_ge(s_v_ps, 2 * s + 1 + half)
                if half == 0:
                    act.wait_ge(s_ring, 16 * G * s + ROWS0)
                act.activation(v_rows[:, 4 * half:4 * half + 4, :],
                               ps_wide[:, 512 * half:512 * (half + 1)].rearrange("p (b d) -> p b d", d=D),
                               ACT.Copy).then_inc(s_v, 1)

            def step_exp(s, j):
                act.wait_ge(s_max, s * TB + j + 1)
                act.activation(wgt[:, j, 0:j + 1], cross[:, 0:j + 1, j], ACT.Exp,
                               bias=neg_max[:, j:j + 1]).then_inc(s_e, 1)

            def tile_cols(n, i):
                act.wait_ge(s_xTp, n + i + 1)
                act.wait_ge(s_h1, n + i + 1)
                act.activation(x_T[:, i % 2, :], ps_x[:, 0:128], ACT.Copy).then_inc(s_xT, 1)

            def relu(n, i, f):
                if f == 0:
                    act.wait_ge(s_h1, n + i + 1 + SEED2)
                    act.wait_ge(s_y, n + i + 1)
                m = act.activation(hid[:, i % 2, f, :], ps_h[:, i % 2, 128 * f:128 * (f + 1)], ACT.Relu,
                                   bias=b1_cur[:, i % 4, f:f + 1])
                if f == FC - 1:
                    m.then_inc(s_hid, 1)

            def tile_out(n, i, used):
                act.wait_ge(s_y, n + i + 1 + SEED2)
                act.wait_ge(s_give[i % RING], 16 * used + 16)
                act.activation(y_out[:, i % RING, :], ps_y[:, 0:128], ACT.Copy).then_inc(s_yo, 1)

            def body(s, blk, done, scan, key, it, n):
                k = STREAMS[key][1] if key else 0
                for t in range(TICKS if blk is not None else k + DONE + 1):
                    i = t - DONE
                    if 0 <= i < k:
                        tile_out(n, i, STREAMS[key][4][i % RING] + it * ring_uses(k, i % RING) + i // RING)
                    if blk is not None and t == 0:
                        tanh_values(blk, blk % NSLOT, done)
                    if scan:
                        if t == 0:
                            window_exp(s)
                            zero_exp(s)
                        if STEP0 <= t < STEP0 + TB:
                            step_exp(s, t - STEP0)
                        if t == STEP0 + 2:
                            old_rows(s)
                        if t == NEXT_Q:
                            queries_out(s + 1)
                        if t == STEP0 + TB:
                            values_out(s, 0)
                            values_out(s, 1)
                    if blk is not None:
                        if t == 1:
                            scale_attn(blk)
                        if EPI_NORM <= t < EPI_NORM + G:
                            normalise(blk, t - EPI_NORM)
                        if t == EPI_LOGITS:
                            h2_cols(blk)
                        if t == STEP0 + TB:
                            top_exp(blk)
                    if 0 <= t - OUT < k:
                        tile_cols(n, t - OUT)
                    if 0 <= t - RELU < k:
                        for f in range(FC):
                            relu(n, t - RELU, f)

            queries_out(0)
            with act.Fori(0, NSLOT - 1) as blk:
                body(None, blk, SEED2, False, None, 0, 0)
            for n, (s0, s1, chunk, k, _) in enumerate(SEGMENTS):
                key = ("seg", n) if chunk is not None else None
                with act.Fori(s0, s1) as s:
                    tile = s * k + (STREAMS[key][3] - s0 * k) if key else 0
                    body(s, s + NSLOT - 1, 2 * s + SEED2, True, key, s - s0, tile)
            body(None, NBLK - 1, 2 * NSCAN + SEED2, False, None, 0, 0)
            for n in range(len(TAIL)):
                key = ("tail", n)
                body(None, None, None, False, key, 0, STREAMS[key][3])

        @block.tensor
        def _(pe):
            pe.wait_ge(s_const, 1)
            pe.wait_ge(s_pro, PRO_SILU)
            pe.wait_ge(s_cond, 48)
            pe.transpose(ps_epi[:, B:B + E * FC], b1_rows, ident[0:E * FC, 0:E * FC])
            pe.transpose(ps_epi[:, 0:B], c_silu, ident[0:B, 0:B]).then_inc(s_ct, 1)
            pe.wait_ge(s_pro, PRO_CT)
            for n, k in enumerate((0, 1)):
                m = pe.matmul(ps_scan[:, B * n:B * (n + 1)], wmod_sb[:, D * k:D * (k + 1)], c_T,
                              start=True, stop=True)
            m.then_inc(s_mod, 1)
            pe.wait_ge(s_ctrep, 1)
            for dst, k in ((ps_wide[:, 0:512], 2), (ps_wide[:, 512:1024], 5), (ps_h[:, 0, :], 4), (ps_h[:, 1, :], 3)):
                for g in range(G):
                    m = pe.matmul(dst[:, D * g:D * (g + 1)], c_rep[:, g, :],
                                  wmod_sb[:, D * k:D * (k + 1)], start=True, stop=True)
            m.then_inc(s_gprod, 1)

            def transpose_groups(dst, src, sem_done):
                for g in range(G):
                    m = pe.transpose(dst[:, 128 * g:128 * (g + 1)], src[:, 128 * g:128 * (g + 1)], ident[:, :])
                m.then_inc(sem_done, 1)

            z_flat = z_sb[:, :, :].rearrange("p g d -> p (g d)")
            with pe.Fori(0, NBLK) as blk:
                pe.wait_ge(s_xn1, blk + 1)
                pe.wait_ge(s_h, blk + SEED)
                transpose_groups(ps_epi, z_flat, s_xt1)

            for half in range(2):
                if half:
                    pe.wait_ge(s_ring, 1)
                else:
                    pe.wait_ge(s_vT, SEED2)
                    pe.wait_ge(s_pro, PRO_GATES)
                for b in range(B):
                    g, b8 = b // GB, b % GB
                    m = pe.matmul(ps_wide[Q32 * g:Q32 * (g + 1), 128 * b8:128 * (b8 + 1)],
                                  ring_T[:, b, Q32 * half:Q32 * (half + 1)], ident[:, :], start=True, stop=True)
                m.then_inc(s_rows_ps, 1)

            def y_to_rows(blk):
                pe.wait_ge(s_yT, blk + 1 + SEED)
                transpose_groups(ps_epi, y_T, s_ytok)

            def h2_to_cols(blk):
                pe.wait_ge(s_h2r, blk + 1)
                for g in range(G):
                    m = pe.transpose(ps_epi[:, 128 * g:128 * (g + 1)], h2_row[:, g, :], ident[:, :])
                m.then_inc(s_h2ps, 1)

            def logits(blk):
                pe.wait_ge(s_h2, blk + 1)
                for g in range(G):
                    m = pe.matmul(ps_epi[:, E * g:E * (g + 1)], h2_T[:, 128 * g:128 * (g + 1)], rw_sb[:, :],
                                  start=True, stop=True)
                m.then_inc(s_lg, 1)

            def queries(s):
                pe.wait_ge(s_r, s * N_R + SEED)
                pe.matmul(ps_scan[:, :], wq_sb[:, :], h_T[:, (s + NSLOT) % NBLK, :], start=True,
                          stop=True).then_inc(s_q_ps, 1)

            def scores(s):
                pe.wait_ge(s_q, s + 1)
                wait_apart(pe, s_vT, 2 * s + SEED2)
                for b in range(B):
                    g, b8 = b // GB, b % GB
                    m = pe.matmul(ps_wide[Q32 * g:Q32 * (g + 1), W * b8:W * (b8 + 1)], q_blk[:, b, :],
                                  ring_T[:, b, :], start=True, stop=True)
                m.then_inc(s_s_ps, 1)
            def cross_scores(s):
                wait_apart(pe, s_sT, s + 1)
                wait_apart(pe, s_pT, s + 1)
                for b in range(B):
                    g, b8 = b // GB, b % GB
                    quad = slice(Q32 * g, Q32 * (g + 1))
                    for k in range(2):
                        m = pe.matmul(ps_scan[quad, TB * b8:TB * (b8 + 1)], s_T[quad, b8, k, :],
                                      prob_T[quad, b8, k, 0:TB], start=(k == 0), stop=(k == 1))
                m.then_inc(s_r_ps, 1)

            def weigh_old(s):
                for b in range(B):
                    g, b8 = b // GB, b % GB
                    quad = slice(Q32 * g, Q32 * (g + 1))
                    for k in range(2):
                        m = pe.matmul(ps_wide[quad, D * b8:D * (b8 + 1)], prob_T[quad, b8, k, :],
                                      ring_rows[quad, k, b8, :], start=(k == 0), stop=(k == 1))
                m.then_inc(s_o_ps, 1)

            def values(s, half):
                wait_apart(pe, s_coef, s + 1)
                pe.wait_ge(s_o, s + 1)
                for b8 in range(4 * half, 4 * half + 4):
                    for g in range(G):
                        rows = slice(Q32 * g, Q32 * g + TB)
                        m = pe.matmul(ps_wide[Q32 * g:Q32 * (g + 1), D * b8:D * (b8 + 1)], coef[rows, :, b8],
                                      o_rows[rows, b8, :], start=True, stop=True)
                m.then_inc(s_v_ps, 1)

            def values_to_cols(s, half):
                pe.wait_ge(s_v, 2 * s + 1 + half)
                for b8 in range(4 * half, 4 * half + 4):
                    m = pe.transpose(ps_wide[:, 128 * b8:128 * (b8 + 1)], v_rows[:, b8, :], ident[:, :])
                m.then_inc(s_vT_ps, 1)

            def route(n):
                blk0, nb, nt = CHUNKS[n]
                t0, nr = G * blk0, G * nb
                pe.wait_ge(s_pick, n + 1)
                pe.matmul(ps_epi[:, 0:E * nr], lower[:, :], pick[:, 0:nr, :], start=True, stop=True)
                pe.matmul(ps_epi[:, 256:256 + E * nr], ones[:, :], pick[:, 0:nr, :], start=True,
                          stop=True).then_inc(s_rank, 1)

                def place(r, c, first, last):
                    pe.wait_ge(s_oh, 2 * r + c + 1)
                    pe.matmul(ps_epi[:, 0:nt], oh_lo[:, c, :], oh_hi[:, c, 0:nt], start=first,
                              stop=last).then_inc(s_tab, 1)

                place(t0, 0, True, False)
                place(t0, 1, False, False)
                with pe.Fori(t0 + 1, t0 + nr - 1) as r:
                    place(r, 0, False, False)
                    place(r, 1, False, False)
                place(t0 + nr - 1, 0, False, False)
                place(t0 + nr - 1, 1, False, True)
                pe.wait_ge(s_tabs, n + 1)

            def tile_transpose(n, i, used):
                pe.wait_ge(s_xg[i % RING], 16 * used + 16)
                pe.wait_ge(s_xT, n + i + 1)
                pe.transpose(ps_x[:, 0:128], xg[:, i % RING, :], ident[:, :]).then_inc(s_xTp, 1)

            def tile_hidden(n, i):
                pe.wait_ge(s_xT, n + i + 1 + SEED)
                pe.wait_ge(s_w1c, n + i + 1)
                pe.wait_ge(s_hid, n + i + 1)
                for f in range(FC):
                    m = pe.matmul(ps_h[:, i % 2, 128 * f:128 * (f + 1)], w1_cur[:, i % 2, 128 * f:128 * (f + 1)],
                                  x_T[:, i % 2, :], start=True, stop=True)
                m.then_inc(s_h1, 1)

            def tile_output(n, i, e):
                pe.wait_ge(s_hid, n + i + 1 + SEED2)
                pe.wait_ge(s_yo, n + i + SEED2)
                for f in range(FC):
                    pe.matmul(ps_y[:, 0:128], hid[:, i % 2, f, :], w2_sb[:, e, f, :], start=(f == 0), stop=False)
                pe.matmul(ps_y[:, 0:128], ones[0:1, :], b2_sb[0:1, e, :], start=False, stop=True).then_inc(s_y, 1)

            pe.wait_ge(s_attn_w, 16 * 6)
            pe.wait_ge(s_router, 16 * 3)
            pe.wait_ge(s_w1, 16)
            pe.wait_ge(s_w2, 16 * E)

            def body(s, blk, scan, key, it, n):
                k = STREAMS[key][1] if key else 0
                m = packed(k)
                words = [pe.value_load(experts[0:1, bass.ds(it * (k // m) + WORD0[key] + w, 1)], min_val=0,
                                       max_val=8 ** m - 1) for w in range(k // m)] if k else []
                for t in range(TICKS if blk is not None else k + DONE + 1):
                    if scan:
                        if t == 0:
                            scores(s)
                            pe.wait_ge(s_ring, 16 * G * s + ROWS0)
                        if t == 1:
                            cross_scores(s)
                            weigh_old(s)
                        if t == NEXT_Q:
                            queries(s + 1)
                        if t == STEP0 + TB:
                            for half in range(2):
                                values(s, half)
                            for half in range(2):
                                values_to_cols(s, half)
                    if blk is not None:
                        if t == 0:
                            y_to_rows(blk)
                        if t == EPI_COLS:
                            h2_to_cols(blk)
                        if t == EPI_LOGITS:
                            logits(blk)
                    i = t - HIDDEN
                    if 0 <= i < k:
                        tile_hidden(n, i)
                    i = t - OUTPUT
                    if 0 <= i < k:
                        tile_output(n, i, words[i // m] // 8 ** (i % m) % 8)
                    if t < k:
                        tile_transpose(n, t, STREAMS[key][4][t % RING] + it * ring_uses(k, t % RING) + t // RING)

            queries(0)
            with pe.Fori(0, NSLOT - 1) as blk:
                body(None, blk, False, None, 0, 0)
            for n, (s0, s1, chunk, k, _) in enumerate(SEGMENTS):
                key = ("seg", n) if chunk is not None else None
                with pe.Fori(s0, s1) as s:
                    tile = s * k + (STREAMS[key][3] - s0 * k) if key else 0
                    body(s, s + NSLOT - 1, True, key, s - s0, tile)
                if n < len(CHUNKS) - 1:
                    route(n)
            body(None, NBLK - 1, False, None, 0, 0)
            route(len(CHUNKS) - 1)
            for n in range(len(TAIL)):
                key = ("tail", n)
                body(None, None, False, key, 0, STREAMS[key][3])

        @block.vector
        def _(dve):
            n = [0]

            def order(ins):
                ins.then_inc(s_pro, 1)
                n[0] += 1
                dve.wait_ge(s_pro, n[0])

            for free in (s_h, s_xt1, s_r, s_p, s_yT, s_xT, s_h2st, s_o_ps):
                dve.sem_inc(free, SEED)
            for free in (s_h1, s_hid, s_y, s_yo):
                dve.sem_inc(free, SEED2)

            dve.wait_ge(s_const, 1)
            dve.wait_ge(s_cexp, 1)
            order(dve.tensor_scalar(c_den, c_exp, 1.0, None, ALU.add))
            order(dve.reciprocal(c_den, c_den))
            order(dve.tensor_tensor(c_silu, c_sb, c_den, ALU.mult))
            assert n[0] == PRO_SILU
            dve.wait_ge(s_ct, 1)
            dve.tensor_copy(w1_sb[:, :, F:F + FC], ps_epi[:, B:B + E * FC].rearrange("p (e c) -> p e c", c=FC))
            order(dve.tensor_copy(c_T, ps_epi[:, 0:B]))
            assert n[0] == PRO_CT
            for g in range(G):
                m = dve.tensor_copy(c_rep[:, g, :].rearrange("p (b t) -> p b t", t=TB),
                                    c_T[:, GB * g:GB * (g + 1)].unsqueeze(2).to_broadcast([128, GB, TB]))
            m.then_inc(s_ctrep, 1)
            dve.wait_ge(s_mod, 1)
            for k in range(2):
                src = ps_scan[:, B * k:B * (k + 1)]
                if k % 2:
                    m = dve.tensor_scalar(mod_T[:, k, :], src, 1.0, None, ALU.add)
                else:
                    m = dve.tensor_copy(mod_T[:, k, :], src)
            m.then_inc(s_moded, 1)

            def clip(dst, src):
                order(dve.tensor_copy(ga_sb, src))
                order(dve.scalar_tensor_tensor(ga_abs, ga_sb, -1.0, ga_sb, ALU.mult, ALU.max))
                order(dve.tensor_scalar(ga_abs, ga_abs, 0.25, None, ALU.max))
                order(dve.tensor_scalar(ga_sgn, ga_sb, 0.0, 2.0, ALU.is_ge, ALU.mult))
                order(dve.scalar_tensor_tensor(dst, ga_sgn, -1.0, ga_abs, ALU.add, ALU.mult))

            dve.wait_ge(s_gprod, 1)
            dve.wait_ge(s_attn_w, 16 * 6)
            clip(g_scale[:, :, :], ps_wide[:, 0:512].rearrange("p (g d) -> p g d", g=G))
            order(dve.tensor_tensor(g_shift[:, :, :], g_scale[:, :, :],
                                    lnb_bc.unsqueeze(1).to_broadcast([128, G, D]), ALU.mult))
            order(dve.tensor_tensor(g_scale[:, :, :], g_scale[:, :, :],
                                    lng_bc.unsqueeze(1).to_broadcast([128, G, D]), ALU.mult))
            clip(g_ffn[:, :, :], ps_wide[:, 512:1024].rearrange("p (g d) -> p g d", g=G))
            order(dve.tensor_scalar(cb_row[:, :, :], ps_h[:, 0, :].rearrange("p (g d) -> p g d", g=G), 1.0, None,
                                    ALU.add))
            order(dve.tensor_copy(sb_row[:, :, :], ps_h[:, 1, :].rearrange("p (g d) -> p g d", g=G)))
            order(dve.tensor_tensor(wqb_w2[:, :], wqb_col[:, :], w2_col[:, :], ALU.mult))
            assert n[0] == PRO_GATES

            dve.wait_ge(s_x, 16 * NBLK * G)
            st_all = score[:, :, :].rearrange("p a b -> p (a b)")[:, 0:NBLK * G * 6].rearrange(
                "p (n k) -> p n k", k=6)
            for i in range(NBLK * G):
                m = dve.bn_stats(st_all[:, i, :], x_sb[:, i // G, i % G, :])
            order(m)
            for i in range(NBLK * G):
                m = dve.bn_aggr(mv_all[:, i, :], st_all[:, i, :])
            m.then_inc(s_mv1, 1)
            dve.wait_ge(s_rstd1, 2)
            dve.wait_ge(s_moded, 1)

            with dve.Fori(0, NBLK) as blk:
                dve.wait_ge(s_xt1, blk + SEED)
                for g in range(G):
                    i = blk * G + g
                    m = dve.tensor_scalar(z_sb[:, g, :], x_sb[:, blk, g, :], mv_all[:, i, 0:1],
                                          rstd_all[:, bass.ds(i, 1)], ALU.subtract, ALU.mult)
                m.then_inc(s_xn1, 1)
                dve.wait_ge(s_xt1, blk + SEED + 1)
                dve.tensor_tensor(y_T[:, :].rearrange("p (b t) -> p b t", t=TB),
                                  ps_epi[:, :].rearrange("p (b t) -> p b t", t=TB),
                                  mod_T[:, 1, :].unsqueeze(2).to_broadcast([128, B, TB]),
                                  ALU.mult).then_inc(s_hmul, 1)
                dve.tensor_tensor(x_sb[:, blk, :, :], x_sb[:, blk, :, :], g_shift[:, :, :],
                                  ALU.add).then_inc(s_shift, 1)
                dve.wait_ge(s_hmul, blk + 1)
                dve.tensor_tensor(h_T[:, blk, :].rearrange("p (b t) -> p b t", t=TB),
                                  y_T[:, :].rearrange("p (b t) -> p b t", t=TB),
                                  mod_T[:, 0, :].unsqueeze(2).to_broadcast([128, B, TB]),
                                  ALU.add).then_inc(s_h, 1)

            dve.wait_ge(s_h, NBLK + SEED)
            for q in range(NSLOT):
                m = dve.tensor_copy(ring_T[:, :, TB * q:TB * (q + 1)],
                                    h_T[:, q, :].rearrange("p (b t) -> p b t", t=TB))
            m.then_inc(s_vT, 1)
            dve.sem_inc(s_vT, 1)
            for half in range(2):
                dve.wait_ge(s_rows_ps, half + 1)
                dve.tensor_copy(ring_rows[:, half, :, :], ps_wide[:, :].rearrange("p (b d) -> p b d", d=D)
                                ).then_inc(s_ring, 1)

            by_batch = "p (b t) -> p b t"

            def gate_h(blk):
                dve.wait_ge(s_tanh, blk + 1)
                dve.scalar_tensor_tensor(y_T[:, :], gate_T[:, :], 1.0, h_T[:, blk, :], ALU.add,
                                         ALU.mult).then_inc(s_yT, 1)

            def norm_stats(src, n_th):
                for g in range(G):
                    m = dve.bn_stats(stats[:, g, :], src(g))
                m.then_inc(s_st, 1)
                dve.wait_ge(s_st, n_th)
                dve.tensor_copy(idle[:, :], stats[:, G - 1, 0:1])
                for g in range(G):
                    dve.bn_aggr(mv[:, g, :], stats[:, g, :]).then_inc(s_mvv, 1)

            def stats_attn(blk):
                dve.wait_ge(s_ytok, blk + 1)
                norm_stats(lambda g: ps_epi[:, D * g:D * (g + 1)], blk + 1)

            def epilogue(p, blk):
                if p % 2:
                    return
                g = p % 8 // 2
                if P_SCALE <= p < P_SCALE + 8:
                    if g == 0:
                        dve.wait_ge(s_z, blk + 1)
                    dve.tensor_tensor(z_sb[:, g, :], z_sb[:, g, :], g_scale[:, g, :], ALU.mult).then_inc(s_zg, 1)
                if P_RES <= p < P_RES + 8:
                    dve.wait_ge(s_zg, G * blk + g + 1)
                    dve.tensor_tensor(x_sb[:, blk, g, :], z_sb[:, g, :], x_sb[:, blk, g, :], ALU.add).then_inc(s_x1, 1)
                if P_STATS <= p < P_STATS + 8:
                    wait_apart(dve, s_x1, G * blk + g + 1)
                    dve.bn_stats(stats[:, g, :], x_sb[:, blk, g, :]).then_inc(s_st2, 1)
                if P_AGGR <= p < P_AGGR + 8:
                    if g == 0:
                        dve.wait_ge(s_st2, G * blk + G)
                        dve.tensor_copy(idle[:, :], stats[:, G - 1, 0:1])
                    dve.bn_aggr(mv[:, g, :], stats[:, g, :]).then_inc(s_mvv, 1)
                g = (p - P_MOD) % 8 // 2
                if P_MOD <= p < P_MOD + 8:
                    dve.wait_ge(s_xn, G * blk + g + 1)
                    dve.tensor_tensor(z_sb[:, g, :], z_sb[:, g, :], cb_row[:, g, :], ALU.mult).then_inc(s_h2a, 1)
                if P_SHIFT <= p < P_SHIFT + 8:
                    if g == 0:
                        dve.wait_ge(s_h2st, 16 * blk + SEED)
                    dve.wait_ge(s_h2a, G * blk + g + 1)
                    m = dve.tensor_tensor(h2_row[:, g, :], z_sb[:, g, :], sb_row[:, g, :], ALU.add)
                    if g == G - 1:
                        m.then_inc(s_h2r, 1)

            def over_e(v):
                return v.unsqueeze(2).to_broadcast([128, G, E])

            def over_g(v):
                return v.unsqueeze(1).to_broadcast([128, G, E])

            def route_a(blk):
                k = [0]

                def step(ins):
                    ins.then_inc(s_rt, 1)
                    k[0] += 1
                    dve.wait_ge(s_rt, blk * N_RT + k[0])

                dve.wait_ge(s_lg, blk + 1)
                step(dve.tensor_tensor(logit, ps_epi[:, 0:G * E].rearrange("p (g e) -> p g e", e=E),
                                       over_g(rb_sb[:, :]), ALU.add))
                hots = [hot[:, bass.ds(blk * G, G), :] for hot in (hot1, hot2)]
                for lg, eq, key, hot, top, arg in ((logit, eq1, key1, hots[0], top1, arg1),
                                                   (logit2, eq2, key2, hots[1], top2, arg2)):
                    if lg is logit2:
                        step(dve.scalar_tensor_tensor(logit2, hots[0], TAKEN, logit, ALU.mult, ALU.add))
                    step(dve.tensor_reduce(top, lg, AX.X, ALU.max))
                    step(dve.tensor_tensor(eq, lg, over_e(top), ALU.is_equal))
                    step(dve.tensor_tensor(key, eq, over_g(rank_w[:, :]), ALU.mult))
                    step(dve.tensor_reduce(arg, key, AX.X, ALU.max))
                    step(dve.tensor_tensor(hot, over_g(rank_w[:, :]), over_e(arg), ALU.is_equal))
                ins = dve.tensor_tensor(dtop, top2, top1, ALU.subtract)
                ins.then_inc(s_rt, 1)
                assert k[0] + 1 == RT_DTOP

            def route_b(blk):
                k = [RT_DTOP]

                def step(ins, last=False):
                    ins.then_inc(s_rt, 1)
                    k[0] += 1
                    if not last:
                        dve.wait_ge(s_rt, blk * N_RT + k[0])

                dve.wait_ge(s_etop, blk + 1)
                step(dve.tensor_scalar(dsum[:, :], etop, 1.0, None, ALU.add))
                step(dve.reciprocal(g1_all[:, bass.ds(blk * G, G)], dsum[:, :]))
                step(dve.tensor_tensor(g2_all[:, bass.ds(blk * G, G)], etop, g1_all[:, bass.ds(blk * G, G)],
                                       ALU.mult), last=True)
                assert k[0] == N_RT

            n_route = [0]

            def route(n):
                blk0, nb, nt = CHUNKS[n]
                t0, nr = G * blk0, G * nb
                rows, tiles = slice(t0, t0 + nr), slice(TILE0[n], TILE0[n] + nt)
                tot, inc = (v[:, 0:E * nr].rearrange("p (e r) -> p e r", e=E) for v in (tot_flat, inc_flat))
                scratch = [v[:, 0:E * nr].rearrange("p (r e) -> p r e", e=E) for v in (tot_flat, inc_flat)]

                def step(ins):
                    ins.then_inc(s_route, 1)
                    n_route[0] += 1
                    dve.wait_ge(s_route, n_route[0])

                dve.wait_ge(s_rt, N_RT * (blk0 + nb))
                dve.tensor_tensor(pick[:, 0:nr, :], hot1[:, rows, :], hot2[:, rows, :], ALU.add).then_inc(s_pick, 1)
                dve.wait_ge(s_rank, n + 1)
                rank = ps_epi[:, 0:E * nr].rearrange("p (r e) -> p r e", e=E)
                step(dve.tensor_copy(tot, ps_epi[:, 256:256 + E * nr].rearrange("p (r e) -> p e r", e=E)))
                step(dve.memset(keep[:, 0:E * nr], 1.0))
                step(dve.memset(keep[:, 0:E * nr].rearrange("p (e r) -> p e r", e=E)[:, :, 0:1], 0.0))
                step(dve.tensor_tensor_scan(inc_flat[:, 0:E * nr], keep[:, 0:E * nr], tot_flat[:, 0:E * nr], 0.0,
                                            ALU.mult, ALU.add))
                count = pick[:, 0:nr, :].rearrange("p r e -> p (r e)").rearrange("p (e k) -> p e k", e=E)
                step(dve.tensor_tensor(count, inc[:, :, nr - 1:nr].to_broadcast([128, E, nr]),
                                       tile_lim[:, 0:nr].unsqueeze(1).to_broadcast([128, E, nr]), ALU.is_gt))
                step(dve.tensor_reduce(tiles_e[:, :], count, AX.X, ALU.add))
                step(dve.tensor_tensor_scan(tiles_to[:, :], ones[:, 0:E], tiles_e[:, :], 0.0, ALU.mult, ALU.add))
                step(dve.tensor_tensor(base_e[:, :], tiles_to[:, :], tiles_e[:, :], ALU.subtract))
                step(dve.tensor_tensor(inc, inc, tot, ALU.subtract))
                step(dve.scalar_tensor_tensor(inc, base_e[:, :].unsqueeze(2).to_broadcast([128, E, nr]),
                                              128.0, inc, ALU.mult, ALU.add))
                step(dve.tensor_tensor(pick[:, 0:nr, :], rank, inc.rearrange("p e r -> p r e"), ALU.add))
                for k, hot in enumerate((hot1, hot2)):
                    step(dve.tensor_tensor(scratch[k], pick[:, 0:nr, :], hot[:, rows, :], ALU.mult))
                    step(dve.tensor_reduce(slot_f[:, k, 0:nr], scratch[k], AX.X, ALU.add))
                step(dve.tensor_copy(slot_i[:, :, 0:nr], slot_f[:, :, 0:nr]))
                step(dve.tensor_scalar(part_i[:, 0, :, 0:nr], slot_i[:, :, 0:nr], 127, None, ALU.bitwise_and))
                step(dve.tensor_scalar(part_i[:, 1, :, 0:nr], slot_i[:, :, 0:nr], 7, None, ALU.arith_shift_right))
                step(dve.tensor_copy(lo_f[:, :, rows], part_i[:, 0, :, 0:nr]))
                step(dve.tensor_copy(hi_f[:, :, rows], part_i[:, 1, :, 0:nr]))

                def one_hots(r, c, first):
                    if not first:
                        dve.wait_ge(s_tab, 2 * r + c - 1)
                    dve.tensor_scalar(oh_lo[:, c, :], iota_q[:, :], lo_f[:, c, bass.ds(r, 1)], None, ALU.is_equal)
                    dve.tensor_scalar(oh_hi[:, c, 0:nt], iota_q[:, 0:nt], hi_f[:, c, bass.ds(r, 1)],
                                      token1[:, c, bass.ds(r, 1)], ALU.is_equal, ALU.mult).then_inc(s_oh, 1)

                for c in range(2):
                    one_hots(t0, c, t0 == 0)
                with dve.Fori(t0 + 1, t0 + nr - 1) as r:
                    for c in range(2):
                        one_hots(r, c, False)
                for c in range(2):
                    one_hots(t0 + nr - 1, c, False)

                ends = y_T[:, 0:nt * (E - 1)].rearrange("p (j e) -> p j e", e=E - 1)
                step(dve.tensor_tensor(ends, iota_q[:, 0:nt].unsqueeze(2).to_broadcast([128, nt, E - 1]),
                                       tiles_to[:, 0:E - 1].unsqueeze(1).to_broadcast([128, nt, E - 1]), ALU.is_ge))
                step(dve.tensor_reduce(exp_f[:, 0:nt], ends, AX.X, ALU.add))
                word0, m, words = PACK[n]
                in_words = exp_f[:, 0:nt].rearrange("p (w i) -> p w i", i=m)
                step(dve.tensor_tensor(in_words, in_words, pow8[:, 0:m].unsqueeze(1).to_broadcast([128, words, m]),
                                       ALU.mult))
                step(dve.tensor_reduce(word_f[:, 0:words], in_words, AX.X, ALU.add))
                step(dve.tensor_copy(experts[:, word0:word0 + words], word_f[:, 0:words]))

                dve.wait_ge(s_tab, 2 * (t0 + nr))
                number, less, second, empty, away = (tab[:, k, 0:nt] for k in range(5))
                step(dve.tensor_copy(number, ps_epi[:, 0:nt]))
                step(dve.tensor_scalar(less, number, -1.0, 0.0, ALU.add, ALU.max))
                step(dve.tensor_scalar(second, number, float(NTOK), -float(NTOK), ALU.is_gt, ALU.mult))
                step(dve.tensor_tensor(take_row[:, tiles], less, second, ALU.add))
                step(dve.tensor_scalar(empty, number, 0.0, 128.0 * TILE0[n], ALU.is_equal, ALU.mult))
                step(dve.tensor_tensor(less, number, empty, ALU.add))
                step(dve.tensor_scalar(second, number, 0.0, None, ALU.is_equal))
                step(dve.tensor_tensor(away, second, spare[:, 0:nt], ALU.mult))
                dve.tensor_tensor(give_row[:, tiles], away, less, ALU.add).then_inc(s_tabs, 1)
                dve.wait_ge(s_tabs, n + 1)

            def tile_weights(n, i, e):
                wait_apart(dve, s_h1, n + i + 1)
                if i < 2:
                    wait_apart(dve, s_hid, n + i + 1)
                dve.tensor_copy(w1_cur[:, i % 2, :], w1_sb[:, e, 0:F])
                dve.tensor_copy(b1_cur[:, i % 4, :], w1_sb[:, e, F:F + FC]).then_inc(s_w1c, 1)

            def combine(i, blk, b, half):
                g = i % G
                y1, y2 = yc[:, b, 0, g, :], yc[:, b, 1, g, :]
                if i == 0:
                    dve.wait_ge(s_yc[b], 32 * half + 32)
                if i >= G:
                    dve.wait_ge(s_cmb, 15 * blk + i - G + 1)
                if i < G:
                    dve.tensor_scalar(y1, y1, g1_all[:, bass.ds(blk * G + g, 1)], None, ALU.mult).then_inc(s_cmb, 1)
                elif i < 2 * G:
                    dve.scalar_tensor_tensor(y1, y2, g2_all[:, bass.ds(blk * G + g, 1)], y1, ALU.mult,
                                             ALU.add).then_inc(s_cmb, 1)
                elif i < 3 * G:
                    dve.tensor_tensor(y1, y1, g_ffn[:, g, :], ALU.mult).then_inc(s_cmb, 1)
                else:
                    m = dve.tensor_tensor(y1, y1, x_sb[:, blk, g, :], ALU.add)
                    m.then_inc(s_cmb if i < 4 * G - 1 else s_res, 1)

            def window_max(s):
                dve.wait_ge(s_s_ps, s + 1)
                dve.scalar_tensor_tensor(score[:, :, :], ps_wide[:, 0:512].rearrange("p (b k) -> p b k", k=W),
                                         w2b_col[:, 0:1],
                                         mask[:, s % NSLOT, :].unsqueeze(1).to_broadcast([128, GB, W]),
                                         ALU.add, ALU.add).then_inc(s_sm, 1)
                dve.wait_ge(s_sm, s * N_SM + 1)
                dve.tensor_reduce(m_score, score[:, :, :], AX.X, ALU.max).then_inc(s_sm, 1)
                dve.wait_ge(s_sm, s * N_SM + 2)
                dve.tensor_scalar(m_old, m_score, w2b_col[:, 0:1], None, ALU.max).then_inc(s_sm, 1)
                dve.wait_ge(s_sm, s * N_SM + 3)
                dve.tensor_tensor(score[:, :, :], score[:, :, :], m_old.unsqueeze(2).to_broadcast([128, GB, W]),
                                  ALU.subtract).then_inc(s_cen, 1)
                dve.transpose(s_T[:, :, :, :].rearrange("p b k i -> p (b k) i"),
                              ps_wide[:, 0:512].rearrange("p (n c) -> p n c", c=Q32)).then_inc(s_sT, 1)
                dve.tensor_scalar(m_rel, m_old, w2b_col[:, 0:1], None, ALU.subtract).then_inc(s_sm, 1)
                dve.wait_ge(s_sm, s * N_SM + 4)
                dve.tensor_tensor(tmp_d[:, :, :], diag[:, :].unsqueeze(2).to_broadcast([128, TB, GB]),
                                  m_rel.unsqueeze(1).to_broadcast([128, TB, GB]), ALU.mult).then_inc(s_sm, 1)

            def window_sum(s):
                dve.wait_ge(s_p, s + SEED + 1)
                dve.wait_ge(s_o_ps, s + SEED)
                dve.transpose(prob_T[:, :, :, :].rearrange("p b k i -> p (b k) i"),
                              prob[:, :, :].rearrange("p b (k c) -> p (b k) c", c=Q32)).then_inc(s_pT, 1)
                dve.tensor_reduce(z_part, prob[:, :, :], AX.X, ALU.add).then_inc(s_sm, 1)
                dve.wait_ge(s_sm, s * N_SM + 6)
                dve.wait_ge(s_ez, s + 1)
                dve.tensor_tensor(r_pad[:, TB, 0:GB], z_part, z_zero, ALU.add).then_inc(s_sm, 1)

            def build_system(s):
                dve.wait_ge(s_r_ps, s + 1)
                r_v = ps_scan[:, 0:GB * TB].rearrange("p (b j) -> p j b", j=TB)
                dve.tensor_tensor(tmp_r[:, :, :], r_v, below[:, :].unsqueeze(2).to_broadcast([128, TB, GB]),
                                  ALU.mult).then_inc(s_r, 1)
                dve.wait_ge(s_r, s * N_R + SEED + 1)
                dve.wait_ge(s_sm, (s + 1) * N_SM)
                dve.tensor_tensor(r_pad[:, 0:TB, 0:GB], tmp_r[:, :, :], tmp_d[:, :, :], ALU.add).then_inc(s_r, 1)
                dve.wait_ge(s_r, s * N_R + SEED + 2)
                dve.transpose(cross[:, :, :], r_pad[:, :, :]).then_inc(s_r, 1)
                dve.wait_ge(s_r, s * N_R + SEED + 3)
                dve.tensor_copy(cross[:, 0:TB, TB], cross[:, TB, 0:TB]).then_inc(s_cross, 1)

            def step_max(s, j):
                if j == 0:
                    dve.wait_ge(s_cross, s + 1)
                else:
                    dve.wait_ge(s_col, s * TB + j)
                dve.tensor_reduce(neg_max[:, j:j + 1], cross[:, 0:j + 1, j], AX.X, ALU.max,
                                  negate=True).then_inc(s_max, 1)

            def step_mix(s, j, place):
                dve.wait_ge(s_e, s * TB + j + 1)
                if j:
                    dve.wait_ge(s_row, s * TB + j)
                dve.tensor_tensor(prod[:, :, 0:j + 1], cross[:, 0:j + 1, 0:TB + 1].rearrange("p l i -> p i l"),
                                  wgt[:, j, 0:j + 1].unsqueeze(1).to_broadcast([128, TB + 1, j + 1]),
                                  ALU.mult).then_inc(s_prod, 1)
                place(4 * j + 1)
                dve.wait_ge(s_prod, s * TB + j + 1)
                dve.tensor_reduce(z_new, prod[:, TB, 0:j + 1], AX.X, ALU.add).then_inc(s_zsum, 1)
                dve.tensor_reduce(col[:, :], prod[:, :, 0:j + 1], AX.X, ALU.add).then_inc(s_sum, 1)
                dve.wait_ge(s_zsum, s * TB + j + 1)
                dve.reciprocal(z_inv, z_new).then_inc(s_zinv, 1)
                place(4 * j + 2)
                dve.wait_ge(s_zinv, s * TB + j + 1)
                dve.tensor_scalar(cross[:, j, 0:TB + 1], col[:, :], z_inv, None, ALU.mult).then_inc(s_col, 1)
                place(4 * j + 3)

            def step_row(s, j):
                dve.scalar_tensor_tensor(cross[:, 0:j + 1, j], wgt[:, j, 0:j + 1], z_inv,
                                         unit[:, TB - 1 - j:TB], ALU.mult, ALU.mult).then_inc(s_row, 1)

            def coefficients(s):
                dve.wait_ge(s_row, s * TB + TB)
                dve.transpose(coef[:, 0:TB, :], cross[:, 0:TB, :]).then_inc(s_coef, 1)

            def values_cols(s, half):
                wait_apart(dve, s_vT_ps, 2 * s + 1 + half)
                dve.tensor_copy(ring_T[:, :, bass.ds((s % NSLOT) * TB, TB)].rearrange(
                                    "p (g b) t -> p g b t", g=G)[:, :, 4 * half:4 * half + 4, :],
                                ps_wide[:, 512 * half:512 * (half + 1)].rearrange(
                                    "p (b g t) -> p g b t", g=G, t=Q32)[:, :, :, 0:TB]).then_inc(s_vT, 1)

            dve.wait_ge(s_router, 16 * 3)
            dve.wait_ge(s_w1, 16)

            def body(s, blk, scan, key, it, n, comb):
                k = STREAMS[key][1] if key else 0
                m = packed(k)

                words = [dve.value_load(experts[0:1, bass.ds(it * (k // m) + WORD0[key] + w, 1)], min_val=0,
                                        max_val=8 ** m - 1) for w in range(k // m)] if k else []

                def place(p):
                    if blk is not None and p < 4 * TB:
                        epilogue(p, blk)
                    if p % 2 and p // 32 < len(comb):
                        combine(p % 32 // 2, *comb[p // 32])

                for t in range(TICKS if blk is not None else k + DONE):
                    j = t - STEP0
                    if blk is not None and t == 0:
                        gate_h(blk)
                    if scan and t == 0:
                        window_max(s)
                    if scan and t == 1:
                        window_sum(s)
                    if blk is not None and t == 1:
                        stats_attn(blk)
                    if scan and t == 1:
                        build_system(s)
                    if scan and 0 <= j < TB:
                        step_max(s, j)
                        if j:
                            step_row(s, j - 1)
                        place(4 * j)
                        step_mix(s, j, place)
                    elif j >= 0 and not scan:
                        for p in range(4):
                            place(4 * j + p)
                    if scan and j == TB:
                        dve.wait_ge(s_col, s * TB + TB)
                        step_row(s, TB - 1)
                        coefficients(s)
                    if blk is not None and j == TB:
                        route_a(blk)
                    if scan and j == TB:
                        values_cols(s, 0)
                        values_cols(s, 1)
                    if blk is not None and j == TB:
                        route_b(blk)
                    i = t - OUT
                    if 0 <= i < k:
                        tile_weights(n, i, words[i // m] // 8 ** (i % m) % 8)

            with dve.Fori(0, NSLOT - 1) as blk:
                body(None, blk, False, None, 0, 0, ())
            for n, (s0, s1, chunk, k, comb) in enumerate(SEGMENTS):
                key = ("seg", n) if chunk is not None else None
                with dve.Fori(s0, s1) as s:
                    tile = s * k + (STREAMS[key][3] - s0 * k) if key else 0
                    pair = ()
                    if comb is not None:
                        first = CHUNKS[comb][0]
                        assert first % 2 == 0
                        pair = [(s * 2 + (first - 2 * s0 + b), b, s + (first // 2 - s0)) for b in range(2)]
                    body(s, s + NSLOT - 1, True, key, s - s0, tile, pair)
                if n < len(CHUNKS) - 1:
                    route(n)
            body(None, NBLK - 1, False, None, 0, 0, ())
            route(len(CHUNKS) - 1)
            for n, (_, _, blocks) in enumerate(TAIL):
                key = ("tail", n)
                body(None, None, False, key, 0, STREAMS[key][3], [(blk, blk % 2, blk // 2) for blk in blocks])
            for blk in range(CHUNKS[-1][0], NBLK):
                for i in range(4 * G):
                    combine(i, blk, blk % 2, blk // 2)


SEED = 1
SEED2 = 2
ROWS0 = 2
PRO_SILU, PRO_CT, PRO_GATES = 3, 4, 19
RT_DTOP, N_RT = 13, 16
N_SM, N_R = 7, 3
EPI_NORM = STEP0 + 8
EPI_COLS = STEP0 + 14
EPI_LOGITS = STEP0 + 15
P_SCALE, P_RES, P_STATS, P_AGGR, P_MOD, P_SHIFT = 0, 8, 16, 24, 40, 48


_INS = ['L0_attn_feature', 'L0_attn_wq_w', 'L0_attn_wq_b', 'L0_attn_w2_w', 'L0_attn_w2_b', 'L0_attn_ln_g',
        'L0_attn_ln_b', 'L0_ffn_router_w', 'L0_ffn_router_b', 'L0_ffn_W1', 'L0_ffn_b1', 'L0_ffn_W2',
        'L0_ffn_b2', 'L0_c', 'L0_wmod']
_OUTS = [((32, 256, 128), 'float32')]


def kernel(**inputs):
    import numpy as _np
    import concourse.bacc as _bacc
    from concourse import mybir as _mybir
    from concourse.bass_utils import run_bass_kernel_spmd as _run

    nc = _bacc.Bacc("TRN2", target_bir_lowering=False, num_devices=1)
    arrays, args = {}, []
    for name in _INS:
        a = _np.ascontiguousarray(inputs[name])
        arrays[f"in_{name}_dram"] = a
        args.append(nc.dram_tensor(f"in_{name}_dram", a.shape, _mybir.dt.from_np(a.dtype), kind="ExternalInput").ap())
    for i, (shape, dtype) in enumerate(_OUTS):
        dt = _mybir.dt.from_np(_np.dtype(dtype))
        args.append(nc.dram_tensor(f"out_{i}_dram", shape, dt, kind="ExternalOutput").ap())
    adaln_block_kernel(nc, *args)
    r = _run(nc, [arrays], core_ids=[0])
    got = tuple(r.results[0][f"out_{i}_dram"] for i in range(len(_OUTS)))
    return got[0]
```

```python
from contextlib import ExitStack

import concourse.bass as bass
from concourse import mybir

F32 = mybir.dt.float32
I32 = mybir.dt.int32
U32 = mybir.dt.uint32
ALU = mybir.AluOpType
ACT = mybir.ActivationFunctionType
AX = mybir.AxisListType

B, T, D = 32, 256, 128
W = 64
TB = 16
NBLK = T // TB
NSLOT = W // TB
G, GB = 4, B // 4
E, F = 8, 512
FC = F // 128
TOK = B * TB
NTOK = B * T
NROWT = NBLK * G
NSCAN = NBLK - NSLOT
LN_EPS = 1e-5
NFIRST = B // 4
MASKED = -1e37
TAKEN = -3e38
Q32 = 32
BY_QUADRANT = [g * GB + b8 for b8 in range(GB) for g in range(G)]
BY_QUADRANT_KEYS = [(g * GB + b8, k) for b8 in range(GB) for k in range(2) for g in range(G)]

CHUNKS = ((0, 6, 56), (6, 4, 42), (10, 3, 32), (13, 3, 32))
TILE0 = [sum(c[2] for c in CHUNKS[:n]) for n in range(len(CHUNKS))]
NTILES = sum(c[2] for c in CHUNKS)
MAXB = max(c[1] for c in CHUNKS)
MAXR = G * MAXB
MAXT = max(c[2] for c in CHUNKS)
RING = 8
LEAD = 5
for _blk0, _nb, _nt in CHUNKS:
    assert _nt >= 2 * G * _nb + E - 1

SEGMENTS = ((0, 3, None, 0, None), (3, 7, 0, 14, None), (7, 10, 1, 14, 0), (10, 12, 2, 16, 1))
TAIL = ((3, 32, (10, 11, 12)),)
TICKS = 21
STEP0 = 2
NEXT_Q = STEP0 + 8

STREAMS = {}


def _streams():
    tile, uses = 0, [0] * RING
    plan = [(("seg", n), c, k, s1 - s0) for n, (s0, s1, c, k, _) in enumerate(SEGMENTS) if k]
    plan += [(("tail", n), c, k, 1) for n, (c, k, _) in enumerate(TAIL)]
    for key, c, k, times in plan:
        STREAMS[key] = (c, k, times, tile, tuple(uses))
        tile += k * times
        for q in range(RING):
            uses[q] += times * ring_uses(k, q)
        CHUNK_USES[c] = tuple(uses)
    assert tile == NTILES
    word = 0
    for key, c, k, times in plan:
        WORD0[key] = word
        PACK.setdefault(c, (word, packed(k), k * times // packed(k)))
        word += k * times // packed(k)
    return word


def ring_uses(k, q):
    return (k - q + RING - 1) // RING


OUT, HIDDEN, RELU, OUTPUT, DONE = 1, 2, 3, 4, 5


def packed(k):
    return min(k // 2, 8)


CHUNK_USES = {}
WORD0, PACK = {}, {}
NWORDS = _streams()


def adaln_block_kernel(nc, feature, wq_w, wq_b, w2_w, w2_b, ln_g, ln_b, router_w, router_b,
                       W1, b1, W2, b2, c, wmod, out):
    h2_dram = nc.dram_tensor("h2_dram", [NTOK, D], F32, kind="Internal").ap()
    y_dram = nc.dram_tensor("y_dram", [1 + 2 * NTOK + 128 * NTILES + RING, D], F32, kind="Internal").ap()
    with ExitStack() as ctx:
        def sb(name, shape, dtype=F32):
            return ctx.enter_context(nc.sbuf_tensor(name, shape, dtype))

        def sem(name):
            return ctx.enter_context(nc.semaphore(name))

        ps_h = ctx.enter_context(nc.psum_tensor("ps_h", [128, 2, 512], F32))
        ps_y = ctx.enter_context(nc.psum_tensor("ps_y", [128, 512], F32))
        ps_x = ctx.enter_context(nc.psum_tensor("ps_x", [128, 512], F32))
        ps_wide = ctx.enter_context(nc.psum_tensor("ps_wide", [128, 1024], F32))
        ps_scan = ctx.enter_context(nc.psum_tensor("ps_scan", [128, 512], F32))
        ps_epi = ctx.enter_context(nc.psum_tensor("ps_epi", [128, 512], F32))

        x_sb = sb("x_sb", [128, NBLK, G, D])
        h_T = sb("h_T", [128, NBLK, TOK])
        w1_sb = sb("w1_sb", [128, E, F + FC])
        w2_sb = sb("w2_sb", [128, E, FC, D])
        ring_rows = sb("ring_rows", [128, 2, GB, D])
        ring_T = sb("ring_T", [128, B, W])
        q_blk = sb("q_blk", [128, B, Q32])
        score = sb("score", [128, GB, W])
        coef = score[:, :, :].rearrange("p b k -> p (b k)").rearrange("p (l c) -> p l c", c=Q32)
        prob = score
        o_rows = sb("o_rows", [128, GB, D])
        s_T = sb("s_T", [128, GB, 2, Q32])
        r_pad = sb("r_pad", [128, TB + 1, Q32])
        cross = sb("cross", [128, TB + 1, Q32])
        prod = sb("prod", [128, TB + 1, TB])
        wgt = sb("wgt", [128, TB, TB])
        coef_bd = sb("coef_bd", [128, GB, G, Q32])
        own_g = sb("own_g", [128, G])
        v_rows = sb("v_rows", [128, GB, D])
        prob_T = sb("prob_T", [128, GB, 2, Q32])
        mask = sb("mask", [128, NSLOT, W])
        below = sb("below", [128, TB])
        diag = sb("diag", [128, TB])
        unit = sb("unit", [128, 2 * TB - 1])
        ident = sb("ident", [128, 128])
        small = sb("small", [128, 16 * TB])
        m_score, m_old, z_part, z_zero, m_rel = (small[:, 8 * k:8 * k + 8] for k in range(5))
        neg_max = small[:, 64:64 + TB]
        z_inv = small[:, 144:145]
        tmp_r = sb("tmp_r", [128, TB, GB])
        tmp_d = sb("tmp_d", [128, TB, GB])
        col = sb("col", [128, TB + 1])

        gate_T = sb("gate_T", [128, 512])
        y_T = sb("y_T", [128, 512])
        z_sb = sb("z_sb", [128, G, D])
        h2_row = sb("h2_row", [128, G, D])
        h2_T = y_T
        stats = sb("stats", [128, G, 6])
        idle = sb("idle", [128, 1])
        mv = sb("mv", [128, G, 2])
        eps_t = sb("eps_t", [128, NROWT])
        mhalf = sb("mhalf", [128, NROWT])
        rstd = sb("rstd", [128, G])
        nmean = sb("nmean", [128, G])
        nmr = sb("nmr", [128, G])
        minus1 = sb("minus1", [128, G])
        mv_all = sb("mv_all", [128, NROWT, 2])
        rstd_all = sb("rstd_all", [128, NROWT])
        rt = sb("rt", [128, 6, G * E])
        logit, eq1, key1, logit2, eq2, key2 = (
            rt[:, k, :].rearrange("p (g e) -> p g e", e=E) for k in range(6))
        rv = sb("rv", [128, 7, G])
        top1, arg1, top2, arg2, dtop, etop, dsum = (rv[:, k, :] for k in range(7))
        rank_w = sb("rank_w", [128, E])
        hot1 = sb("hot1", [128, NROWT, E])
        hot2 = sb("hot2", [128, NROWT, E])
        g1_all = sb("g1_all", [128, NROWT])
        g2_all = sb("g2_all", [128, NROWT])

        lower = sb("lower", [128, 128])
        ones = sb("ones", [128, 128])
        iota_q = sb("iota_q", [128, 128])
        token1 = sb("token1", [128, 2, NROWT])
        spare = sb("spare", [128, MAXT])
        tile_lim = sb("tile_lim", [128, MAXR])
        keep = sb("keep", [128, E * MAXR])
        pick = sb("pick", [128, MAXR, E])
        tot_flat = prod[:, :, :].rearrange("p a b -> p (a b)")
        inc_flat = wgt[:, :, :].rearrange("p a b -> p (a b)")
        tiles_e = sb("tiles_e", [128, E])
        tiles_to = sb("tiles_to", [128, E])
        base_e = sb("base_e", [128, E])
        slot_f = sb("slot_f", [128, 2, MAXR])
        slot_i = sb("slot_i", [128, 2, MAXR], I32)
        part_i = sb("part_i", [128, 2, 2, MAXR], I32)
        lo_f = sb("lo_f", [128, 2, NROWT])
        hi_f = sb("hi_f", [128, 2, NROWT])
        o_flat = o_rows[:, :, :].rearrange("p b t -> p (b t)")
        v_flat = v_rows[:, :, :].rearrange("p b t -> p (b t)")
        oh_lo = [o_flat[:, 512 * h:512 * (h + 1)].rearrange("p (c r q) -> p c r q", c=2, r=2) for h in range(2)]
        oh_hi = [v_flat[:, 512 * h:512 * h + 4 * MAXT].rearrange("p (c r q) -> p c r q", c=2, r=2) for h in range(2)]
        z_flat = z_sb[:, :, :].rearrange("p g d -> p (g d)")
        tab = z_flat[:, 0:5 * MAXT].rearrange("p (n j) -> p n j", n=5)
        exp_f = sb("exp_f", [128, MAXT])
        pow8 = sb("pow8", [128, 8])
        word_f = sb("word_f", [128, 8])
        experts = sb("experts", [128, NWORDS], U32)
        take_row = sb("take_row", [128, NTILES], U32)
        give_row = sb("give_row", [128, NTILES], U32)

        xg = sb("xg", [128, RING, D])
        x_T = sb("x_T", [128, 2, 128])
        w1_cur = sb("w1_cur", [128, 3, F + FC])
        hid = sb("hid", [128, 2, FC, 128])
        y_out = sb("y_out", [128, RING, D])
        yc = sb("yc", [128, 2, 2, G, D])

        wq_sb = sb("wq_sb", [128, D])
        rw_sb = sb("rw_sb", [128, E])
        rb_sb = sb("rb_sb", [128, E])
        b2_sb = sb("b2_sb", [1, E, D])
        wqb_col = sb("wqb_col", [128, 1])
        wqb_w2 = sb("wqb_w2", [128, 1])
        w2_col = sb("w2_col", [128, 1])
        w2b_col = sb("w2b_col", [128, 1])
        mod_T = sb("mod_T", [128, 2, B])
        g_scale = sb("g_scale", [128, G, D])
        g_ffn = sb("g_ffn", [128, G, D])
        cb_row = sb("cb_row", [128, G, D])
        sb_row = sb("sb_row", [128, G, D])

        rows_in = [o_rows[:, :, :], v_rows[:, :, :], xg[:, :, :],
                   w1_cur[:, :, :].rearrange("p a f -> p (a f)")[:, 0:8 * D].rearrange("p (n d) -> p n d", d=D)]

        early = yc[:, :, :, :, :].rearrange("p a c g d -> p (a c g d)")
        wmod_sb = early[:, 0:6 * D]
        c_sb = early[0:B, 768:896]
        c_exp = early[0:B, 896:1024]
        c_den = early[0:B, 1024:1152]
        c_silu = early[0:B, 1152:1280]
        c_T = early[:, 1280:1280 + B]
        b1_rows = early[0:E * FC, 1312:1440]
        lng_bc = early[:, 1440:1568]
        lnb_bc = early[:, 1568:1696]
        iota_i = y_out[:, 0, :].bitcast(I32)
        early2 = hid[:, :, :, :].rearrange("p a c q -> p (a c q)")
        c_rep = early2[:, 0:512].rearrange("p (g q) -> p g q", g=G)
        ga_sb = early2[:, 512:1024].rearrange("p (g q) -> p g q", g=G)
        ga_abs = y_T[:, :].rearrange("p (g q) -> p g q", g=G)
        ga_sgn = z_sb[:, :, :]
        g_shift = h2_row[:, :, :]

        s_x = sem("s_x")
        s_x2 = [sem(f"s_x2_{q}") for q in range(4)]
        s_ident = sem("s_ident")
        s_cond = sem("s_cond")
        s_attn_w = sem("s_attn_w")
        s_w1 = sem("s_w1")
        s_w2 = sem("s_w2")
        s_router = sem("s_router")
        s_const = sem("s_const")
        s_pool = sem("s_pool")
        s_cexp = sem("s_cexp")
        s_pro = sem("s_pro")
        s_ct = sem("s_ct")
        s_ctrep = sem("s_ctrep")
        s_mod = sem("s_mod")
        s_moded = sem("s_moded")
        s_gprod = sem("s_gprod")
        s_st1 = sem("s_st1")
        s_mv1 = sem("s_mv1")
        s_rstd1 = sem("s_rstd1")
        s_xn1 = sem("s_xn1")
        s_xt1 = sem("s_xt1")
        s_h = sem("s_h")
        s_shift = sem("s_shift")
        s_rows_ps = sem("s_rows_ps")


        s_tanh = sem("s_tanh")
        s_yT = sem("s_yT")
        s_ytok = sem("s_ytok")
        s_st = sem("s_st")
        s_st2 = sem("s_st2")
        s_mvv = sem("s_mvv")
        s_var = sem("s_var")
        s_rs = sem("s_rs")
        s_z = sem("s_z")
        s_xn = sem("s_xn")
        s_zg = sem("s_zg")
        s_x1 = sem("s_x1")
        s_lg = sem("s_lg")
        s_rt = sem("s_rt")
        s_etop = sem("s_etop")

        s_q_ps = sem("s_q_ps")
        s_q = sem("s_q")
        s_s_ps = sem("s_s_ps")
        s_sm = sem("s_sm")
        s_cen = sem("s_cen")
        s_ez = sem("s_ez")
        s_p = sem("s_p")
        s_pT = sem("s_pT")
        s_o_ps = sem("s_o_ps")
        s_o = sem("s_o")
        s_r_ps = sem("s_r_ps")
        s_r = sem("s_r")
        s_cross = sem("s_cross")
        s_max = sem("s_max")
        s_e = sem("s_e")
        s_prod = sem("s_prod")
        s_sum = sem("s_sum")
        s_zsum = sem("s_zsum")
        s_col = sem("s_col")
        s_row = sem("s_row")
        s_coef_T = sem("s_coef_T")
        s_coef = sem("s_coef")
        s_v_ps = sem("s_v_ps")
        s_v = sem("s_v")
        s_vT_ps = sem("s_vT_ps")
        s_vT = sem("s_vT")
        s_ring = sem("s_ring")
        s_rows = sem("s_rows")

        s_h2a = sem("s_h2a")
        s_h2r = sem("s_h2r")
        s_h2st = sem("s_h2st")
        s_h2ps = sem("s_h2ps")
        s_h2 = sem("s_h2")

        s_route = sem("s_route")
        s_pick = sem("s_pick")
        s_rank = sem("s_rank")
        s_hi = sem("s_hi")
        s_oh = sem("s_oh")
        s_tab = sem("s_tab")
        s_tabs = sem("s_tabs")

        s_xg = [sem(f"s_xg{q}") for q in range(RING)]
        s_xTp = sem("s_xTp")
        s_xT = sem("s_xT")
        s_w1c = sem("s_w1c")
        s_h1 = sem("s_h1")
        s_hid = sem("s_hid")
        s_y = sem("s_y")
        s_yo = sem("s_yo")
        s_give = [sem(f"s_give{q}") for q in range(RING)]
        s_yc = [sem(f"s_yc{b}") for b in range(2)]
        s_cmb = sem("s_cmb")
        s_res = sem("s_res")
        s_out = [sem(f"s_out{b}") for b in range(2)]

        block = ctx.enter_context(nc.Block())

        def wait_apart(eng, semaphore, value):
            value = value if isinstance(value, int) else eng.snap(value)
            eng.wait_ge(s_const, 1)
            eng.wait_ge(semaphore, value)

        def load_rows(eng, n):
            eng.dma_start(rows_in[n % 4], feature[4 * n:4 * (n + 1)].rearrange("b (h p) d -> p (b h) d", p=128)
                          ).then_inc(s_x2[n % 4], 16)

        def norm_banks(n):
            return (ps_x, ps_y) if n % 2 == 0 else (ps_scan, ps_epi)

        @block.sync
        def _(sp):
            sp.dma_start(c_sb, c).then_inc(s_cond, 16)
            sp.dma_start(wmod_sb, wmod).then_inc(s_cond, 16)
            sp.dma_start(b1_rows, b1.rearrange("e (c p) -> (e c) p", p=128)).then_inc(s_cond, 16)
            load_rows(sp, 0)
            load_rows(sp, 2)
            sp.dma_start(wq_sb[:, :], wq_w).then_inc(s_attn_w, 16)
            sp.dma_start(wqb_col[:, :], wq_b.rearrange("(d a) -> d a", a=1)).then_inc(s_attn_w, 16)
            sp.dma_start(w2_col[:, :], w2_w.rearrange("(d a) -> d a", a=1)).then_inc(s_attn_w, 16)
            sp.dma_start(w2b_col[:, :], w2_b.rearrange("(d a) -> d a", a=1).to_broadcast([128, 1])
                         ).then_inc(s_attn_w, 16)
            sp.dma_start(lng_bc, ln_g.rearrange("(a d) -> a d", a=1).to_broadcast([128, D])).then_inc(s_attn_w, 16)
            sp.dma_start(lnb_bc, ln_b.rearrange("(a d) -> a d", a=1).to_broadcast([128, D])).then_inc(s_attn_w, 16)
            sp.dma_start(rw_sb[:, :], router_w).then_inc(s_router, 16)
            sp.dma_start(rb_sb[:, :], router_b.rearrange("(a e) -> a e", a=1).to_broadcast([128, E])
                         ).then_inc(s_router, 16)
            sp.dma_start(b2_sb[:, :, :], b2.rearrange("(a e) d -> a e d", a=1)).then_inc(s_router, 16)
            for b in range(B):
                g, b8 = b // GB, b % GB
                sp.dma_start(x_sb[TB * b8:TB * (b8 + 1), :, g, :],
                             feature[b].rearrange("(k t) d -> t k d", t=TB)).then_inc(s_x, 16)
            for n in range(4, NFIRST):
                sp.wait_ge(s_xt1, n - 3)
                load_rows(sp, n)
            sp.dma_start(w1_sb[:, :, 0:F], W1.rearrange("e d f -> d e f")).then_inc(s_w1, 16)
            for e in range(E):
                sp.dma_start(w2_sb[:, e, :, :], W2[e].rearrange("(c p) d -> p c d", p=128)).then_inc(s_w2, 16)

            def store_values(s):
                slot = s % NSLOT
                sp.wait_ge(s_v, 2 * s + 2)
                for g in range(G):
                    row = Q32 * g + TB * (slot % 2)
                    sp.dma_start(ring_rows[row:row + TB, slot // 2, :, :],
                                 v_rows[Q32 * g:Q32 * g + TB, :, :]).then_inc(s_ring, 16)

            def store_h2(blk):
                sp.wait_ge(s_h2r, blk + 1)
                sp.dma_start(h2_dram[TOK * blk:TOK * (blk + 1), :].rearrange("(g p) d -> p g d", p=128),
                             h2_row[:, :, :]).then_inc(s_h2st, 16)

            def load_results(blk):
                b = blk % 2
                for n, (blk0, _, _) in enumerate(CHUNKS):
                    if blk == blk0:
                        for q in range(RING):
                            sp.wait_ge(s_give[q], 16 * CHUNK_USES[n][q] + 16)
                if blk >= 2:
                    sp.wait_ge(s_out[b], 16 * G * (blk // 2))
                else:
                    sp.wait_ge(s_shift, 1)
                for k in range(2):
                    rows = 1 + k * NTOK + TOK * blk
                    sp.dma_start(yc[:, b, k, :, :],
                                 y_dram[rows:rows + TOK, :].rearrange("(g p) d -> p g d", p=128)
                                 ).then_inc(s_yc[b], 16)

            def store_result(blk):
                sp.wait_ge(s_res, blk + 1)
                for g in range(G):
                    sp.dma_start(out[GB * g:GB * (g + 1), TB * blk:TB * (blk + 1), :],
                                 yc[:, blk % 2, 0, g, :]).then_inc(s_out[blk % 2], 16)

            def rows_stored(blocks):
                sp.wait_ge(s_ring, 16 * G * blocks + ROWS0)
                sp.sem_inc(s_rows, 1)

            rows_stored(0)
            for blk in range(NSLOT - 1):
                store_h2(blk)
            for s0, s1, _, _, comb in SEGMENTS:
                for s in range(s0, s1):
                    first = None if comb is None else CHUNKS[comb][0] + 2 * (s - s0)
                    if first is not None:
                        load_results(first)
                        load_results(first + 1)
                        store_result(first)
                    store_h2(s + NSLOT - 1)
                    if first is not None:
                        store_result(first + 1)
                    store_values(s)
                    rows_stored(s + 1)
            store_h2(NBLK - 1)
            rest = range(TAIL[0][2][0], NBLK)
            for blk in rest[:2]:
                load_results(blk)
            for blk in rest:
                store_result(blk)
                if blk + 2 in rest:
                    load_results(blk + 2)
            sp.wait_ge(s_ring, 16 * G * NSCAN + ROWS0)
            sp.wait_ge(s_h2st, 16 * NBLK + SEED)
            for b in range(2):
                sp.wait_ge(s_out[b], 16 * G * (NBLK // 2))
            for q in range(RING):
                sp.wait_ge(s_give[q], 16 * CHUNK_USES[len(CHUNKS) - 1][q] + 16)

        @block.gpsimd
        def _(pool):
            n = [0]

            def order(ins):
                ins.then_inc(s_pool, 1)
                n[0] += 1
                pool.wait_ge(s_pool, n[0])

            order(pool.memset(ident[:, :], 0.0))
            order(pool.affine_select(out=ident[:, :], in_=ident[:, :], compare_op=ALU.not_equal, fill=1.0,
                                     base=0, pattern=[[-1, 128]], channel_multiplier=1))
            pool.sem_inc(s_ident, 1)
            order(pool.memset(mask[:, :, :], 0.0))
            order(pool.memset(below[:, :], 1.0))
            order(pool.memset(diag[:, :], 0.0))
            order(pool.memset(unit[:, :], 0.0))
            order(pool.memset(q_blk[:, :, :], 0.0))
            order(pool.memset(r_pad[:, 0:TB, :], 0.0))
            order(pool.memset(r_pad[:, TB, :], 1.0))
            order(pool.memset(coef_bd[:, :, :, :], 0.0))
            order(pool.memset(own_g[:, :], 0.0))
            for g in range(G):
                order(pool.memset(own_g[Q32 * g:Q32 * g + TB, g:g + 1], 1.0))
            order(pool.memset(eps_t[:, :], LN_EPS))
            order(pool.memset(mhalf[:, :], -0.5))
            order(pool.memset(minus1[:, :], -1.0))
            for e in range(E):
                order(pool.memset(rank_w[:, e:e + 1], float(E - e)))
            for i in range(8):
                order(pool.memset(pow8[:, i:i + 1], float(8 ** i)))
            pool.wait_ge(s_pool, n[0])
            order(pool.memset(unit[:, TB - 1:TB], 1.0))
            for g in range(G):
                rows = slice(Q32 * g, Q32 * (g + 1))
                order(pool.affine_select(out=below[rows, :], in_=below[rows, :], compare_op=ALU.is_gt, fill=0.0,
                                         base=0, pattern=[[-1, TB]], channel_multiplier=1))
                order(pool.affine_select(out=diag[rows, :], in_=diag[rows, :], compare_op=ALU.not_equal, fill=1.0,
                                         base=0, pattern=[[-1, TB]], channel_multiplier=1))
                for q in range(NSLOT):
                    m = mask[rows, q, TB * q:TB * (q + 1)]
                    order(pool.affine_select(out=m, in_=m, compare_op=ALU.is_ge, fill=MASKED,
                                             base=0, pattern=[[1, TB]], channel_multiplier=-1))
            order(pool.memset(lower[:, :], 1.0))
            order(pool.affine_select(out=lower[:, :], in_=lower[:, :], compare_op=ALU.is_gt, fill=0.0,
                                     base=0, pattern=[[1, 128]], channel_multiplier=-1))
            order(pool.memset(ones[:, :], 1.0))
            order(pool.memset(y_out[:, :, :], 0.0))
            for dst, count, step, base, per_row in (
                    (iota_q[:, :], 128, 1, 0, 0),
                    (token1[:, 0, :], NROWT, 128, 1, 1),
                    (token1[:, 1, :], NROWT, 128, 1 + NTOK, 1),
                    (spare[:, :], MAXT, 128, 1 + 2 * NTOK, 1),
                    (tile_lim[:, :], MAXR, 128, 0, 0)):
                order(pool.iota(iota_i[:, 0:count], [[step, count]], base=base, channel_multiplier=per_row))
                order(pool.tensor_copy(dst, iota_i[:, 0:count]))
            pool.wait_ge(s_pool, n[0])
            pool.memset(small[:, :], 0.0).then_inc(s_const, 1)

            for k in range(NFIRST):
                tiles = slice(8 * k, 8 * (k + 1))
                pool.wait_ge(s_mv1, k + 1)
                pool.tensor_tensor(rstd_all[:, tiles], mv_all[:, tiles, 1], eps_t[:, tiles], ALU.add
                                   ).then_inc(s_rstd1, 1)
                pool.wait_ge(s_rstd1, 2 * k + 1)
                pool.tensor_tensor(rstd_all[:, tiles], rstd_all[:, tiles], mhalf[:, tiles], ALU.pow
                                   ).then_inc(s_rstd1, 1)
                if k == 2:
                    pool.wait_ge(s_x, 16 * B)
                    pool.wait_ge(s_pro, PRO_GATES)
                for blk in range(3 * (k - 2), min(3 * (k - 1), NBLK)) if k >= 2 else ():
                    m = pool.tensor_tensor(x_sb[:, blk, :, :], x_sb[:, blk, :, :], g_shift, ALU.add)
            m.then_inc(s_shift, 1)

            for q in range(RING):
                row = 1 + 2 * NTOK + 128 * NTILES + q
                pool.dma_start(y_dram[row:row + 1, :], y_out[0:1, q, :]).then_inc(s_give[q], 16)

            def rstd_of(n_th):
                pool.wait_ge(s_mvv, n_th * G)
                pool.tensor_tensor(rstd[:, :], mv[:, :, 1], eps_t[:, 0:G], ALU.add).then_inc(s_var, 1)
                pool.tensor_tensor(nmean[:, :], mv[:, :, 0], minus1[:, :], ALU.mult).then_inc(s_var, 1)
                pool.wait_ge(s_var, 3 * n_th - 1)
                pool.tensor_tensor(rstd[:, :], rstd[:, :], mhalf[:, 0:G], ALU.pow).then_inc(s_var, 1)
                pool.wait_ge(s_var, 3 * n_th)
                pool.tensor_tensor(nmr[:, :], nmean[:, :], rstd[:, :], ALU.mult).then_inc(s_rs, 1)

            taken_by = [None] * RING

            def gather(key, n):
                chunk, k, _, tile0, _ = STREAMS[key]
                blk0, nb, _ = CHUNKS[chunk]
                q = n % k % RING
                if taken_by[q] is not None:
                    pool.wait_ge(s_xTp, taken_by[q] + 1)
                taken_by[q] = tile0 + n
                pool.indirect_dma_start(xg[:, q, :], None, h2_dram[0:TOK * (blk0 + nb), :],
                                        bass.IndirectOffsetOnAxis(take_row[:, tile0 + n:tile0 + n + 1], 0)
                                        ).then_inc(s_xg[q], 16)

            def scatter(key, n):
                _, k, _, tile0, _ = STREAMS[key]
                q = n % k % RING
                pool.wait_ge(s_yo, tile0 + n + 1 + SEED2)
                pool.indirect_dma_start(y_dram, bass.IndirectOffsetOnAxis(give_row[:, tile0 + n:tile0 + n + 1], 0),
                                        y_out[:, q, :], None).then_inc(s_give[q], 16)

            def begin(key):
                pool.wait_ge(s_tabs, STREAMS[key][0] + 1)
                blk0, nb, _ = CHUNKS[STREAMS[key][0]]
                pool.wait_ge(s_h2st, 16 * (blk0 + nb) + SEED)
                for n in range(LEAD):
                    gather(key, n)

            def body(blk, key, it):
                k, times = STREAMS[key][1:3] if key else (0, 0)
                for t in range(TICKS if blk is not None else k + DONE + 1):
                    if blk is not None and t == 1:
                        rstd_of(2 * blk + 1)
                    if blk is not None and t == EPI_NORM - 1:
                        rstd_of(2 * blk + 2)
                    if t < k and it * k + t + LEAD < k * times:
                        gather(key, it * k + t + LEAD)
                    if 0 <= t - DONE < k:
                        scatter(key, it * k + t - DONE)

            for blk in range(NSLOT - 1):
                body(blk, None, 0)
            for n, (s0, s1, chunk, _, _) in enumerate(SEGMENTS):
                key = ("seg", n) if chunk is not None else None
                if key:
                    begin(key)
                for s in range(s0, s1):
                    body(s + NSLOT - 1, key, s - s0)
            body(NBLK - 1, None, 0)
            for n in range(len(TAIL)):
                begin(("tail", n))
                body(None, ("tail", n), 0)

        @block.scalar
        def _(act):
            load_rows(act, 1)
            load_rows(act, 3)
            act.wait_ge(s_cond, 48)
            act.activation(c_exp, c_sb, ACT.Exp, scale=-1.0).then_inc(s_cexp, 1)
            act.wait_ge(s_moded, 1)
            for n in range(NFIRST):
                act.wait_ge(s_xt1, n + 1)
                for i in range(8):
                    b, half = 4 * n + i // 2, i % 2
                    m = act.activation(h_T[:, 8 * half:8 * (half + 1), TB * b:TB * (b + 1)],
                                       norm_banks(n)[i // 4][:, 128 * (i % 4):128 * (i % 4 + 1)].rearrange(
                                           "p (k t) -> p k t", t=TB),
                                       ACT.Identity, scale=mod_T[:, 1, b:b + 1], bias=mod_T[:, 0, b:b + 1])
                m.then_inc(s_h, 1)
            act.wait_ge(s_const, 1)
            act.wait_ge(s_attn_w, 16 * 6)
            act.wait_ge(s_pro, PRO_GATES)
            act.wait_ge(s_shift, 1)

            def tanh_values(blk, slot, done):
                wait_apart(act, s_yT, blk + SEED)
                wait_apart(act, s_vT, done)
                act.activation(gate_T[:, :].rearrange("p (b t) -> p b t", t=TB),
                               ring_T[:, :, bass.ds(slot * TB, TB)], ACT.Tanh).then_inc(s_tanh, 1)

            def scale_attn(blk, groups):
                if 0 in groups:
                    act.wait_ge(s_rs, 2 * blk + 1)
                for g in groups:
                    act.activation(z_sb[:, g, :], ps_epi[:, D * g:D * (g + 1)], ACT.Identity,
                                   scale=rstd[:, g:g + 1], bias=nmr[:, g:g + 1]).then_inc(s_z, 1)

            def normalise(blk, g):
                if g == 0:
                    wait_apart(act, s_rs, 2 * blk + 2)
                act.activation(z_sb[:, g, :], x_sb[:, blk, g, :], ACT.Identity,
                               scale=rstd[:, g:g + 1], bias=nmr[:, g:g + 1]).then_inc(s_xn, 1)

            def h2_cols(blk):
                act.wait_ge(s_h2ps, blk + 1)
                act.activation(h2_T[:, :], ps_epi[:, :], ACT.Copy).then_inc(s_h2, 1)

            def top_exp(blk):
                act.wait_ge(s_rt, blk * N_RT + RT_DTOP)
                act.activation(etop, dtop, ACT.Exp).then_inc(s_etop, 1)

            def queries_out(s):
                act.wait_ge(s_q_ps, s + 1)
                act.activation(q_blk[:, :, 0:TB], ps_scan[:, :].rearrange("p (b t) -> p b t", t=TB), ACT.Identity,
                               scale=w2_col[:, 0:1], bias=wqb_w2[:, 0:1]).then_inc(s_q, 1)

            def window_exp(s):
                act.wait_ge(s_cen, s + 1)
                act.activation(prob[:, :, :], score[:, :, :], ACT.Exp).then_inc(s_p, 1)

            def zero_exp(s):
                act.activation(z_zero, m_old, ACT.Exp, scale=-1.0, bias=w2b_col[:, 0:1]).then_inc(s_ez, 1)

            def old_rows(s):
                act.wait_ge(s_o_ps, s + 1 + SEED)
                act.activation(o_rows[:, :, :], ps_wide[:, :].rearrange("p (b d) -> p b d", d=D),
                               ACT.Copy).then_inc(s_o, 1)

            def values_out(s, half):
                act.wait_ge(s_v_ps, 2 * s + 1 + half)
                if half == 0:
                    act.wait_ge(s_ring, 16 * G * s + ROWS0)
                act.activation(v_rows[:, 4 * half:4 * half + 4, :],
                               ps_wide[:, 512 * half:512 * (half + 1)].rearrange("p (b d) -> p b d", d=D),
                               ACT.Copy).then_inc(s_v, 1)

            def step_exp(s, j):
                act.wait_ge(s_max, s * TB + j + 1)
                act.activation(wgt[:, j, 0:j + 1], cross[:, 0:j + 1, j], ACT.Exp,
                               bias=neg_max[:, j:j + 1]).then_inc(s_e, 1)

            def tile_cols(n, i):
                act.wait_ge(s_xTp, n + i + 1)
                act.wait_ge(s_h1, n + i + 1)
                act.activation(x_T[:, i % 2, :], ps_x[:, 0:128], ACT.Copy).then_inc(s_xT, 1)

            def relu(n, i, f):
                if f == 0:
                    act.wait_ge(s_h1, n + i + 1 + SEED2)
                    act.wait_ge(s_y, n + i + 1)
                m = act.activation(hid[:, i % 2, f, :], ps_h[:, i % 2, 128 * f:128 * (f + 1)], ACT.Relu,
                                   bias=w1_cur[:, i % 3, F + f:F + f + 1])
                if f == FC - 1:
                    m.then_inc(s_hid, 1)

            def tile_out(n, i, used):
                act.wait_ge(s_y, n + i + 1 + SEED2)
                act.wait_ge(s_give[i % RING], 16 * used + 16)
                act.activation(y_out[:, i % RING, :], ps_y[:, 0:128], ACT.Copy).then_inc(s_yo, 1)

            def body(s, blk, done, scan, key, it, n):
                k = STREAMS[key][1] if key else 0
                for t in range(TICKS if blk is not None else k + DONE + 1):
                    if scan:
                        if STEP0 <= t < STEP0 + TB:
                            step_exp(s, t - STEP0)
                    i = t - DONE
                    if 0 <= i < k:
                        tile_out(n, i, STREAMS[key][4][i % RING] + it * ring_uses(k, i % RING) + i // RING)
                    if scan:
                        if t == STEP0 + 2:
                            old_rows(s)
                        if t == NEXT_Q:
                            queries_out(s + 1)
                    if blk is not None:
                        if t == STEP0 + TB:
                            top_exp(blk)
                            if done is not None:
                                tanh_values(blk + 1, (blk + 1) % NSLOT, done)
                        if t in (STEP0, STEP0 + 1):
                            scale_attn(blk, range(2 * (t - STEP0), 2 * (t - STEP0) + 2))
                        if EPI_NORM <= t < EPI_NORM + G:
                            normalise(blk, t - EPI_NORM)
                        if t == EPI_LOGITS:
                            h2_cols(blk)
                    if scan and t == STEP0 + TB:
                        window_exp(s + 1)
                        zero_exp(s + 1)
                        for half in range(2):
                            values_out(s, half)
                    if 0 <= t - OUT < k:
                        tile_cols(n, t - OUT)
                    if 0 <= t - RELU < k:
                        for f in range(FC):
                            relu(n, t - RELU, f)

            queries_out(0)
            tanh_values(0, 0, SEED2)
            window_exp(0)
            zero_exp(0)
            with act.Fori(0, NSLOT - 1) as blk:
                body(None, blk, SEED2, False, None, 0, 0)
            for n, (s0, s1, chunk, k, _) in enumerate(SEGMENTS):
                key = ("seg", n) if chunk is not None else None
                with act.Fori(s0, s1) as s:
                    tile = s * k + (STREAMS[key][3] - s0 * k) if key else 0
                    body(s, s + NSLOT - 1, 2 * s + 2 + SEED2, True, key, s - s0, tile)
            body(None, NBLK - 1, None, False, None, 0, 0)
            for n in range(len(TAIL)):
                key = ("tail", n)
                body(None, None, None, False, key, 0, STREAMS[key][3])

        @block.tensor
        def _(pe):
            pe.wait_ge(s_ident, 1)
            pe.wait_ge(s_pro, PRO_SILU)
            pe.wait_ge(s_cond, 48)
            pe.transpose(ps_epi[:, B:B + E * FC], b1_rows, ident[0:E * FC, 0:E * FC])
            pe.transpose(ps_epi[:, 0:B], c_silu, ident[0:B, 0:B]).then_inc(s_ct, 1)
            pe.wait_ge(s_pro, PRO_CT)
            for n, k in enumerate((0, 1)):
                m = pe.matmul(ps_scan[:, B * n:B * (n + 1)], wmod_sb[:, D * k:D * (k + 1)], c_T,
                              start=True, stop=True)
            m.then_inc(s_mod, 1)
            pe.wait_ge(s_ctrep, 1)
            for dst, k in ((ps_wide[:, 0:512], 2), (ps_wide[:, 512:1024], 5), (ps_h[:, 0, :], 4), (ps_h[:, 1, :], 3)):
                for g in range(G):
                    m = pe.matmul(dst[:, D * g:D * (g + 1)], c_rep[:, g, :],
                                  wmod_sb[:, D * k:D * (k + 1)], start=True, stop=True)
            m.then_inc(s_gprod, 1)

            def transpose_groups(dst, src, sem_done):
                for g in range(G):
                    m = pe.transpose(dst[:, 128 * g:128 * (g + 1)], src[:, 128 * g:128 * (g + 1)], ident[:, :])
                m.then_inc(sem_done, 1)

            pe.wait_ge(s_moded, 1)
            for n in range(NFIRST):
                pe.wait_ge(s_xn1, n + 1)
                if n >= 2:
                    pe.wait_ge(s_h, n - 1)
                for i in range(8):
                    m = pe.transpose(norm_banks(n)[i // 4][:, 128 * (i % 4):128 * (i % 4 + 1)],
                                     rows_in[n % 4][:, i, :], ident[:, :])
                m.then_inc(s_xt1, 1)
            pe.wait_ge(s_const, 1)

            for half in range(2):
                if half:
                    pe.wait_ge(s_ring, 1)
                else:
                    pe.wait_ge(s_vT, SEED2)
                    pe.wait_ge(s_pro, PRO_GATES)
                for b in range(B):
                    g, b8 = b // GB, b % GB
                    m = pe.matmul(ps_wide[Q32 * g:Q32 * (g + 1), 128 * b8:128 * (b8 + 1)],
                                  ring_T[:, b, Q32 * half:Q32 * (half + 1)], ident[:, :], start=True, stop=True)
                m.then_inc(s_rows_ps, 1)

            def y_to_rows(blk):
                pe.wait_ge(s_yT, blk + 1 + SEED)
                transpose_groups(ps_epi, y_T, s_ytok)

            def h2_to_cols(blk):
                pe.wait_ge(s_h2r, blk + 1)
                for g in range(G):
                    m = pe.transpose(ps_epi[:, 128 * g:128 * (g + 1)], h2_row[:, g, :], ident[:, :])
                m.then_inc(s_h2ps, 1)

            def logits(blk):
                pe.wait_ge(s_h2, blk + 1)
                for g in range(G):
                    m = pe.matmul(ps_epi[:, E * g:E * (g + 1)], h2_T[:, 128 * g:128 * (g + 1)], rw_sb[:, :],
                                  start=True, stop=True)
                m.then_inc(s_lg, 1)

            def queries(s):
                pe.wait_ge(s_r, s * N_R + SEED)
                pe.matmul(ps_scan[:, :], wq_sb[:, :], h_T[:, (s + NSLOT) % NBLK, :], start=True,
                          stop=True).then_inc(s_q_ps, 1)

            def scores(s):
                pe.wait_ge(s_q, s + 1)
                wait_apart(pe, s_vT, 2 * s + SEED2)
                for b in BY_QUADRANT:
                    g, b8 = b // GB, b % GB
                    m = pe.matmul(ps_scan[Q32 * g:Q32 * (g + 1), W * b8:W * (b8 + 1)], q_blk[:, b, :],
                                  ring_T[:, b, :], start=True, stop=True)
                m.then_inc(s_s_ps, 1)

            def cross_scores(s):
                wait_apart(pe, s_pT, s + 1)
                for b, k in BY_QUADRANT_KEYS:
                        g, b8 = b // GB, b % GB
                        quad = slice(Q32 * g, Q32 * (g + 1))
                        m = pe.matmul(ps_scan[quad, TB * b8:TB * (b8 + 1)], s_T[quad, b8, k, :],
                                      prob_T[quad, b8, k, 0:TB], start=(k == 0), stop=(k == 1))
                m.then_inc(s_r_ps, 1)

            def weigh_old(s):
                wait_apart(pe, s_rows, s + 1)
                for b, k in BY_QUADRANT_KEYS:
                        g, b8 = b // GB, b % GB
                        quad = slice(Q32 * g, Q32 * (g + 1))
                        m = pe.matmul(ps_wide[quad, D * b8:D * (b8 + 1)], prob_T[quad, b8, k, :],
                                      ring_rows[quad, k, b8, :], start=(k == 0), stop=(k == 1))
                m.then_inc(s_o_ps, 1)

            def values_cols(s):
                for half in range(2):
                    wait_apart(pe, s_coef, 2 * s + 1 + half)
                    if half == 0:
                        pe.wait_ge(s_o, s + 1)
                    for b8 in range(4 * half, 4 * half + 4):
                        at = 512 * half + G * TB * (b8 % 4)
                        m = pe.matmul(ps_wide[:, at:at + G * TB], o_rows[:, b8, :],
                                      coef_bd[:, b8, :, 0:TB], start=True, stop=True)
                    m.then_inc(s_vT_ps, 1)

            def values_rows(s, half):
                for b8 in range(4 * half, 4 * half + 4):
                    m = pe.matmul(ps_wide[:, D * b8:D * (b8 + 1)], coef_bd[:, b8, :, :], o_rows[:, b8, :],
                                  start=True, stop=True)
                m.then_inc(s_v_ps, 1)

            def route(n):
                blk0, nb, nt = CHUNKS[n]
                t0, nr = G * blk0, G * nb
                pe.wait_ge(s_pick, n + 1)
                pe.matmul(ps_epi[:, 0:E * nr], lower[:, :], pick[:, 0:nr, :], start=True, stop=True)
                pe.matmul(ps_epi[:, 256:256 + E * nr], ones[:, :], pick[:, 0:nr, :], start=True,
                          stop=True).then_inc(s_rank, 1)

                for m in range(2 * t0, 2 * (t0 + nr)):
                    q, c, r = m // 4, m // 2 % 2, m % 2
                    pe.wait_ge(s_oh, q + 1)
                    pe.matmul(ps_epi[:, 0:nt], oh_lo[q % 2][:, c, r, :], oh_hi[q % 2][:, c, r, 0:nt],
                              start=(m == 2 * t0), stop=(m == 2 * (t0 + nr) - 1)).then_inc(s_tab, 1)
                pe.wait_ge(s_tabs, n + 1)

            def tile_transpose(n, i, used):
                pe.wait_ge(s_xg[i % RING], 16 * used + 16)
                pe.wait_ge(s_xT, n + i + 1)
                pe.transpose(ps_x[:, 0:128], xg[:, i % RING, :], ident[:, :]).then_inc(s_xTp, 1)

            def tile_hidden(n, i):
                pe.wait_ge(s_xT, n + i + 1 + SEED)
                pe.wait_ge(s_w1c, n + i + 1)
                pe.wait_ge(s_hid, n + i + 1)
                for f in range(FC):
                    m = pe.matmul(ps_h[:, i % 2, 128 * f:128 * (f + 1)], w1_cur[:, i % 3, 128 * f:128 * (f + 1)],
                                  x_T[:, i % 2, :], start=True, stop=True)
                m.then_inc(s_h1, 1)

            def tile_output(n, i, e):
                pe.wait_ge(s_hid, n + i + 1 + SEED2)
                pe.wait_ge(s_yo, n + i + SEED2)
                for f in range(FC):
                    pe.matmul(ps_y[:, 0:128], hid[:, i % 2, f, :], w2_sb[:, e, f, :], start=(f == 0), stop=False)
                pe.matmul(ps_y[:, 0:128], ones[0:1, :], b2_sb[0:1, e, :], start=False, stop=True).then_inc(s_y, 1)

            pe.wait_ge(s_attn_w, 16 * 6)
            pe.wait_ge(s_router, 16 * 3)
            pe.wait_ge(s_w1, 16)
            pe.wait_ge(s_w2, 16 * E)

            def body(s, blk, scan, key, it, n):
                k = STREAMS[key][1] if key else 0
                m = packed(k)
                words = [pe.value_load(experts[0:1, bass.ds(it * (k // m) + WORD0[key] + w, 1)], min_val=0,
                                       max_val=8 ** m - 1) for w in range(k // m)] if k else []
                for t in range(TICKS if blk is not None else k + DONE + 1):
                    if scan:
                        if t == 1:
                            cross_scores(s)
                            weigh_old(s)
                        if t == NEXT_Q:
                            queries(s + 1)
                        if t == STEP0 + TB:
                            values_cols(s)
                            scores(s + 1)
                            for half in range(2):
                                values_rows(s, half)
                    if blk is not None:
                        if t == 0:
                            if scan:
                                pe.wait_ge(s_cen, s + 1)
                            y_to_rows(blk)
                        if t == EPI_COLS:
                            h2_to_cols(blk)
                        if t == EPI_LOGITS:
                            logits(blk)
                    i = t - HIDDEN
                    if 0 <= i < k:
                        tile_hidden(n, i)
                    i = t - OUTPUT
                    if 0 <= i < k:
                        tile_output(n, i, words[i // m] // 8 ** (i % m) % 8)
                    if t < k:
                        tile_transpose(n, t, STREAMS[key][4][t % RING] + it * ring_uses(k, t % RING) + t // RING)

            queries(0)
            scores(0)
            with pe.Fori(0, NSLOT - 1) as blk:
                body(None, blk, False, None, 0, 0)
            for n, (s0, s1, chunk, k, _) in enumerate(SEGMENTS):
                key = ("seg", n) if chunk is not None else None
                with pe.Fori(s0, s1) as s:
                    tile = s * k + (STREAMS[key][3] - s0 * k) if key else 0
                    body(s, s + NSLOT - 1, True, key, s - s0, tile)
                if n < len(CHUNKS) - 1:
                    route(n)
            body(None, NBLK - 1, False, None, 0, 0)
            route(len(CHUNKS) - 1)
            for n in range(len(TAIL)):
                key = ("tail", n)
                body(None, None, False, key, 0, STREAMS[key][3])

        @block.vector
        def _(dve):
            n = [0]

            def order(ins):
                ins.then_inc(s_pro, 1)
                n[0] += 1
                dve.wait_ge(s_pro, n[0])

            for free in (s_r, s_p, s_yT, s_xT, s_h2st, s_o_ps):
                dve.sem_inc(free, SEED)
            for free in (s_h1, s_hid, s_y, s_yo):
                dve.sem_inc(free, SEED2)

            dve.wait_ge(s_cexp, 1)
            order(dve.tensor_scalar(c_den, c_exp, 1.0, None, ALU.add))
            order(dve.reciprocal(c_den, c_den))
            order(dve.tensor_tensor(c_silu, c_sb, c_den, ALU.mult))
            assert n[0] == PRO_SILU
            dve.wait_ge(s_ct, 1)
            dve.tensor_copy(w1_sb[:, :, F:F + FC], ps_epi[:, B:B + E * FC].rearrange("p (e c) -> p e c", c=FC))
            order(dve.tensor_copy(c_T, ps_epi[:, 0:B]))
            assert n[0] == PRO_CT
            for g in range(G):
                m = dve.tensor_copy(c_rep[:, g, :].rearrange("p (b t) -> p b t", t=TB),
                                    c_T[:, GB * g:GB * (g + 1)].unsqueeze(2).to_broadcast([128, GB, TB]))
            m.then_inc(s_ctrep, 1)
            dve.wait_ge(s_mod, 1)
            for k in range(2):
                src = ps_scan[:, B * k:B * (k + 1)]
                if k % 2:
                    m = dve.tensor_scalar(mod_T[:, k, :], src, 1.0, None, ALU.add)
                else:
                    m = dve.tensor_copy(mod_T[:, k, :], src)
            m.then_inc(s_moded, 1)

            st_all = score[:, :, :].rearrange("p a b -> p (a b)")[:, 0:NROWT * 6].rearrange("p (n k) -> p n k", k=6)

            def first_stats(k):
                dve.wait_ge(s_x2[k % 4], 16 * (k // 4 + 1))
                for i in range(8):
                    m = dve.bn_stats(st_all[:, 8 * k + i, :], rows_in[k % 4][:, i, :])
                m.then_inc(s_st1, 1)
                dve.wait_ge(s_st1, k + 1)
                for i in range(8):
                    m = dve.bn_aggr(mv_all[:, 8 * k + i, :], st_all[:, 8 * k + i, :])
                m.then_inc(s_mv1, 1)

            def first_scale(k):
                dve.wait_ge(s_rstd1, 2 * k + 2)
                for i in range(8):
                    n_th = 8 * k + i
                    m = dve.tensor_scalar(rows_in[k % 4][:, i, :], rows_in[k % 4][:, i, :], mv_all[:, n_th, 0:1],
                                          rstd_all[:, n_th:n_th + 1], ALU.subtract, ALU.mult)
                m.then_inc(s_xn1, 1)

            first_stats(0)
            first_stats(1)

            def clip(dst, src):
                order(dve.tensor_copy(ga_sb, src))
                order(dve.scalar_tensor_tensor(ga_abs, ga_sb, -1.0, ga_sb, ALU.mult, ALU.max))
                order(dve.tensor_scalar(ga_abs, ga_abs, 0.25, None, ALU.max))
                order(dve.tensor_scalar(ga_sgn, ga_sb, 0.0, 2.0, ALU.is_ge, ALU.mult))
                order(dve.scalar_tensor_tensor(dst, ga_sgn, -1.0, ga_abs, ALU.add, ALU.mult))

            dve.wait_ge(s_gprod, 1)
            dve.wait_ge(s_attn_w, 16 * 6)
            clip(g_scale[:, :, :], ps_wide[:, 0:512].rearrange("p (g d) -> p g d", g=G))
            order(dve.tensor_tensor(g_shift[:, :, :], g_scale[:, :, :],
                                    lnb_bc.unsqueeze(1).to_broadcast([128, G, D]), ALU.mult))
            order(dve.tensor_tensor(g_scale[:, :, :], g_scale[:, :, :],
                                    lng_bc.unsqueeze(1).to_broadcast([128, G, D]), ALU.mult))
            clip(g_ffn[:, :, :], ps_wide[:, 512:1024].rearrange("p (g d) -> p g d", g=G))
            order(dve.tensor_scalar(cb_row[:, :, :], ps_h[:, 0, :].rearrange("p (g d) -> p g d", g=G), 1.0, None,
                                    ALU.add))
            order(dve.tensor_copy(sb_row[:, :, :], ps_h[:, 1, :].rearrange("p (g d) -> p g d", g=G)))
            order(dve.tensor_tensor(wqb_w2[:, :], wqb_col[:, :], w2_col[:, :], ALU.mult))
            assert n[0] == PRO_GATES

            for k in range(NFIRST):
                first_scale(k)
                if k + 2 < NFIRST:
                    first_stats(k + 2)

            dve.wait_ge(s_h, NFIRST)
            for q in range(NSLOT):
                m = dve.tensor_copy(ring_T[:, :, TB * q:TB * (q + 1)],
                                    h_T[:, q, :].rearrange("p (b t) -> p b t", t=TB))
            m.then_inc(s_vT, 1)
            dve.sem_inc(s_vT, 1)
            for half in range(2):
                dve.wait_ge(s_rows_ps, half + 1)
                dve.tensor_copy(ring_rows[:, half, :, :], ps_wide[:, :].rearrange("p (b d) -> p b d", d=D)
                                ).then_inc(s_ring, 1)

            by_batch = "p (b t) -> p b t"

            def gate_h(blk):
                dve.wait_ge(s_tanh, blk + 1)
                dve.scalar_tensor_tensor(y_T[:, :], gate_T[:, :], 1.0, h_T[:, blk, :], ALU.add,
                                         ALU.mult).then_inc(s_yT, 1)

            def norm_stats(src, n_th):
                for g in range(G):
                    m = dve.bn_stats(stats[:, g, :], src(g))
                m.then_inc(s_st, 1)
                dve.wait_ge(s_st, n_th)
                dve.tensor_copy(idle[:, :], stats[:, G - 1, 0:1])
                for g in range(G):
                    dve.bn_aggr(mv[:, g, :], stats[:, g, :]).then_inc(s_mvv, 1)

            def stats_attn(blk):
                dve.wait_ge(s_ytok, blk + 1)
                norm_stats(lambda g: ps_epi[:, D * g:D * (g + 1)], blk + 1)

            def epilogue(p, blk):
                if p % 2:
                    return
                g = (p - P_SCALE) % 8 // 2
                if P_SCALE <= p < P_SCALE + 8:
                    dve.wait_ge(s_z, G * blk + g + 1)
                    dve.tensor_tensor(z_sb[:, g, :], z_sb[:, g, :], g_scale[:, g, :], ALU.mult).then_inc(s_zg, 1)
                g = p % 8 // 2
                if P_RES <= p < P_RES + 8:
                    dve.wait_ge(s_zg, G * blk + g + 1)
                    dve.tensor_tensor(x_sb[:, blk, g, :], z_sb[:, g, :], x_sb[:, blk, g, :], ALU.add).then_inc(s_x1, 1)
                if P_STATS <= p < P_STATS + 8:
                    wait_apart(dve, s_x1, G * blk + g + 1)
                    dve.bn_stats(stats[:, g, :], x_sb[:, blk, g, :]).then_inc(s_st2, 1)
                if P_AGGR <= p < P_AGGR + 8:
                    if g == 0:
                        dve.wait_ge(s_st2, G * blk + G)
                        dve.tensor_copy(idle[:, :], stats[:, G - 1, 0:1])
                    dve.bn_aggr(mv[:, g, :], stats[:, g, :]).then_inc(s_mvv, 1)
                g = (p - P_MOD) % 8 // 2
                if P_MOD <= p < P_MOD + 8:
                    dve.wait_ge(s_xn, G * blk + g + 1)
                    dve.tensor_tensor(z_sb[:, g, :], z_sb[:, g, :], cb_row[:, g, :], ALU.mult).then_inc(s_h2a, 1)
                if P_SHIFT <= p < P_SHIFT + 8:
                    if g == 0:
                        dve.wait_ge(s_h2st, 16 * blk + SEED)
                    dve.wait_ge(s_h2a, G * blk + g + 1)
                    m = dve.tensor_tensor(h2_row[:, g, :], z_sb[:, g, :], sb_row[:, g, :], ALU.add)
                    if g == G - 1:
                        m.then_inc(s_h2r, 1)

            def over_e(v):
                return v.unsqueeze(2).to_broadcast([128, G, E])

            def over_g(v):
                return v.unsqueeze(1).to_broadcast([128, G, E])

            def route_a(blk):
                k = [0]

                def step(ins):
                    ins.then_inc(s_rt, 1)
                    k[0] += 1
                    dve.wait_ge(s_rt, blk * N_RT + k[0])

                dve.wait_ge(s_lg, blk + 1)
                step(dve.tensor_tensor(logit, ps_epi[:, 0:G * E].rearrange("p (g e) -> p g e", e=E),
                                       over_g(rb_sb[:, :]), ALU.add))
                hots = [hot[:, bass.ds(blk * G, G), :] for hot in (hot1, hot2)]
                for lg, eq, key, hot, top, arg in ((logit, eq1, key1, hots[0], top1, arg1),
                                                   (logit2, eq2, key2, hots[1], top2, arg2)):
                    if lg is logit2:
                        step(dve.scalar_tensor_tensor(logit2, hots[0], TAKEN, logit, ALU.mult, ALU.add))
                    step(dve.tensor_reduce(top, lg, AX.X, ALU.max))
                    step(dve.tensor_tensor(eq, lg, over_e(top), ALU.is_equal))
                    step(dve.tensor_tensor(key, eq, over_g(rank_w[:, :]), ALU.mult))
                    step(dve.tensor_reduce(arg, key, AX.X, ALU.max))
                    step(dve.tensor_tensor(hot, over_g(rank_w[:, :]), over_e(arg), ALU.is_equal))
                ins = dve.tensor_tensor(dtop, top2, top1, ALU.subtract)
                ins.then_inc(s_rt, 1)
                assert k[0] + 1 == RT_DTOP

            def route_b(blk):
                k = [RT_DTOP]

                def step(ins, last=False):
                    ins.then_inc(s_rt, 1)
                    k[0] += 1
                    if not last:
                        dve.wait_ge(s_rt, blk * N_RT + k[0])

                dve.wait_ge(s_etop, blk + 1)
                step(dve.tensor_scalar(dsum[:, :], etop, 1.0, None, ALU.add))
                step(dve.reciprocal(g1_all[:, bass.ds(blk * G, G)], dsum[:, :]))
                step(dve.tensor_tensor(g2_all[:, bass.ds(blk * G, G)], etop, g1_all[:, bass.ds(blk * G, G)],
                                       ALU.mult), last=True)
                assert k[0] == N_RT

            n_route = [0]

            def route(n):
                blk0, nb, nt = CHUNKS[n]
                t0, nr = G * blk0, G * nb
                rows, tiles = slice(t0, t0 + nr), slice(TILE0[n], TILE0[n] + nt)
                tot, inc = (v[:, 0:E * nr].rearrange("p (e r) -> p e r", e=E) for v in (tot_flat, inc_flat))
                scratch = [v[:, 0:E * nr].rearrange("p (r e) -> p r e", e=E) for v in (tot_flat, inc_flat)]

                def step(ins):
                    ins.then_inc(s_route, 1)
                    n_route[0] += 1
                    dve.wait_ge(s_route, n_route[0])

                dve.wait_ge(s_rt, N_RT * (blk0 + nb))
                dve.tensor_tensor(pick[:, 0:nr, :], hot1[:, rows, :], hot2[:, rows, :], ALU.add).then_inc(s_pick, 1)
                dve.wait_ge(s_rank, n + 1)
                rank = ps_epi[:, 0:E * nr].rearrange("p (r e) -> p r e", e=E)
                step(dve.tensor_copy(tot, ps_epi[:, 256:256 + E * nr].rearrange("p (r e) -> p e r", e=E)))
                step(dve.memset(keep[:, 0:E * nr], 1.0))
                step(dve.memset(keep[:, 0:E * nr].rearrange("p (e r) -> p e r", e=E)[:, :, 0:1], 0.0))
                step(dve.tensor_tensor_scan(inc_flat[:, 0:E * nr], keep[:, 0:E * nr], tot_flat[:, 0:E * nr], 0.0,
                                            ALU.mult, ALU.add))
                count = pick[:, 0:nr, :].rearrange("p r e -> p (r e)").rearrange("p (e k) -> p e k", e=E)
                step(dve.tensor_tensor(count, inc[:, :, nr - 1:nr].to_broadcast([128, E, nr]),
                                       tile_lim[:, 0:nr].unsqueeze(1).to_broadcast([128, E, nr]), ALU.is_gt))
                step(dve.tensor_reduce(tiles_e[:, :], count, AX.X, ALU.add))
                step(dve.tensor_tensor_scan(tiles_to[:, :], ones[:, 0:E], tiles_e[:, :], 0.0, ALU.mult, ALU.add))
                step(dve.tensor_tensor(base_e[:, :], tiles_to[:, :], tiles_e[:, :], ALU.subtract))
                step(dve.tensor_tensor(inc, inc, tot, ALU.subtract))
                step(dve.scalar_tensor_tensor(inc, base_e[:, :].unsqueeze(2).to_broadcast([128, E, nr]),
                                              128.0, inc, ALU.mult, ALU.add))
                step(dve.tensor_tensor(pick[:, 0:nr, :], rank, inc.rearrange("p e r -> p r e"), ALU.add))
                for k, hot in enumerate((hot1, hot2)):
                    step(dve.tensor_tensor(scratch[k], pick[:, 0:nr, :], hot[:, rows, :], ALU.mult))
                    step(dve.tensor_reduce(slot_f[:, k, 0:nr], scratch[k], AX.X, ALU.add))
                step(dve.tensor_copy(slot_i[:, :, 0:nr], slot_f[:, :, 0:nr]))
                step(dve.tensor_scalar(part_i[:, 0, :, 0:nr], slot_i[:, :, 0:nr], 127, None, ALU.bitwise_and))
                step(dve.tensor_scalar(part_i[:, 1, :, 0:nr], slot_i[:, :, 0:nr], 7, None, ALU.arith_shift_right))
                step(dve.tensor_copy(lo_f[:, :, rows], part_i[:, 0, :, 0:nr]))
                step(dve.tensor_copy(hi_f[:, :, rows], part_i[:, 1, :, 0:nr]))

                dve.wait_ge(s_ring, 16 * G * SEGMENTS[n][1] + ROWS0)
                for q in range(t0 // 2, (t0 + nr) // 2):
                    two, h = slice(2 * q, 2 * q + 2), q % 2
                    if q >= 2:
                        dve.wait_ge(s_tab, 4 * (q - 1))
                    dve.tensor_tensor(oh_lo[h], iota_q[:, :].unsqueeze(1).unsqueeze(1).to_broadcast([128, 2, 2, 128]),
                                      lo_f[:, :, two].unsqueeze(3).to_broadcast([128, 2, 2, 128]), ALU.is_equal)
                    dve.tensor_tensor(oh_hi[h][:, :, :, 0:nt],
                                      iota_q[:, 0:nt].unsqueeze(1).unsqueeze(1).to_broadcast([128, 2, 2, nt]),
                                      hi_f[:, :, two].unsqueeze(3).to_broadcast([128, 2, 2, nt]),
                                      ALU.is_equal).then_inc(s_hi, 1)
                    dve.wait_ge(s_hi, q + 1)
                    dve.tensor_tensor(oh_hi[h][:, :, :, 0:nt], oh_hi[h][:, :, :, 0:nt],
                                      token1[:, :, two].unsqueeze(3).to_broadcast([128, 2, 2, nt]),
                                      ALU.mult).then_inc(s_oh, 1)

                ends = z_flat[:, 0:nt * (E - 1)].rearrange("p (j e) -> p j e", e=E - 1)
                step(dve.tensor_tensor(ends, iota_q[:, 0:nt].unsqueeze(2).to_broadcast([128, nt, E - 1]),
                                       tiles_to[:, 0:E - 1].unsqueeze(1).to_broadcast([128, nt, E - 1]), ALU.is_ge))
                step(dve.tensor_reduce(exp_f[:, 0:nt], ends, AX.X, ALU.add))
                word0, m, words = PACK[n]
                in_words = exp_f[:, 0:nt].rearrange("p (w i) -> p w i", i=m)
                step(dve.tensor_tensor(in_words, in_words, pow8[:, 0:m].unsqueeze(1).to_broadcast([128, words, m]),
                                       ALU.mult))
                step(dve.tensor_reduce(word_f[:, 0:words], in_words, AX.X, ALU.add))
                step(dve.tensor_copy(experts[:, word0:word0 + words], word_f[:, 0:words]))

                dve.wait_ge(s_tab, 2 * (t0 + nr))
                number, less, second, empty, away = (tab[:, k, 0:nt] for k in range(5))
                step(dve.tensor_copy(number, ps_epi[:, 0:nt]))
                step(dve.tensor_scalar(less, number, -1.0, 0.0, ALU.add, ALU.max))
                step(dve.tensor_scalar(second, number, float(NTOK), -float(NTOK), ALU.is_gt, ALU.mult))
                step(dve.tensor_tensor(take_row[:, tiles], less, second, ALU.add))
                step(dve.tensor_scalar(empty, number, 0.0, 128.0 * TILE0[n], ALU.is_equal, ALU.mult))
                step(dve.tensor_tensor(less, number, empty, ALU.add))
                step(dve.tensor_scalar(second, number, 0.0, None, ALU.is_equal))
                step(dve.tensor_tensor(away, second, spare[:, 0:nt], ALU.mult))
                dve.tensor_tensor(give_row[:, tiles], away, less, ALU.add).then_inc(s_tabs, 1)
                dve.wait_ge(s_tabs, n + 1)

            def tile_weights(n, i, e):
                wait_apart(dve, s_hid, n + (i if i >= 3 else SEED2))
                dve.tensor_copy(w1_cur[:, i % 3, :], w1_sb[:, e, :]).then_inc(s_w1c, 1)

            def combine(i, blk, b, half):
                g = i % G
                y1, y2 = yc[:, b, 0, g, :], yc[:, b, 1, g, :]
                if i == 0:
                    dve.wait_ge(s_yc[b], 32 * half + 32)
                if i >= G:
                    dve.wait_ge(s_cmb, 15 * blk + i - G + 1)
                if i < G:
                    dve.tensor_scalar(y1, y1, g1_all[:, bass.ds(blk * G + g, 1)], None, ALU.mult).then_inc(s_cmb, 1)
                elif i < 2 * G:
                    dve.scalar_tensor_tensor(y1, y2, g2_all[:, bass.ds(blk * G + g, 1)], y1, ALU.mult,
                                             ALU.add).then_inc(s_cmb, 1)
                elif i < 3 * G:
                    dve.tensor_tensor(y1, y1, g_ffn[:, g, :], ALU.mult).then_inc(s_cmb, 1)
                else:
                    m = dve.tensor_tensor(y1, y1, x_sb[:, blk, g, :], ALU.add)
                    m.then_inc(s_cmb if i < 4 * G - 1 else s_res, 1)

            def window_max(s):
                dve.wait_ge(s_s_ps, s + 1)
                dve.scalar_tensor_tensor(score[:, :, :], ps_scan[:, :].rearrange("p (b k) -> p b k", k=W),
                                         w2b_col[:, 0:1],
                                         mask[:, s % NSLOT, :].unsqueeze(1).to_broadcast([128, GB, W]),
                                         ALU.add, ALU.add).then_inc(s_sm, 1)
                dve.wait_ge(s_sm, s * N_SM + 1)
                dve.tensor_reduce(m_score, score[:, :, :], AX.X, ALU.max).then_inc(s_sm, 1)
                dve.wait_ge(s_sm, s * N_SM + 2)
                dve.tensor_scalar(m_old, m_score, w2b_col[:, 0:1], None, ALU.max).then_inc(s_sm, 1)
                dve.wait_ge(s_sm, s * N_SM + 3)
                dve.tensor_tensor(score[:, :, :], score[:, :, :], m_old.unsqueeze(2).to_broadcast([128, GB, W]),
                                  ALU.subtract).then_inc(s_cen, 1)
                dve.transpose(s_T[:, :, :, :].rearrange("p b k i -> p (b k) i"),
                              ps_scan[:, :].rearrange("p (n c) -> p n c", c=Q32))

            def window_sum(s):
                dve.wait_ge(s_p, s + SEED + 1)
                dve.wait_ge(s_o_ps, s + SEED)
                dve.transpose(prob_T[:, :, :, :].rearrange("p b k i -> p (b k) i"),
                              prob[:, :, :].rearrange("p b (k c) -> p (b k) c", c=Q32)).then_inc(s_pT, 1)
                dve.tensor_scalar(m_rel, m_old, w2b_col[:, 0:1], None, ALU.subtract).then_inc(s_sm, 1)
                dve.wait_ge(s_sm, s * N_SM + 4)
                dve.tensor_tensor(tmp_d[:, :, :], diag[:, :].unsqueeze(2).to_broadcast([128, TB, GB]),
                                  m_rel.unsqueeze(1).to_broadcast([128, TB, GB]), ALU.mult).then_inc(s_sm, 1)
                dve.tensor_reduce(z_part, prob[:, :, :], AX.X, ALU.add).then_inc(s_sm, 1)
                dve.wait_ge(s_sm, s * N_SM + 6)
                dve.wait_ge(s_ez, s + 1)
                dve.tensor_tensor(r_pad[:, TB, 0:GB], z_part, z_zero, ALU.add).then_inc(s_sm, 1)

            def build_system(s):
                dve.wait_ge(s_r_ps, s + 1)
                r_v = ps_scan[:, 0:GB * TB].rearrange("p (b j) -> p j b", j=TB)
                dve.tensor_tensor(tmp_r[:, :, :], r_v, below[:, :].unsqueeze(2).to_broadcast([128, TB, GB]),
                                  ALU.mult).then_inc(s_r, 1)
                dve.wait_ge(s_r, s * N_R + SEED + 1)
                dve.wait_ge(s_sm, (s + 1) * N_SM)
                dve.tensor_tensor(r_pad[:, 0:TB, 0:GB], tmp_r[:, :, :], tmp_d[:, :, :], ALU.add).then_inc(s_r, 1)
                dve.wait_ge(s_r, s * N_R + SEED + 2)
                dve.transpose(cross[:, :, :], r_pad[:, :, :]).then_inc(s_r, 1)
                dve.wait_ge(s_r, s * N_R + SEED + 3)
                dve.tensor_copy(cross[:, 0:TB, TB], cross[:, TB, 0:TB]).then_inc(s_cross, 1)

            def step_max(s, j):
                if j == 0:
                    dve.wait_ge(s_cross, s + 1)
                else:
                    dve.wait_ge(s_col, s * TB + j)
                dve.tensor_reduce(neg_max[:, j:j + 1], cross[:, 0:j + 1, j], AX.X, ALU.max,
                                  negate=True).then_inc(s_max, 1)

            def step_mix(s, j, place):
                dve.wait_ge(s_e, s * TB + j + 1)
                if j:
                    dve.wait_ge(s_row, s * TB + j)
                dve.scalar_tensor_tensor(prod[:, TB, 0:j + 1], wgt[:, j, 0:j + 1], 1.0, cross[:, 0:j + 1, TB],
                                         ALU.mult, ALU.mult, accum_out=col[:, TB:TB + 1]).then_inc(s_zsum, 1)
                dve.tensor_tensor(prod[:, 0:TB, 0:j + 1], cross[:, 0:j + 1, 0:TB].rearrange("p l i -> p i l"),
                                  wgt[:, j, 0:j + 1].unsqueeze(1).to_broadcast([128, TB, j + 1]),
                                  ALU.mult).then_inc(s_prod, 1)
                dve.wait_ge(s_zsum, s * TB + j + 1)
                dve.reciprocal(z_inv, col[:, TB:TB + 1]).then_inc(s_sum, 1)
                place(4 * j + 1)
                dve.wait_ge(s_prod, s * TB + j + 1)
                dve.tensor_reduce(col[:, 0:TB], prod[:, 0:TB, 0:j + 1], AX.X, ALU.add).then_inc(s_sum, 1)
                place(4 * j + 2)
                dve.wait_ge(s_sum, 2 * (s * TB + j + 1))
                dve.tensor_scalar(cross[:, j, 0:TB + 1], col[:, :], z_inv, None, ALU.mult).then_inc(s_col, 1)
                place(4 * j + 3)

            def step_row(s, j):
                dve.scalar_tensor_tensor(cross[:, 0:j + 1, j], wgt[:, j, 0:j + 1], z_inv,
                                         unit[:, TB - 1 - j:TB], ALU.mult, ALU.mult).then_inc(s_row, 1)

            def coefficients(s):
                dve.wait_ge(s_row, s * TB + TB)
                dve.transpose(coef[:, :, :], cross[:, 0:TB, :]).then_inc(s_coef_T, 1)
                dve.wait_ge(s_coef_T, s + 1)
                for half in range(2):
                    some = slice(4 * half, 4 * half + 4)
                    dve.tensor_tensor(coef_bd[:, some, :, 0:TB].rearrange("p b g l -> p g b l"),
                                      coef[:, :, some].rearrange("p l b -> p b l").unsqueeze(1).to_broadcast(
                                          [128, G, 4, TB]),
                                      own_g[:, :].unsqueeze(2).unsqueeze(3).to_broadcast([128, G, 4, TB]),
                                      ALU.mult).then_inc(s_coef, 1)

            def values_cols(s, half):
                wait_apart(dve, s_vT_ps, 2 * s + 1 + half)
                some = slice(4 * half, 4 * half + 4)
                dve.tensor_copy(ring_T[:, :, bass.ds((s % NSLOT) * TB, TB)].rearrange(
                                    "p (g b) t -> p g b t", g=G)[:, :, some, :],
                                ps_wide[:, 512 * half:512 * half + 4 * G * TB].rearrange(
                                    "p (b g t) -> p g b t", g=G, t=TB)
                                ).then_inc(s_vT, 1)

            dve.wait_ge(s_router, 16 * 3)
            dve.wait_ge(s_w1, 16)
            dve.wait_ge(s_const, 1)
            dve.wait_ge(s_shift, 1)

            def body(s, blk, scan, key, it, n, comb, more=True):
                k = STREAMS[key][1] if key else 0
                m = packed(k)

                words = [dve.value_load(experts[0:1, bass.ds(it * (k // m) + WORD0[key] + w, 1)], min_val=0,
                                        max_val=8 ** m - 1) for w in range(k // m)] if k else []

                def place(p):
                    if blk is not None and p < 4 * TB:
                        epilogue(p, blk)
                    if p % 2 and p // 32 < len(comb):
                        combine(p % 32 // 2, *comb[p // 32])

                for t in range(TICKS if blk is not None else k + DONE):
                    j = t - STEP0
                    if scan and t == 1:
                        window_sum(s)
                    if blk is not None and t == 1:
                        stats_attn(blk)
                    if scan and t == 1:
                        build_system(s)
                    if scan and 0 <= j < TB:
                        step_max(s, j)
                        if j:
                            step_row(s, j - 1)
                        if 0 <= t - OUT < k:
                            i = t - OUT
                            tile_weights(n, i, words[i // m] // 8 ** (i % m) % 8)
                        place(4 * j)
                        step_mix(s, j, place)
                    elif j >= 0 and not scan:
                        for p in range(4):
                            place(4 * j + p)
                    if scan and j == TB:
                        dve.wait_ge(s_col, s * TB + TB)
                        step_row(s, TB - 1)
                        coefficients(s)
                    if blk is not None and j == TB:
                        route_a(blk)
                    if scan and j == TB:
                        values_cols(s, 0)
                        values_cols(s, 1)
                    if blk is not None and j == TB:
                        route_b(blk)
                        if more:
                            gate_h(blk + 1)
                    if scan and j == TB:
                        window_max(s + 1)
                    i = t - OUT
                    if 0 <= i < k and not (scan and 0 <= j < TB):
                        tile_weights(n, i, words[i // m] // 8 ** (i % m) % 8)

            gate_h(0)
            window_max(0)
            with dve.Fori(0, NSLOT - 1) as blk:
                body(None, blk, False, None, 0, 0, ())
            for n, (s0, s1, chunk, k, comb) in enumerate(SEGMENTS):
                key = ("seg", n) if chunk is not None else None
                with dve.Fori(s0, s1) as s:
                    tile = s * k + (STREAMS[key][3] - s0 * k) if key else 0
                    pair = ()
                    if comb is not None:
                        first = CHUNKS[comb][0]
                        assert first % 2 == 0
                        pair = [(s * 2 + (first - 2 * s0 + b), b, s + (first // 2 - s0)) for b in range(2)]
                    body(s, s + NSLOT - 1, True, key, s - s0, tile, pair)
                if n < len(CHUNKS) - 1:
                    route(n)
            body(None, NBLK - 1, False, None, 0, 0, (), more=False)
            route(len(CHUNKS) - 1)
            for n, (_, _, blocks) in enumerate(TAIL):
                key = ("tail", n)
                body(None, None, False, key, 0, STREAMS[key][3], [(blk, blk % 2, blk // 2) for blk in blocks])
            for blk in range(CHUNKS[-1][0], NBLK):
                for i in range(4 * G):
                    combine(i, blk, blk % 2, blk // 2)


SEED = 1
SEED2 = 2
ROWS0 = 2
PRO_SILU, PRO_CT, PRO_GATES = 3, 4, 19
RT_DTOP, N_RT = 13, 16
N_SM, N_R = 7, 3
EPI_NORM = STEP0 + 8
EPI_COLS = STEP0 + 14
EPI_LOGITS = STEP0 + 15
P_SCALE, P_RES, P_STATS, P_AGGR, P_MOD, P_SHIFT = 4, 8, 16, 24, 40, 48


_INS = ['L0_attn_feature', 'L0_attn_wq_w', 'L0_attn_wq_b', 'L0_attn_w2_w', 'L0_attn_w2_b', 'L0_attn_ln_g',
        'L0_attn_ln_b', 'L0_ffn_router_w', 'L0_ffn_router_b', 'L0_ffn_W1', 'L0_ffn_b1', 'L0_ffn_W2',
        'L0_ffn_b2', 'L0_c', 'L0_wmod']
_OUTS = [((32, 256, 128), 'float32')]


def kernel(**inputs):
    import numpy as _np
    import concourse.bacc as _bacc
    from concourse import mybir as _mybir
    from concourse.bass_utils import run_bass_kernel_spmd as _run

    nc = _bacc.Bacc("TRN2", target_bir_lowering=False, num_devices=1)
    arrays, args = {}, []
    for name in _INS:
        a = _np.ascontiguousarray(inputs[name])
        arrays[f"in_{name}_dram"] = a
        args.append(nc.dram_tensor(f"in_{name}_dram", a.shape, _mybir.dt.from_np(a.dtype), kind="ExternalInput").ap())
    for i, (shape, dtype) in enumerate(_OUTS):
        dt = _mybir.dt.from_np(_np.dtype(dtype))
        args.append(nc.dram_tensor(f"out_{i}_dram", shape, dt, kind="ExternalOutput").ap())
    adaln_block_kernel(nc, *args)
    r = _run(nc, [arrays], core_ids=[0])
    got = tuple(r.results[0][f"out_{i}_dram"] for i in range(len(_OUTS)))
    return got[0]
```
